# Optimizing a Trainium2 kernel written in Bass

```python
import numpy as np
import jax
import jax.numpy as jnp

def _softmax(x, axis=-1):
    return jax.nn.softmax(x, axis=axis)

def _gelu(x):
    return jax.nn.gelu(x, approximate=True)

def _silu(x):
    return jax.nn.silu(x)

def _sigmoid(x):
    return jax.nn.sigmoid(x)

def _layernorm(x, axis=-1, eps=1e-05):
    m = jnp.mean(x, axis=axis, keepdims=True)
    v = jnp.var(x, axis=axis, keepdims=True)
    return (x - m) / jnp.sqrt(v + eps)

def _scatter_add(tgt, idx, src, axis=0):
    return tgt.at[idx].add(src)

def _segment_sum(src, seg, n):
    return jax.ops.segment_sum(src, seg, n)
kernel_name = 'mk_xattn_ffn_d2_seqx_r4_4dfbb6'

def setup_inputs(seed: int=0):
    np.random.seed(seed)
    _w = jnp.asarray

    def _rec_inputs():
        import jax
        import jax.numpy as jnp
        _rk = jax.random.key(seed)
        x = -0.0002928 + 1 * jax.random.normal(jax.random.fold_in(_rk, 1), (4, 512, 512), jnp.float32)
        _lenS = 512 - jax.random.randint(jax.random.fold_in(_rk, 7), (4,), 0, max(1, 512 // 4) + 1, jnp.int32)
        _lenS2 = 512 - jax.random.randint(jax.random.fold_in(_rk, 8), (4,), 0, max(1, 512 // 4) + 1, jnp.int32)
        _ctx_2048P = jax.random.normal(jax.random.fold_in(_rk, 11), (4, 16, 512), jnp.float32)
        _ctx_2048c = jax.random.dirichlet(jax.random.fold_in(_rk, 511), 0.3 * jnp.ones((16,), jnp.float32), (4, 512))
        _ctx_2048t = jnp.einsum('bsk,bkd->bsd', _ctx_2048c, _ctx_2048P)
        _ctx_2048t = _ctx_2048t * jax.lax.rsqrt(jnp.mean(jnp.square(_ctx_2048t)) + 1e-12) * 0.953939
        ctx_2048 = -1.39393e-06 + 0.999914 * (_ctx_2048t + 0.3 * jax.random.normal(jax.random.fold_in(_rk, 611), (4, 512, 512), jnp.float32))
        return (x, ctx_2048)
    x, ctx_2048 = _rec_inputs()

    def _L0_xattn_setup():
        import jax, jax.numpy as jnp
        import numpy as np
        B, S, E, NH = (2, 256, 512, 16)
        DH = E // NH
        EPS = 1e-06

        def _mlstm_forward(q, k, v, Wi, bi, Wf, bf, ln_scale):
            b, s, e = q.shape
            nh = Wi.shape[1]
            dh = e // nh
            x = jnp.concatenate([q, k, v], axis=-1)
            ig = (x @ Wi + bi).transpose(0, 2, 1)[..., None]
            fg = (x @ Wf + bf).transpose(0, 2, 1)[..., None]
            split = lambda t: t.reshape(b, s, nh, dh).transpose(0, 2, 1, 3)
            qh, kh, vh = (split(q), split(k), split(v))
            log_f = jax.nn.log_sigmoid(fg)
            log_f_cum = jnp.concatenate([jnp.zeros((b, nh, 1, 1), q.dtype), jnp.cumsum(log_f, axis=2)], axis=2)
            fg_mat = log_f_cum - jnp.transpose(log_f_cum, (0, 1, 3, 2))
            ltr = jnp.tril(jnp.ones((s, s), dtype=bool))
            log_fg = jnp.where(ltr, fg_mat[:, :, 1:, 1:], -jnp.inf)
            log_D = log_fg + jnp.transpose(ig, (0, 1, 3, 2))
            max_log_D = jnp.max(log_D, axis=-1, keepdims=True)
            D = jnp.exp(log_D - max_log_D)
            qk = jnp.einsum('bhsd,bhtd->bhst', qh, kh) / jnp.sqrt(jnp.asarray(dh, q.dtype))
            C = qk * D
            normalizer = jnp.maximum(jnp.abs(C.sum(-1, keepdims=True)), jnp.exp(-max_log_D))
            Cn = C / (normalizer + EPS)
            h = jnp.einsum('bhst,bhtd->bhsd', Cn, vh)
            mu = h.mean(-1, keepdims=True)
            var = ((h - mu) ** 2).mean(-1, keepdims=True)
            hn = (h - mu) * jax.lax.rsqrt(var + EPS)
            hn = hn * ln_scale.reshape(1, nh, 1, dh)
            return hn.transpose(0, 2, 1, 3).reshape(b, s, e)
        key = jax.random.key(seed)
        ks = jax.random.split(key, 6)
        q = jax.random.normal(ks[0], (B, S, E), dtype=jnp.float32)
        k = jax.random.normal(ks[1], (B, S, E), dtype=jnp.float32)
        v = jax.random.normal(ks[2], (B, S, E), dtype=jnp.float32)
        Wi = jax.random.normal(ks[3], (3 * E, NH), dtype=jnp.float32) * 0.02
        bi = jax.random.normal(ks[4], (NH,), dtype=jnp.float32) * 0.1
        Wf = jax.random.normal(ks[5], (3 * E, NH), dtype=jnp.float32) * 0.02
        bf = jnp.linspace(3.0, 6.0, NH, dtype=jnp.float32)
        ln_scale = jnp.ones((E,), dtype=jnp.float32)
        return {'q': q, 'k': k, 'v': v, 'Wi': Wi, 'bi': bi, 'Wf': Wf, 'bf': bf, 'ln_scale': ln_scale}
    _L0_xattn_all = _L0_xattn_setup()
    _L0_xattn_in = {k: v for k, v in _L0_xattn_all.items() if k in ('Wi', 'bi', 'Wf', 'bf', 'ln_scale')}
    del _L0_xattn_all

    def _L0_ffn_setup():
        import jax, jax.numpy as jnp
        import numpy as np
        TOP_K = 4
        ROUTED_SCALE = 1.0
        NORM_TOPK = True
        B, S, H = (1, 512, 512)
        E, I = (16, 192)
        IS = 192
        key = jax.random.key(seed)
        ks = jax.random.split(key, 8)
        s = 0.02
        return {'hidden_states': jax.random.normal(ks[0], (B, S, H), jnp.float32), 'router_w': jax.random.normal(ks[1], (E, H), jnp.float32) * s, 'e_bias': jax.random.normal(ks[2], (E,), jnp.float32) * s, 'gate_up_proj': jax.random.normal(ks[3], (E, 2 * I, H), jnp.float32) * s, 'down_proj': jax.random.normal(ks[4], (E, H, I), jnp.float32) * s, 'shared_gate_w': jax.random.normal(ks[5], (IS, H), jnp.float32) * s, 'shared_up_w': jax.random.normal(ks[6], (IS, H), jnp.float32) * s, 'shared_down_w': jax.random.normal(ks[7], (H, IS), jnp.float32) * s}
    _L0_ffn_all = _L0_ffn_setup()
    _L0_ffn_in = {k: v for k, v in _L0_ffn_all.items() if k in ('router_w', 'e_bias', 'gate_up_proj', 'down_proj', 'shared_gate_w', 'shared_up_w', 'shared_down_w')}
    del _L0_ffn_all

    def _L1_xattn_setup():
        import jax, jax.numpy as jnp
        import numpy as np
        from math import sqrt
        key = jax.random.key(seed)
        kq, kk, kv = jax.random.split(key, 3)
        B, D, N = (8, 128, 512)
        Q = jax.random.normal(kq, (B, D, N), dtype=jnp.float32)
        K = jax.random.normal(kk, (B, D, N), dtype=jnp.float32)
        V = jax.random.normal(kv, (B, D, N), dtype=jnp.float32)
        return {'Q': Q, 'K': K, 'V': V}
    _L1_xattn_all = _L1_xattn_setup()
    _L1_xattn_in = {k: v for k, v in _L1_xattn_all.items() if k in ()}
    del _L1_xattn_all

    def _L1_ffn_setup():
        import jax, jax.numpy as jnp
        import numpy as np
        DIM_IN = 512
        DIM_HIDDEN = 2048
        key = jax.random.key(seed)
        k_x, k_g, k_u, k_d = jax.random.split(key, 4)
        s_in = 1.0 / np.sqrt(DIM_IN)
        s_hid = 1.0 / np.sqrt(DIM_HIDDEN)
        x = jax.random.normal(k_x, (4, 512, DIM_IN), dtype=jnp.float32)
        w_gate = jax.random.uniform(k_g, (DIM_HIDDEN, DIM_IN), jnp.float32, -s_in, s_in)
        w_up = jax.random.uniform(k_u, (DIM_HIDDEN, DIM_IN), jnp.float32, -s_in, s_in)
        w_down = jax.random.uniform(k_d, (DIM_IN, DIM_HIDDEN), jnp.float32, -s_hid, s_hid)
        return {'x': x, 'w_gate': w_gate, 'w_up': w_up, 'w_down': w_down}
    _L1_ffn_all = _L1_ffn_setup()
    _L1_ffn_in = {k: v for k, v in _L1_ffn_all.items() if k in ('w_gate', 'w_up', 'w_down')}
    del _L1_ffn_all
    return {'x': x, 'ctx_2048': ctx_2048, 'L0_xattn_Wi': _L0_xattn_in['Wi'], 'L0_xattn_bi': _L0_xattn_in['bi'], 'L0_xattn_Wf': _L0_xattn_in['Wf'], 'L0_xattn_bf': _L0_xattn_in['bf'], 'L0_xattn_ln_scale': _L0_xattn_in['ln_scale'], 'L0_ffn_router_w': _L0_ffn_in['router_w'], 'L0_ffn_e_bias': _L0_ffn_in['e_bias'], 'L0_ffn_gate_up_proj': _L0_ffn_in['gate_up_proj'], 'L0_ffn_down_proj': _L0_ffn_in['down_proj'], 'L0_ffn_shared_gate_w': _L0_ffn_in['shared_gate_w'], 'L0_ffn_shared_up_w': _L0_ffn_in['shared_up_w'], 'L0_ffn_shared_down_w': _L0_ffn_in['shared_down_w'], 'L1_ffn_w_gate': _L1_ffn_in['w_gate'], 'L1_ffn_w_up': _L1_ffn_in['w_up'], 'L1_ffn_w_down': _L1_ffn_in['w_down']}

def reference(x, ctx_2048, L0_xattn_Wi, L0_xattn_bi, L0_xattn_Wf, L0_xattn_bf, L0_xattn_ln_scale, L0_ffn_router_w, L0_ffn_e_bias, L0_ffn_gate_up_proj, L0_ffn_down_proj, L0_ffn_shared_gate_w, L0_ffn_shared_up_w, L0_ffn_shared_down_w, L1_ffn_w_gate, L1_ffn_w_up, L1_ffn_w_down):
    import jax
    import jax.numpy as jnp

    def _L0_xattn_ref(q, k, v, Wi, bi, Wf, bf, ln_scale):
        import jax, jax.numpy as jnp
        import numpy as np
        B, S, E, NH = (2, 256, 512, 16)
        DH = E // NH
        EPS = 1e-06

        def _mlstm_forward(q, k, v, Wi, bi, Wf, bf, ln_scale):
            b, s, e = q.shape
            nh = Wi.shape[1]
            dh = e // nh
            x = jnp.concatenate([q, k, v], axis=-1)
            ig = (x @ Wi + bi).transpose(0, 2, 1)[..., None]
            fg = (x @ Wf + bf).transpose(0, 2, 1)[..., None]
            split = lambda t: t.reshape(b, s, nh, dh).transpose(0, 2, 1, 3)
            qh, kh, vh = (split(q), split(k), split(v))
            log_f = jax.nn.log_sigmoid(fg)
            log_f_cum = jnp.concatenate([jnp.zeros((b, nh, 1, 1), q.dtype), jnp.cumsum(log_f, axis=2)], axis=2)
            fg_mat = log_f_cum - jnp.transpose(log_f_cum, (0, 1, 3, 2))
            ltr = jnp.tril(jnp.ones((s, s), dtype=bool))
            log_fg = jnp.where(ltr, fg_mat[:, :, 1:, 1:], -jnp.inf)
            log_D = log_fg + jnp.transpose(ig, (0, 1, 3, 2))
            max_log_D = jnp.max(log_D, axis=-1, keepdims=True)
            D = jnp.exp(log_D - max_log_D)
            qk = jnp.einsum('bhsd,bhtd->bhst', qh, kh) / jnp.sqrt(jnp.asarray(dh, q.dtype))
            C = qk * D
            normalizer = jnp.maximum(jnp.abs(C.sum(-1, keepdims=True)), jnp.exp(-max_log_D))
            Cn = C / (normalizer + EPS)
            h = jnp.einsum('bhst,bhtd->bhsd', Cn, vh)
            mu = h.mean(-1, keepdims=True)
            var = ((h - mu) ** 2).mean(-1, keepdims=True)
            hn = (h - mu) * jax.lax.rsqrt(var + EPS)
            hn = hn * ln_scale.reshape(1, nh, 1, dh)
            return hn.transpose(0, 2, 1, 3).reshape(b, s, e)
        return _mlstm_forward(q, k, v, Wi, bi, Wf, bf, ln_scale)

    def _L0_ffn_ref(hidden_states, router_w, e_bias, gate_up_proj, down_proj, shared_gate_w, shared_up_w, shared_down_w):
        import jax, jax.numpy as jnp
        import numpy as np
        TOP_K = 4
        ROUTED_SCALE = 1.0
        NORM_TOPK = True
        B, S, H = (1, 512, 512)
        E, I = (16, 192)
        IS = 192
        orig_shape = hidden_states.shape
        x = hidden_states.reshape(-1, orig_shape[-1])
        T = x.shape[0]
        scores = jax.nn.sigmoid(x @ router_w.T)
        _, topk_idx = jax.lax.top_k(scores + e_bias[None, :], TOP_K)
        topk_w = jnp.take_along_axis(scores, topk_idx, axis=1)
        if NORM_TOPK:
            topk_w = topk_w / (topk_w.sum(axis=-1, keepdims=True) + 1e-20)
        topk_w = topk_w * ROUTED_SCALE
        combine = jnp.zeros((T, E), x.dtype).at[jnp.arange(T)[:, None], topk_idx].add(topk_w)

        def step(acc, xs):
            gu_w, d_w, c = xs
            gu = x @ gu_w.T
            g, u = jnp.split(gu, 2, axis=1)
            y = jax.nn.silu(g) * u @ d_w.T
            return (acc + c[:, None] * y, None)
        routed, _ = jax.lax.scan(step, jnp.zeros_like(x), (gate_up_proj, down_proj, combine.T))
        shared = jax.nn.silu(x @ shared_gate_w.T) * (x @ shared_up_w.T) @ shared_down_w.T
        return (routed + shared).reshape(orig_shape)

    def _L1_xattn_ref(Q, K, V):
        import jax, jax.numpy as jnp
        import numpy as np
        from math import sqrt
        dk = Q.shape[1]
        x = jnp.einsum('bdn,bdm->bnm', Q, K) / sqrt(dk)
        score = jax.nn.sigmoid(x)
        out = jnp.einsum('bvn,bnm->bvm', V, score)
        return out

    def _L1_ffn_ref(x, w_gate, w_up, w_down):
        import jax, jax.numpy as jnp
        import numpy as np
        DIM_IN = 512
        DIM_HIDDEN = 2048
        gate = jnp.einsum('bsd,hd->bsh', x, w_gate)
        up = jnp.einsum('bsd,hd->bsh', x, w_up)
        gated = jax.nn.silu(gate) * up
        return jnp.einsum('bsh,dh->bsd', gated, w_down)
    x = x + _L0_xattn_ref(_layernorm(x, axis=-1), ctx_2048, ctx_2048, L0_xattn_Wi, L0_xattn_bi, L0_xattn_Wf, L0_xattn_bf, L0_xattn_ln_scale)
    x = x + _L0_ffn_ref(_layernorm(x, axis=-1), L0_ffn_router_w, L0_ffn_e_bias, L0_ffn_gate_up_proj, L0_ffn_down_proj, L0_ffn_shared_gate_w, L0_ffn_shared_up_w, L0_ffn_shared_down_w)
    x = x + _L1_xattn_ref(_layernorm(x, axis=-1), ctx_2048, ctx_2048)
    x = x + _L1_ffn_ref(_layernorm(x, axis=-1), L1_ffn_w_gate, L1_ffn_w_up, L1_ffn_w_down)
    return x

_drawn_inputs = setup_inputs


def setup_inputs(seed=0):
    import zlib

    import numpy as np

    out = dict(_drawn_inputs(seed))
    spreads = {'L0_xattn_ln_scale': (1.0, 0.2)}
    factors = {'L0_xattn_bi': 64.0,
     'L0_ffn_router_w': 8.0,
     'L0_ffn_e_bias': 8.0,
     'L0_ffn_gate_up_proj': 8.0,
     'L0_ffn_down_proj': 8.0,
     'L0_ffn_shared_gate_w': 7.422,
     'L0_ffn_shared_up_w': 6.788,
     'L0_ffn_shared_down_w': 7.16,
     'L1_ffn_w_gate': 7.354,
     'L1_ffn_w_up': 7.142,
     'L1_ffn_w_down': 7.145}
    for name, (base, spread) in spreads.items():
        noise = np.random.default_rng([zlib.crc32(name.encode()), seed]).standard_normal(out[name].shape)
        drawn = base * np.exp(spread * noise) if base else spread * noise
        out[name] = jnp.asarray(drawn.astype(out[name].dtype))
    for name, factor in factors.items():
        out[name] = (out[name] * factor).astype(out[name].dtype)
    return out
```

```python
from contextlib import ExitStack, contextmanager

import concourse.bass as bass
from concourse import mybir

F32 = mybir.dt.float32
F32R = mybir.dt.float32r
BF16 = mybir.dt.bfloat16
I32 = mybir.dt.int32
U32 = mybir.dt.uint32
ALU = mybir.AluOpType
ACT = mybir.ActivationFunctionType
AX = mybir.AxisListType

P = 128
B, S, E = 4, 512, 512
NT = B * S // P
CPB = S // P
KC = E // P
NH, DH = 16, 32
HPG = P // DH
NG = NH // HPG
V1 = DH + 1
QSCALE = float(DH) ** -0.5
EPS_LN, EPS_H = 1e-5, 1e-6
NEG = -1e30

NE, TOPK, FI = 16, 4, 192
FH = FI // 2
MT = 256
SHARED_T = B * S // MT
ROUTED_T = (TOPK * B * S + NE * (MT - 1)) // MT
ETILES = SHARED_T + ROUTED_T
HALVES = 2 * ETILES
SHARED_ROWS = SHARED_T * MT
ROWS = ETILES * MT

HID = 2048
BLK = 256
NBLK = HID // BLK
HCB = BLK // P
XSCALE = float(S) ** -0.5

MLSTM_STEPS = 39


class Steps:

    def __init__(self, eng, sem):
        self.eng, self.sem, self.base, self.n = eng, sem, 0, 0

    def __call__(self, ins):
        ins.then_inc(self.sem, 1)
        self.n += 1
        self.eng.wait_ge(self.sem, self.base + self.n)

    @contextmanager
    def loop(self, trips, per):
        start = self.base + self.n
        with self.eng.Fori(0, trips) as i:
            self.base, self.n = start + i * per, 0
            yield i
            assert self.n == per, (self.n, per)
        self.base, self.n = start + trips * per, 0


def done(n, credit=2):
    return n + 1 + credit


class Arena:

    def __init__(self, nc, at):
        self.nc, self.at = nc, at

    def __call__(self, name, shape, dt=F32):
        size = {BF16: 2}.get(dt, 4)
        for n in shape[1:]:
            size *= n
        t = self.nc.alloc_sbuf_tensor_at(name, shape, dt, offset=self.at)
        self.at += (size + 31) // 32 * 32
        assert self.at <= self.nc.sbuf_usable_end, (name, self.at)
        return t


def build(nc, x, ctx, ctxT, Wi, bi, Wf, bf, ln_scale, router_wT, e_bias, gate_upT, downT,
          w_gateT, w_upT, w_downT, out, stop=99):
    with ExitStack() as stack:
        def sem(name):
            return stack.enter_context(nc.semaphore(name))

        base = (nc.sbuf_base + 63) // 64 * 64
        keep = Arena(nc, base)
        X = keep("X", [P, NT, E])
        ident = keep("ident", [P, P])
        stats = keep("stats", [P, NT, 6])
        mv = keep("mv", [P, NT, 2])
        lnv = keep("lnv", [P, NT])
        rstd = keep("rstd", [P, NT])
        eps = keep("eps", [P, 2])
        slot = keep("slot", [P, NT, TOPK], U32)
        ck = keep("ck", [P, NT, TOPK])
        etab = keep("etab", [1, ETILES + 1], I32)

        pA, pB, pC, pD = [stack.enter_context(nc.psum_tensor(f"p{n}", [P, 2, 512], F32)) for n in "ABCD"]

        M_dram = nc.dram_tensor("M_dram", (P, S), F32, kind="Internal").ap()
        Xs = nc.dram_tensor("Xs", (ROWS, E), F32, kind="Internal").ap()
        Ys = nc.dram_tensor("Ys", (ROWS, E), F32, kind="Internal").ap()

        a1 = Arena(nc, keep.at)
        qT = a1("qT", [P, KC, NT * P])
        tk = a1("tk", [P, 4, CPB, P])
        decB = a1("decB", [P, CPB, P])
        lnb = a1("lnb", [P, E])
        bms = a1("bms", [P, HPG])
        bmask = a1("bmask", [P, HPG])
        mask264 = a1("mask264", [P, 2 * HPG, V1])
        zero = a1("zero", [P, E])
        wg = a1("wg", [P, 3 * KC, 64])
        gb = a1("gb", [64, 1])
        a1a = Arena(nc, a1.at)
        ctxTb = a1a("ctxTb", [P, 2, KC, S])
        qn = a1a("qn", [P, 2, CPB, E])
        IG = a1a("IG", [P, S])
        FG = a1a("FG", [P, S])
        t1 = a1a("t1", [P, S])
        t2 = a1a("t2", [P, S])
        onesf = a1a("onesf", [P, S])
        Fc = a1a("Fc", [P, S])
        Aq = a1a("Aq", [P, S])
        Mq = a1a("Mq", [P, S])
        WQ = a1a("WQ", [P, S])
        WK = a1a("WK", [P, S])
        NR = a1a("NR", [P, S])
        mprev = a1a("mprev", [P, CPB])
        mneg = a1a("mneg", [P, CPB])
        dec = a1a("dec", [P, CPB])
        DG = a1a("DG", [P, CPB, P])
        a1b = Arena(nc, a1.at)
        kT = a1b("kT", [P, 2, KC, P])
        Mb = a1b("Mb", [P, 2, NH, P])
        cx = a1b("cx", [P, 2, E])
        v1 = a1b("v1", [P, 2, NH, V1])
        kw = a1b("kw", [P, 2, NH, DH])
        qs = a1b("qs", [P, 2, KC, P])
        qe = a1b("qe", [P, 2, NG, HPG, P])
        Dm = a1b("Dm", [P, 2, NH, P])
        Cm = a1b("Cm", [P, 2, NH, P])
        St = a1b("St", [P, NH, V1])
        stm = a1b("stm", [P, NH, V1])
        h1 = a1b("h1", [P, NH, V1])
        hs = a1b("hs", [P, NH, DH])
        hc = a1b("hc", [P, NH, DH])
        sq = a1b("sq", [P, NH, DH])
        den = a1b("den", [P, NH])
        rec = a1b("rec", [P, NH])
        hsum = a1b("hsum", [P, NH])
        vsum = a1b("vsum", [P, NH])
        lnh = a1b("lnh", [P, NH])
        rsh = a1b("rsh", [P, NH])

        a2 = Arena(nc, keep.at)
        xn2 = a2("xn2", [P, NT, E])
        xT2 = a2("xT2", [P, 2, KC, P])
        rw = a2("rw", [P, KC, NE])
        eb = a2("eb", [P, NE])
        sc = a2("sc", [P, NT, NE])
        sw = a2("sw", [P, NT, NE])
        eq = a2("eq", [P, NT, NE])
        oh = a2("oh", [P, TOPK, NT, NE])
        pr = a2("pr", [P, NT, NE])
        mx = a2("mx", [P, NT])
        ix = a2("ix", [P, NT])
        csum = a2("csum", [P, NT])
        crec = a2("crec", [P, NT])
        slf = a2("slf", [P, TOPK, NT])
        ckr = a2("ckr", [P, TOPK, NT])
        selb = a2("selb", [P, NT, NE], BF16)
        tri = a2("tri", [P, P], BF16)
        onesb = a2("onesb", [P, P], BF16)
        iotam = a2("iotam", [P, NE])
        iota256 = a2("iota256", [P, 8])
        iotan = a2("iotan", [1, ETILES + 1])
        cnt = a2("cnt", [P, NE, NT])
        d0 = a2("d0", [P, NE, NT])
        incl = a2("incl", [P, NE, NT])
        excl = a2("excl", [P, NE, NT])
        nt8 = a2("nt8", [P, NE, 8])
        nte = a2("nte", [P, NE])
        ton = a2("ton", [P, NE])
        tinc = a2("tinc", [P, NE])
        texc = a2("texc", [P, NE])
        rowb = a2("rowb", [P, NE])
        full = a2("full", [P, NT, NE])
        ecmp = a2("ecmp", [1, ETILES + 1, NE])
        ecf = a2("ecf", [1, ETILES + 1])

        a3 = Arena(nc, keep.at)
        gu_raw = a3("gu_raw", [P, 2, KC, 2 * FI])
        dn_raw = a3("dn_raw", [FH, 2, 2, E])
        gu_hi = a3("gu_hi", [P, 2, KC, 2 * FI], F32R)
        gu_lo = a3("gu_lo", [P, 2, KC, 2 * FI], F32R)
        dn_hi = a3("dn_hi", [FH, 2, 2, E], F32R)
        dn_lo = a3("dn_lo", [FH, 2, 2, E], F32R)
        xr = a3("xr", [P, 2, 2, E])
        x_hi = a3("x_hi", [P, 2, KC, P], F32R)
        x_lo = a3("x_lo", [P, 2, KC, P], F32R)
        sg = a3("sg", [P, 2, FI])
        hh = a3("hh", [P, 2, FI])
        h_hi = a3("h_hi", [FH, 2, 2, P], F32R)
        h_lo = a3("h_lo", [FH, 2, 2, P], F32R)
        yo = a3("yo", [P, 2, E])

        a4 = Arena(nc, keep.at)
        G = a4("G", [P, 2, TOPK + 1, E])
        cr = a4("cr", [P, 2, CPB, E])
        k_hi = a4("k_hi", [P, CPB, E], F32R)
        k_lo = a4("k_lo", [P, CPB, E], F32R)
        v_hi = a4("v_hi", [P, KC, S], F32R)
        v_lo = a4("v_lo", [P, KC, S], F32R)
        qf = a4("qf", [P, CPB, E])
        q_hi = a4("q_hi", [P, CPB, E], F32R)
        q_lo = a4("q_lo", [P, CPB, E], F32R)
        sf = a4("sf", [P, KC, E])
        s_hi = a4("s_hi", [P, KC, E], F32R)
        s_lo = a4("s_lo", [P, KC, E], F32R)

        a5 = Arena(nc, keep.at)
        f_hi = a5("f_hi", [P, KC, NT * P], F32R)
        f_lo = a5("f_lo", [P, KC, NT * P], F32R)
        w_raw = a5("w_raw", [P, 2, 3, KC * BLK])
        w_hi = a5("w_hi", [P, 2, 3, KC * BLK], F32R)
        w_lo = a5("w_lo", [P, 2, 3, KC * BLK], F32R)
        xn4 = a5("xn4", [P, 2, E])
        fsg = a5("fsg", [P, 2, 512])
        fh = a5("fh", [P, 2, 512])
        fh_hi = a5("fh_hi", [P, 2, HCB, 512], F32R)
        fh_lo = a5("fh_lo", [P, 2, HCB, 512], F32R)

        sp_note, pool_note = sem("sp_note"), sem("pool_note")
        dve_step, act_step, pool_step = sem("dve_step"), sem("act_step"), sem("pool_step")
        stage_done = [sem(f"stage_done{k}") for k in range(6)]
        x_loaded = [sem(f"x_loaded{b}") for b in range(B)]
        ctxT_loaded = [sem(f"ctxT_loaded{b}") for b in range(2)]
        small_loaded, consts_ready = sem("small_loaded"), sem("consts_ready")
        wg_zeroed, wg_ready = sem("wg_zeroed"), sem("wg_ready")
        mv_ready, rstd_ready, qn_ready = sem("mv_ready"), sem("rstd_ready"), sem("qn_ready")
        xT_done, xT_kept = sem("xT_done"), sem("xT_kept")
        gates_done, gates_kept = sem("gates_done"), sem("gates_kept")
        lsig_ready, aM_ready, exps_ready, dg_ready = sem("lsig_ready"), sem("aM_ready"), sem("exps_ready"), sem("dg_ready")
        tok_done, M_stored, zero_filled = sem("tok_done"), sem("M_stored"), sem("zero_filled")
        tile_loaded = [sem(f"tile_loaded{p}") for p in range(2)]
        qk_done, inter_done, intra_done, st_done = sem("qk_done"), sem("inter_done"), sem("intra_done"), sem("st_done")
        arg_ready, C_ready, h1_read, stm_ready = sem("arg_ready"), sem("C_ready"), sem("h1_read"), sem("stm_ready")
        hc_ready, var_ready = sem("hc_ready"), sem("var_ready")
        qs_ready, v1_ready, D_ready, sq_ready, rsh_ready = [sem(n) for n in ("qs_ready", "v1_ready", "D_ready", "sq_ready", "rsh_ready")]
        qe_ready, kw_ready, arg_masked, St_ready, St_decayed = [sem(n) for n in ("qe_ready", "kw_ready", "arg_masked", "St_ready", "St_decayed")]
        xn2_ready, rout_loaded = sem("xn2_ready"), sem("rout_loaded")
        sc_done, sc_ready, sel_ready, pos_done = sem("sc_done"), sem("sc_ready"), sem("sel_ready"), sem("pos_done")
        slots_ready, xs_written = sem("slots_ready"), sem("xs_written")
        ew_loaded = [sem(f"ew_loaded{p}") for p in range(2)]
        xr_loaded = [sem(f"xr_loaded{p}") for p in range(2)]
        gw_hi, gw_lo, dw_hi, dw_lo = sem("gw_hi"), sem("gw_lo"), sem("dw_hi"), sem("dw_lo")
        xT_e, x_hi_e, x_lo_e = sem("xT_e"), sem("x_hi_e"), sem("x_lo_e")
        gu_e, sg_e, hh_e = sem("gu_e"), sem("sg_e"), sem("hh_e")
        hT_e, h_hi_e, h_lo_e, dn_e, y_e = sem("hT_e"), sem("h_hi_e"), sem("h_lo_e"), sem("dn_e"), sem("y_e")
        ys_written = [sem(f"ys_written{q}") for q in range(2)]
        g_loaded = [sem(f"g_loaded{p}") for p in range(2)]
        gs_loaded = [sem(f"gs_loaded{p}") for p in range(2)]
        g_used, cr_loaded = sem("g_used"), sem("cr_loaded")
        ctx_hi, ctx_lo, qf_ready, q_hi_x, q_lo_x = [sem(n) for n in ("ctx_hi", "ctx_lo", "qf_ready", "q_hi_x", "q_lo_x")]
        s_done, s_sig, s_hi_x, s_lo_x, o_done, o_added = [sem(n) for n in ("s_done", "s_sig", "s_hi_x", "s_lo_x", "o_done", "o_added")]
        xn4_ready, fT_done, f_hi_ready, f_lo_ready = [sem(n) for n in ("xn4_ready", "fT_done", "f_hi_ready", "f_lo_ready")]
        fw_loaded = [sem(f"fw_loaded{p}") for p in range(2)]
        fw_hi, fw_lo = sem("fw_hi"), sem("fw_lo")
        fgu, fsg_ready, fh_ready, fh_hi_ready, fh_lo_ready, fdn, fadd = [
            sem(n) for n in ("fgu", "fsg_ready", "fh_ready", "fh_hi_ready", "fh_lo_ready", "fdn", "fadd")]
        out_written = sem("out_written")

        ENGINES = 5

        def stage_end(eng, k):
            eng.drain().then_inc(stage_done[k], 1)
            eng.wait_ge(stage_done[k], ENGINES)

        def bc(ap, shape):
            while len(ap.shape) < len(shape):
                ap = ap.unsqueeze(len(ap.shape))
            return ap.to_broadcast(shape)

        def flat(ap):
            return ap.rearrange("p a b -> p (a b)")

        def heads(ap):
            return ap.rearrange("p (h d) -> p h d", h=NH)

        E_LOOPS = (HALVES - 2) // 4 - 1

        def expert_steps(eng):
            with eng.Fori(0, E_LOOPS) as i:
                for k in range(1, 5):
                    yield i, k, True
            for k in range(1, HALVES - 4 * E_LOOPS):
                yield E_LOOPS, k, False

        UNITS = NBLK * B
        F_LOOPS = UNITS // 8 - 1

        def ffn_steps(eng):
            with eng.Fori(0, F_LOOPS) as i:
                for k in range(1, 9):
                    yield i, k, True
            for k in range(1, UNITS - 8 * F_LOOPS):
                yield F_LOOPS, k, False

        block = stack.enter_context(nc.Block())

        @block.sync
        def _(sp):
            def store_X():
                for b in range(B):
                    sp.dma_start(out[b].rearrange("(i p) f -> p i f", p=P), X[:, CPB * b:CPB * (b + 1), :]).then_inc(out_written, 16)
                sp.wait_ge(out_written, 16 * B)

            for q in range(2):
                sp.sem_inc(ys_written[q], 16)
            for b in range(B):
                sp.dma_start(X[:, CPB * b:CPB * (b + 1), :],
                             x[b].rearrange("(i p) f -> p i f", p=P)).then_inc(x_loaded[b], 16)
                if b == 0:
                    sp.wait_ge(wg_zeroed, 1)
                    with nc.allow_non_contiguous_dma(reason="one value per partition"):
                        sp.dma_start(wg[:, :, 0:NH], Wi.rearrange("(c p) h -> p c h", p=P)).then_inc(small_loaded, 16)
                        sp.dma_start(wg[:, :, 32:32 + NH], Wf.rearrange("(c p) h -> p c h", p=P)).then_inc(small_loaded, 16)
                        sp.dma_start(gb[0:NH, :], bi.rearrange("(h o) -> h o", o=1)).then_inc(small_loaded, 16)
                        sp.dma_start(gb[32:32 + NH, :], bf.rearrange("(h o) -> h o", o=1)).then_inc(small_loaded, 16)
                    sp.dma_start(lnb[:, :], ln_scale.rearrange("(o f) -> o f", o=1).to_broadcast([P, E])).then_inc(small_loaded, 16)
                if b >= 2:
                    sp.wait_ge(gates_done, b - 1)
                sp.dma_start(ctxTb[:, b % 2], ctxT[b].rearrange("(k p) s -> p k s", p=P)).then_inc(ctxT_loaded[b % 2], 16)
            sp.wait_ge(consts_ready, 1)
            R = (ROWS - SHARED_ROWS) // P
            sp.dma_start(Xs[SHARED_ROWS:, :].rearrange("(r p) f -> p r f", p=P),
                         zero[:, :].unsqueeze(1).to_broadcast([P, R, E])).then_inc(zero_filled, 16)
            sp.wait_ge(aM_ready, 1)
            sp.dma_start(M_dram, Mq[:, :]).then_inc(M_stored, 16)
            sp.wait_ge(M_stored, 16)
            stage_end(sp, 0)

            with sp.Fori(0, B) as b:
                for c in range(CPB):
                    p, t = c % 2, CPB * b + c
                    sp.wait_ge(intra_done, done(t - 2))
                    sp.dma_start(kT[:, p], ctxT[bass.ds(b, 1), :, c * P:(c + 1) * P].rearrange("o (k p) s -> p (o k) s", p=P)).then_inc(tile_loaded[p], 16)
                    sp.dma_start(cx[:, p], ctx[bass.ds(b, 1), c * P:(c + 1) * P, :].rearrange("o p f -> p (o f)")).then_inc(tile_loaded[p], 16)
                    sp.dma_start(Mb[:, p], M_dram[bass.ds(b * 32, NH), c * P:(c + 1) * P].unsqueeze(0).to_broadcast([P, NH, P])).then_inc(tile_loaded[p], 16)
            stage_end(sp, 1)
            if stop <= 1:
                store_X()
                return

            sp.dma_start(rw[:, :, :], router_wT.rearrange("(k p) e -> p k e", p=P)).then_inc(rout_loaded, 16)
            sp.dma_start(eb[:, :], e_bias.rearrange("(o f) -> o f", o=1).to_broadcast([P, NE])).then_inc(rout_loaded, 16)
            sp.wait_ge(xn2_ready, NT)
            sp.dma_start(Xs[0:SHARED_ROWS, :].rearrange("(t p) f -> p t f", p=P), xn2[:, :, :]).then_inc(zero_filled, 16)
            sp.wait_ge(zero_filled, 32)
            stage_end(sp, 2)
            if stop <= 2:
                return

            def load_tile(i, m):
                p, n = m % 2, sp.snap(2 * i + m)
                row, turned, split = sp.snap(n * MT), sp.snap(done(2 * n - 3, 3)), sp.snap(done(n - 2))
                sp.wait_ge(xT_e, turned)
                sp.sem_inc(sp_note, 1)
                for s in (gw_hi, gw_lo, dw_hi, dw_lo):
                    sp.wait_ge(s, split)
                sp.dma_start(xr[:, p], Xs[bass.ds(row, MT), :].rearrange("(q p) f -> p q f", p=P)).then_inc(xr_loaded[p], 16)
                e = sp.value_load(etab[0:1, bass.ds(n, 1)], min_val=0, max_val=NE)
                sp.dma_start(gu_raw[:, p], gate_upT[bass.ds(e, 1)].rearrange("o p k f -> p (o k) f")).then_inc(ew_loaded[p], 16)
                sp.dma_start(dn_raw[:, p], downT[bass.ds(e, 1)].rearrange("o p j f -> p (o j) f")).then_inc(ew_loaded[p], 16)

            def store_half(i, k):
                u, q = 4 * i + k, k % 2
                sp.wait_ge(y_e, done(u))
                sp.dma_start(Ys[bass.ds(u * P, P), :], yo[:, q]).then_inc(ys_written[q], 16)

            for m in range(3):
                load_tile(0, m)
            for i, k, looped in expert_steps(sp):
                if k % 2 == 0 and (looped or 2 * i + k // 2 + 2 < ETILES):
                    load_tile(i, k // 2 + 2)
                store_half(i, k - 1)
            store_half(0, HALVES - 1)
            for q in range(2):
                sp.wait_ge(ys_written[q], 16 * (ETILES + 1))
            stage_end(sp, 3)

            for t in range(NT):
                if t >= 2:
                    sp.wait_ge(g_used, t - 1)
                sp.dma_start(G[:, t % 2, TOPK, :], Ys[t * P:(t + 1) * P, :]).then_inc(gs_loaded[t % 2], 16)
            with sp.Fori(0, B) as b:
                sp.wait_ge(ctx_hi, done(b - 1))
                sp.wait_ge(ctx_lo, done(b - 1))
                sp.dma_start(cr[:, 0], ctx[bass.ds(b, 1)].rearrange("o (i p) f -> p (o i) f", p=P)).then_inc(cr_loaded, 16)
                sp.dma_start(cr[:, 1], ctxT[bass.ds(b, 1)].rearrange("o (k p) s -> p (o k) s", p=P)).then_inc(cr_loaded, 16)
            stage_end(sp, 4)
            if stop <= 4:
                store_X()
                return

            with sp.Fori(0, NBLK // 2) as i:
                for p in range(2):
                    blk = 2 * i + p
                    sp.wait_ge(fw_hi, done(blk - 2))
                    sp.wait_ge(fw_lo, done(blk - 2))
                    for m, w in enumerate((w_gateT, w_upT, w_downT)):
                        sp.dma_start(w_raw[:, p, m], w[bass.ds(blk, 1)].rearrange("o p f -> p (o f)")).then_inc(fw_loaded[p], 16)
            for g in range(B):
                sp.wait_ge(fadd, done(4 * (UNITS - B + g) + 3, 4))
                sp.dma_start(out[g].rearrange("(i p) f -> p i f", p=P), X[:, CPB * g:CPB * (g + 1), :]).then_inc(out_written, 16)
            sp.wait_ge(out_written, 16 * B)

        @block.gpsimd
        def _(pool):
            for s in (qe_ready, kw_ready, arg_masked, St_ready, gw_lo, dw_lo, ctx_lo, fw_lo, fh_lo_ready):
                pool.sem_inc(s, 2)
            steps = Steps(pool, pool_step)
            steps(pool.memset(wg[:, :, :], 0.0))
            pool.sem_inc(wg_zeroed, 1)
            pool.memset(eps[:, 0:1], EPS_LN)
            pool.memset(eps[:, 1:2], EPS_H)
            pool.memset(onesf[:, :], 1.0)
            pool.memset(zero[:, :], 0.0)
            pool.memset(IG[:, :], 0.0)
            pool.memset(FG[:, :], 0.0)
            pool.memset(bms[:, :], QSCALE)
            pool.memset(bmask[:, :], 1.0)
            steps(pool.memset(ident[:, :], 0.0))
            steps(pool.affine_select(out=ident[:, :], in_=ident[:, :], compare_op=ALU.not_equal, fill=1.0,
                                     base=0, pattern=[[-1, P]], channel_multiplier=1))
            for m in (bms, bmask):
                steps(pool.affine_select(out=m[:, :], in_=m[:, :], compare_op=ALU.is_ge, fill=0.0,
                                         base=0, pattern=[[-DH, HPG]], channel_multiplier=1))
                steps(pool.affine_select(out=m[:, :], in_=m[:, :], compare_op=ALU.is_ge, fill=0.0,
                                         base=DH - 1, pattern=[[DH, HPG]], channel_multiplier=-1))
            for j in range(2):
                steps(pool.tensor_copy(mask264[:, HPG * j:HPG * (j + 1), :], bc(bmask[:, :], [P, HPG, V1])))
            pool.sem_inc(consts_ready, 1)
            stage_end(pool, 0)

            steps(pool.memset(v1[:, :, :, :], 1.0))
            pool.sem_inc(consts_ready, 1)
            masked = pool.to_reg(NEG)
            with pool.Fori(0, B) as b:
                for c in range(CPB):
                    p, t = c % 2, CPB * b + c
                    pool.wait_ge(intra_done, done(t - 2))
                    for j in range(NG):
                        ins = pool.tensor_tensor(qe[:, p, j], qT[:, j, bass.ds(t * P, P)].unsqueeze(1).to_broadcast([P, HPG, P]),
                                                 bc(bms[:, :], [P, HPG, P]), ALU.mult)
                    ins.then_inc(qe_ready, 1)
                    if c < CPB - 1:
                        pool.wait_ge(tile_loaded[p], 48 * (2 * b + c // 2 + 1))
                        pool.tensor_tensor(kw[:, p], heads(cx[:, p]), bc(tk[:, 1, c, bass.ds(b * 32, NH)], [P, NH, DH]),
                                           ALU.mult).then_inc(kw_ready, 1)
                    pool.wait_ge(arg_ready, done(t))
                    pool.sem_inc(pool_note, 1)
                    pool.affine_select(out=Dm[:, p], in_=Dm[:, p], compare_op=ALU.is_ge, fill=masked,
                                       base=0, pattern=[[0, NH], [1, P]], channel_multiplier=-1).then_inc(arg_masked, 1)
                    if c < CPB - 1:
                        pool.wait_ge(inter_done, done(3 * b + c - 1))
                        if c > 0:
                            pool.tensor_tensor(St[:, :, :], St[:, :, :], bc(decB[:, c, bass.ds(b * 32, NH)], [P, NH, V1]),
                                               ALU.mult).then_inc(St_decayed, 1)
                            pool.wait_ge(St_decayed, 3 * b + c + 1)
                        pool.wait_ge(stm_ready, done(3 * b + c))
                        if c == 0:
                            pool.sem_inc(St_decayed, 1)
                            pool.tensor_copy(St[:, :, :], stm[:, :, :]).then_inc(St_ready, 1)
                        else:
                            pool.tensor_tensor(St[:, :, :], St[:, :, :], stm[:, :, :], ALU.add).then_inc(St_ready, 1)
            stage_end(pool, 1)
            if stop <= 1:
                return

            pool.memset(onesb[:, :], 1.0)
            pool.memset(tri[:, :], 1.0)
            pool.memset(d0[:, :, :], 1.0)
            pool.memset(ton[:, :], 1.0)
            pool.iota(iota256[:, :], [[MT, 8]], base=0, channel_multiplier=0, allow_small_or_imprecise_dtypes=True)
            pool.iota(iotan[:, :], [[1, ETILES + 1]], base=0, channel_multiplier=0, allow_small_or_imprecise_dtypes=True)
            steps(pool.iota(iotam[:, :], [[1, NE]], base=-99, channel_multiplier=0, allow_small_or_imprecise_dtypes=True))
            pool.affine_select(out=tri[:, :], in_=tri[:, :], compare_op=ALU.is_gt, fill=0.0,
                               base=0, pattern=[[1, P]], channel_multiplier=-1)
            steps(pool.affine_select(out=d0[:, :, :], in_=d0[:, :, :], compare_op=ALU.is_gt, fill=0.0,
                                     base=0, pattern=[[0, NE], [1, NT]], channel_multiplier=0))
            pool.sem_inc(consts_ready, 1)
            pool.wait_ge(slots_ready, 1)
            pool.wait_ge(zero_filled, 32)
            for t in range(NT):
                for k in range(TOPK):
                    pool.indirect_dma_start(out=Xs, out_offset=bass.IndirectOffsetOnAxis(ap=slot[:, t, k:k + 1], axis=0),
                                            in_=xn2[:, t, :], in_offset=None).then_inc(xs_written, 16)
            pool.wait_ge(xs_written, 16 * NT * TOPK)
            stage_end(pool, 2)
            if stop <= 2:
                return

            def gu_split(i, m):
                p, n = m % 2, 2 * i + m
                pool.wait_ge(gw_hi, done(n))
                pool.tensor_tensor(gu_lo[:, p], gu_raw[:, p], gu_hi[:, p].bitcast(F32), ALU.subtract).then_inc(gw_lo, 1)

            def dn_split(i, m):
                p, n = m % 2, 2 * i + m
                pool.wait_ge(dw_hi, done(n))
                pool.tensor_tensor(dn_lo[:, p], dn_raw[:, p], dn_hi[:, p].bitcast(F32), ALU.subtract).then_inc(dw_lo, 1)

            gu_split(0, 0)
            dn_split(0, 0)
            gu_split(0, 1)
            for i, k, looped in expert_steps(pool):
                if k % 2 == 1 and (looped or 2 * i + (k + 1) // 2 < ETILES):
                    dn_split(i, (k + 1) // 2)
                if k % 2 == 0 and (looped or 2 * i + (k + 2) // 2 < ETILES):
                    gu_split(i, (k + 2) // 2)
            stage_end(pool, 3)

            for t in range(NT):
                if t >= 2:
                    pool.wait_ge(g_used, t - 1)
                for k in range(TOPK):
                    pool.indirect_dma_start(out=G[:, t % 2, k, :], out_offset=None, in_=Ys,
                                            in_offset=bass.IndirectOffsetOnAxis(ap=slot[:, t, k:k + 1], axis=0)).then_inc(g_loaded[t % 2], 16)
            with pool.Fori(0, B) as b:
                pool.wait_ge(ctx_hi, done(b))
                pool.tensor_tensor(k_lo[:, :, :], cr[:, 0], k_hi[:, :, :].bitcast(F32), ALU.subtract)
                pool.tensor_tensor(v_lo[:, :, :], cr[:, 1], v_hi[:, :, :].bitcast(F32), ALU.subtract).then_inc(ctx_lo, 1)
            stage_end(pool, 4)
            if stop <= 4:
                return

            def w_split(i, m):
                p, blk = m % 2, 2 * i + m
                pool.wait_ge(fw_hi, done(blk))
                pool.tensor_tensor(w_lo[:, p], w_raw[:, p], w_hi[:, p].bitcast(F32), ALU.subtract).then_inc(fw_lo, 1)

            def h_split(i, k):
                for j in range(HCB):
                    pool.wait_ge(fh_hi_ready, done(HCB * (8 * i + k) + j))
                    pool.tensor_tensor(fh_lo[:, k % 2, j], fh[:, j], fh_hi[:, k % 2, j].bitcast(F32), ALU.subtract).then_inc(fh_lo_ready, 1)

            w_split(0, 0)
            h_split(0, 0)
            for i, k, looped in ffn_steps(pool):
                h_split(i, k)
                if k % 4 == 2 and (looped or 2 * i + (k + 2) // 4 < NBLK):
                    w_split(i, (k + 2) // 4)

        @block.scalar
        def _(act):
            for s in (qs_ready, v1_ready, D_ready, sq_ready, rsh_ready, gw_hi, dw_hi, x_hi_e, sg_e, h_hi_e, y_e,
                      ctx_hi, q_hi_x, s_sig, fw_hi, fsg_ready, fh_hi_ready):
                act.sem_inc(s, 2)
            steps = Steps(act, act_step)

            def rstd_of(tiles):
                steps(act.activation(lnv[:, tiles], mv[:, tiles, 1], ACT.Ln, bias=eps[:, 0:1]))
                return act.activation(rstd[:, tiles], lnv[:, tiles], ACT.Exp, scale=-0.5)

            act.wait_ge(consts_ready, 1)
            for b in range(B):
                act.wait_ge(mv_ready, b + 1)
                rstd_of(slice(CPB * b, CPB * (b + 1))).then_inc(rstd_ready, 1)
                for k in range(KC):
                    act.wait_ge(xT_done, KC * b + k + 1)
                    act.activation(qT[:, k, b * S:(b + 1) * S], (pA, pB)[k // 2][:, k % 2], ACT.Copy).then_inc(xT_kept, 1)
            act.wait_ge(gates_kept, B)
            steps(act.activation(t1[:, :], FG[:, :], ACT.Abs))
            steps(act.activation(t2[:, :], t1[:, :], ACT.Exp, scale=-1.0))
            act.activation(t1[:, :], t2[:, :], ACT.Ln, bias=1.0).then_inc(lsig_ready, 1)
            act.wait_ge(aM_ready, 2)
            for c in range(CPB):
                cs = slice(c * P, (c + 1) * P)
                act.activation(WQ[:, cs], Mq[:, cs], ACT.Exp, bias=mprev[:, c:c + 1], scale=-1.0)
                act.activation(WK[:, cs], Aq[:, cs], ACT.Exp, bias=mneg[:, c:c + 1])
                act.activation(dec[:, c:c + 1], mprev[:, c:c + 1], ACT.Exp, bias=mneg[:, c:c + 1])
            act.activation(NR[:, :], t2[:, :], ACT.Exp, scale=-1.0).then_inc(exps_ready, 1)
            for q in range(4):
                act.wait_ge(tok_done, q + 1)
                act.activation(flat(tk[:, q]), (pA, pB)[q // 2][:, q % 2], ACT.Copy)
            act.wait_ge(tok_done, 5)
            act.activation(flat(decB[:, :, :]), pC[:, 0], ACT.Copy)
            stage_end(act, 0)

            act.wait_ge(consts_ready, 2)
            with steps.loop(B, CPB) as b:
                for c in range(CPB):
                    p, t = c % 2, CPB * b + c
                    act.wait_ge(intra_done, done(t - 2))
                    if c > 0:
                        act.activation(qs[:, p], qT[:, :, bass.ds(t * P, P)], ACT.Copy, scale=QSCALE).then_inc(qs_ready, 1)
                    act.wait_ge(tile_loaded[p], 48 * (2 * b + c // 2 + 1))
                    act.activation(v1[:, p, :, 0:DH], heads(cx[:, p]), ACT.Copy).then_inc(v1_ready, 1)
                    act.wait_ge(arg_masked, done(t))
                    act.activation(Dm[:, p], Dm[:, p], ACT.Exp).then_inc(D_ready, 1)
                    act.wait_ge(hc_ready, done(t))
                    act.activation(sq[:, :, :], hc[:, :, :], ACT.Square).then_inc(sq_ready, 1)
                    act.wait_ge(var_ready, done(t))
                    steps(act.activation(lnh[:, :], vsum[:, :], ACT.Ln, bias=eps[:, 1:2], scale=1.0 / DH))
                    act.activation(rsh[:, :], lnh[:, :], ACT.Exp, scale=-0.5).then_inc(rsh_ready, 1)
            stage_end(act, 1)
            if stop <= 1:
                return

            act.wait_ge(mv_ready, B + 1)
            rstd_of(slice(0, NT)).then_inc(rstd_ready, 1)
            for t in range(NT):
                act.wait_ge(xT_done, KC * B + t + 1)
                if t >= 2:
                    act.wait_ge(sc_done, t - 1)
                act.activation(flat(xT2[:, t % 2]), pA[:, t % 2], ACT.Copy).then_inc(xT_kept, 1)
            act.wait_ge(sc_done, NT)
            act.activation(flat(sc[:, :, :]), pC[:, 0, 0:NT * NE], ACT.Sigmoid).then_inc(sc_ready, 1)
            stage_end(act, 2)
            if stop <= 2:
                return

            def gu_split(i, m):
                p, n = m % 2, 2 * i + m
                act.wait_ge(ew_loaded[p], 32 * (i + m // 2 + 1))
                act.wait_ge(gu_e, done(2 * n - 3, 3))
                act.activation(gu_hi[:, p], gu_raw[:, p], ACT.Copy).then_inc(gw_hi, 1)

            def dn_split(i, m):
                p, n = m % 2, 2 * i + m
                act.wait_ge(ew_loaded[p], 32 * (i + m // 2 + 1))
                act.wait_ge(dn_e, done(2 * n - 3, 3))
                act.activation(dn_hi[:, p], dn_raw[:, p], ACT.Copy).then_inc(dw_hi, 1)

            def x_split(i, k):
                u, q = 4 * i + k, k % 2
                act.wait_ge(xT_e, done(u, 3))
                act.wait_ge(gu_e, done(u - 2, 3))
                act.activation(flat(x_hi[:, q]), pA[:, q], ACT.Copy).then_inc(x_hi_e, 1)

            def silu(i, k):
                u, q = 4 * i + k, k % 2
                act.wait_ge(gu_e, done(u, 3))
                act.wait_ge(hh_e, done(u - 2))
                act.activation(sg[:, q], pB[:, q, 0:FI], ACT.Silu).then_inc(sg_e, 1)

            def h_split(i, k):
                u, q = 4 * i + k, k % 2
                act.wait_ge(hT_e, done(u))
                act.wait_ge(dn_e, done(u - 2, 3))
                act.activation(flat(h_hi[:, q]), pC[0:FH, q, 0:2 * P], ACT.Copy).then_inc(h_hi_e, 1)

            def y_keep(i, k):
                u, q = 4 * i + k, k % 2
                act.wait_ge(dn_e, done(u, 3))
                act.wait_ge(ys_written[q], 16 * (2 * i + k // 2 + 1))
                act.activation(yo[:, q], pD[:, q], ACT.Copy).then_inc(y_e, 1)

            gu_split(0, 0)
            x_split(0, 0)
            x_split(0, 1)
            dn_split(0, 0)
            silu(0, 0)
            gu_split(0, 1)
            for i, k, looped in expert_steps(act):
                h_split(i, k - 1)
                if looped or 4 * i + k + 1 < HALVES:
                    x_split(i, k + 1)
                silu(i, k)
                y_keep(i, k - 1)
                if k % 2 == 1 and (looped or 2 * i + (k + 1) // 2 < ETILES):
                    dn_split(i, (k + 1) // 2)
                if k % 2 == 0 and (looped or 2 * i + (k + 2) // 2 < ETILES):
                    gu_split(i, (k + 2) // 2)
            h_split(0, HALVES - 1)
            y_keep(0, HALVES - 1)
            stage_end(act, 3)

            act.wait_ge(mv_ready, B + 2)
            rstd_of(slice(0, NT)).then_inc(rstd_ready, 1)
            with act.Fori(0, B) as b:
                act.wait_ge(cr_loaded, 32 * (b + 1))
                act.wait_ge(o_done, done(KC * b - 1))
                act.activation(k_hi[:, :, :], cr[:, 0], ACT.Copy)
                act.activation(v_hi[:, :, :], cr[:, 1], ACT.Copy).then_inc(ctx_hi, 1)
                act.wait_ge(qf_ready, b + 1)
                act.activation(q_hi[:, :, :], qf[:, :, :], ACT.Copy).then_inc(q_hi_x, 1)
                for n in range(KC):
                    act.wait_ge(s_done, KC * b + n + 1)
                    act.activation(sf[:, n], pA[:, n % 2], ACT.Sigmoid, scale=XSCALE).then_inc(s_sig, 1)
                    act.wait_ge(s_sig, done(KC * b + n))
                    act.activation(s_hi[:, n], sf[:, n], ACT.Copy).then_inc(s_hi_x, 1)
            stage_end(act, 4)
            if stop <= 4:
                return

            act.wait_ge(mv_ready, B + 3)
            rstd_of(slice(0, NT)).then_inc(rstd_ready, 1)
            with act.Fori(0, NT // 2) as i:
                for q in range(2):
                    t = 2 * i + q
                    act.wait_ge(fT_done, t + 1)
                    act.activation(f_hi[:, :, bass.ds(t * P, P)], pA[:, q].rearrange("p (k n) -> p k n", k=KC), ACT.Copy).then_inc(f_hi_ready, 1)

            def w_split(i, m):
                p, blk = m % 2, 2 * i + m
                act.wait_ge(fw_loaded[p], 48 * (i + m // 2 + 1))
                act.wait_ge(fdn, done(4 * (4 * blk - 5) + 3, 20))
                act.activation(w_hi[:, p], w_raw[:, p], ACT.Copy).then_inc(fw_hi, 1)

            def gated(i, k):
                v = 8 * i + k
                for j in range(HCB):
                    act.wait_ge(fgu, done(HCB * v + j))
                    act.wait_ge(fh_ready, done(HCB * v + j - 2))
                    act.activation(fsg[:, j], pA[:, j], ACT.Silu).then_inc(fsg_ready, 1)
                for j in range(HCB):
                    act.wait_ge(fh_ready, done(HCB * v + j))
                    act.wait_ge(fdn, done(4 * (v - 2) + 3, 20))
                    act.activation(fh_hi[:, k % 2, j], fh[:, j], ACT.Copy).then_inc(fh_hi_ready, 1)

            w_split(0, 0)
            gated(0, 0)
            for i, k, looped in ffn_steps(act):
                gated(i, k)
                if k % 4 == 2 and (looped or 2 * i + (k + 2) // 4 < NBLK):
                    w_split(i, (k + 2) // 4)

        @block.vector
        def _(dve):
            for s in (arg_ready, C_ready, h1_read, stm_ready, hc_ready, var_ready, x_lo_e, hh_e, h_lo_e, o_added, fh_ready):
                dve.sem_inc(s, 2)
            dve.sem_inc(fadd, 4)
            steps = Steps(dve, dve_step)

            def gates_keep(b):
                dve.wait_ge(gates_done, b + 1)
                dve.tensor_scalar(IG[32 * b:32 * b + NH, :], pC[0:NH, b % 2], gb[0:NH, 0:1], None, ALU.add)
                dve.tensor_scalar(FG[32 * b:32 * b + NH, :], pC[32:32 + NH, b % 2], gb[32:32 + NH, 0:1], None, ALU.add).then_inc(gates_kept, 1)

            def f_split(t):
                dve.wait_ge(f_hi_ready, t + 1)
                ts = slice(t * P, (t + 1) * P)
                dve.tensor_tensor(f_lo[:, :, ts], pA[:, t % 2].rearrange("p (k n) -> p k n", k=KC), f_hi[:, :, ts].bitcast(F32),
                                  ALU.subtract).then_inc(f_lo_ready, 1)

            def stats_of(t):
                steps(dve.bn_stats(stats[:, t, :], X[:, t, :]))
                return dve.bn_aggr(mv[:, t, :], stats[:, t, :])

            def normed(dst, t):
                return dve.tensor_scalar(dst, X[:, t, :], mv[:, t, 0:1], rstd[:, t:t + 1], ALU.subtract, ALU.mult)

            dve.wait_ge(small_loaded, 80)
            dve.tensor_tensor(wg[:, KC:2 * KC, :], wg[:, KC:2 * KC, :], wg[:, 2 * KC:, :], ALU.add).then_inc(wg_ready, 1)
            for b in range(B):
                dve.wait_ge(x_loaded[b], 16)
                for i in range(CPB):
                    ins = stats_of(CPB * b + i)
                ins.then_inc(mv_ready, 1)
                dve.wait_ge(mv_ready, b + 1)
                dve.wait_ge(rstd_ready, b + 1)
                if b >= 2:
                    dve.wait_ge(xT_done, KC * (b - 1))
                for i in range(CPB):
                    ins = normed(qn[:, b % 2, i, :], CPB * b + i)
                ins.then_inc(qn_ready, 1)
                if b >= 1:
                    gates_keep(b - 1)
            gates_keep(B - 1)
            dve.wait_ge(gates_kept, B)
            dve.wait_ge(lsig_ready, 1)
            steps(dve.scalar_tensor_tensor(out=t2[:, :], in0=FG[:, :], scalar=0.0, in1=t1[:, :], op0=ALU.min, op1=ALU.subtract))
            steps(dve.tensor_tensor_scan(Fc[:, :], onesf[:, :], t2[:, :], 0.0, ALU.mult, ALU.add))
            steps(dve.tensor_tensor(Aq[:, :], IG[:, :], Fc[:, :], ALU.subtract))
            dve.tensor_tensor_scan(Mq[:, :], onesf[:, :], Aq[:, :], -3e38, ALU.mult, ALU.max).then_inc(aM_ready, 1)
            dve.wait_ge(aM_ready, 1)
            dve.tensor_tensor(t2[:, :], Fc[:, :], Mq[:, :], ALU.add)
            dve.tensor_copy(mprev[:, 0:1], Mq[:, 0:1])
            dve.tensor_copy(mprev[:, 1:CPB], Mq[:, P - 1:S - P:P])
            dve.tensor_scalar(mneg[:, :], Mq[:, P - 1:S:P], -1.0, None, ALU.mult).then_inc(aM_ready, 1)
            dve.wait_ge(exps_ready, 1)
            for c in range(CPB):
                ins = dve.tensor_scalar(DG[:, c, :], ident[:, :], dec[:, c:c + 1], None, ALU.mult)
            ins.then_inc(dg_ready, 1)
            stage_end(dve, 0)

            dve.wait_ge(small_loaded, 80)
            with steps.loop(B, MLSTM_STEPS) as b:
                for c in range(CPB):
                    p, t, ic = c % 2, CPB * b + c, 3 * b + c - 1
                    cols = bass.ds(b * 32, NH)
                    dve.wait_ge(tile_loaded[p], 48 * (2 * b + c // 2 + 1))
                    dve.tensor_tensor(Dm[:, p], bc(tk[:, 3, c, cols], [P, NH, P]), Mb[:, p], ALU.subtract).then_inc(arg_ready, 1)
                    dve.wait_ge(D_ready, done(t))
                    dve.wait_ge(intra_done, done(t - 2))
                    for j in range(NG):
                        dve.wait_ge(qk_done, done(NG * t + j))
                        dve.tensor_tensor(Cm[:, p, HPG * j:HPG * (j + 1), :], Dm[:, p, HPG * j:HPG * (j + 1), :],
                                          pA[:, j % 2].rearrange("p (i s) -> p i s", i=HPG), ALU.mult).then_inc(C_ready, 1)
                    if c < CPB - 1:
                        dve.wait_ge(st_done, done(3 * b + c))
                        dve.wait_ge(St_ready, done(3 * b + c - 1))
                        dve.tensor_tensor(stm[:, :, :].rearrange("p (j h) e -> p j (h e)", j=2), pD[:, :, 0:8 * V1],
                                          mask264[:, :, :].rearrange("p h e -> p (h e)").unsqueeze(1).to_broadcast([P, 2, 8 * V1]),
                                          ALU.mult).then_inc(stm_ready, 1)
                    OUT = pB[:, :, 0:8 * V1].rearrange("p j (h e) -> p j h e", e=V1)
                    INT = pC[:, :, 0:8 * V1].rearrange("p j (h e) -> p j h e", e=V1)
                    H1 = h1[:, :, :].rearrange("p (j h) e -> p j h e", j=2)
                    dve.wait_ge(intra_done, done(t))
                    if c == 0:
                        dve.tensor_copy(H1, OUT).then_inc(h1_read, 1)
                    else:
                        dve.wait_ge(inter_done, done(ic))
                        wq = tk[:, 0, c, cols].rearrange("p (j h) -> p j h", j=2).unsqueeze(3).to_broadcast([P, 2, 8, V1])
                        steps(dve.tensor_tensor(H1, INT, wq, ALU.mult))
                        dve.tensor_tensor(H1, H1, OUT, ALU.add).then_inc(h1_read, 1)
                    dve.wait_ge(h1_read, done(t))
                    steps(dve.scalar_tensor_tensor(out=den[:, :], in0=h1[:, :, DH], scalar=-1.0, in1=h1[:, :, DH],
                                                   op0=ALU.mult, op1=ALU.max))
                    steps(dve.tensor_tensor(den[:, :], den[:, :], tk[:, 2, c, cols], ALU.max))
                    steps(dve.tensor_scalar(den[:, :], den[:, :], EPS_H, None, ALU.add))
                    steps(dve.reciprocal(rec[:, :], den[:, :]))
                    steps(dve.tensor_tensor(hs[:, :, :], h1[:, :, 0:DH], bc(rec[:, :], [P, NH, DH]), ALU.mult))
                    steps(dve.tensor_reduce(hsum[:, :], hs[:, :, :], AX.X, ALU.add))
                    dve.scalar_tensor_tensor(out=hc[:, :, :], in0=bc(hsum[:, :], [P, NH, DH]), scalar=-1.0 / DH, in1=hs[:, :, :],
                                             op0=ALU.mult, op1=ALU.add).then_inc(hc_ready, 1)
                    dve.wait_ge(sq_ready, done(t))
                    dve.tensor_reduce(vsum[:, :], sq[:, :, :], AX.X, ALU.add).then_inc(var_ready, 1)
                    steps(dve.tensor_tensor(hs[:, :, :], hc[:, :, :], heads(lnb[:, :]), ALU.mult))
                    dve.wait_ge(rsh_ready, done(t))
                    steps(dve.tensor_tensor(hs[:, :, :], hs[:, :, :], bc(rsh[:, :], [P, NH, DH]), ALU.mult))
                    Xt = X[:, bass.ds(t, 1), :].rearrange("p o f -> p (o f)")
                    steps(dve.tensor_tensor(Xt, Xt, hs[:, :, :].rearrange("p h d -> p (h d)"), ALU.add))
            stage_end(dve, 1)
            if stop <= 1:
                return

            for t in range(NT):
                ins = stats_of(t)
            ins.then_inc(mv_ready, 1)
            dve.wait_ge(mv_ready, B + 1)
            dve.wait_ge(rstd_ready, B + 1)
            for t in range(NT):
                normed(xn2[:, t, :], t).then_inc(xn2_ready, 1)
            dve.wait_ge(rout_loaded, 32)
            dve.wait_ge(consts_ready, 3)
            dve.wait_ge(sc_ready, 1)
            steps(dve.tensor_tensor(sw[:, :, :], sc[:, :, :], eb[:, :].unsqueeze(1).to_broadcast([P, NT, NE]), ALU.add))
            iot = iotam[:, :].unsqueeze(1).to_broadcast([P, NT, NE])
            for k in range(TOPK):
                steps(dve.tensor_reduce(mx[:, :], sw[:, :, :], AX.X, ALU.max))
                steps(dve.tensor_tensor(eq[:, :, :], sw[:, :, :], bc(mx[:, :], [P, NT, NE]), ALU.is_equal))
                steps(dve.tensor_tensor(eq[:, :, :], eq[:, :, :], iot, ALU.mult))
                steps(dve.tensor_reduce(ix[:, :], eq[:, :, :], AX.X, ALU.min))
                steps(dve.tensor_tensor(oh[:, k], iot, bc(ix[:, :], [P, NT, NE]), ALU.is_equal))
                steps(dve.scalar_tensor_tensor(out=flat(sw[:, :, :]), in0=flat(oh[:, k]), scalar=NEG, in1=flat(sw[:, :, :]),
                                               op0=ALU.mult, op1=ALU.add))
                steps(dve.tensor_tensor(pr[:, :, :], oh[:, k], sc[:, :, :], ALU.mult))
                steps(dve.tensor_reduce(ckr[:, k], pr[:, :, :], AX.X, ALU.add))
            steps(dve.tensor_tensor(pr[:, :, :], oh[:, 0], oh[:, 1], ALU.add))
            steps(dve.tensor_tensor(eq[:, :, :], oh[:, 2], oh[:, 3], ALU.add))
            dve.tensor_tensor(selb[:, :, :], pr[:, :, :], eq[:, :, :], ALU.add).then_inc(sel_ready, 1)
            steps(dve.tensor_reduce(csum[:, :], ckr[:, :, :].rearrange("p k t -> p t k"), AX.X, ALU.add))
            steps(dve.tensor_scalar(csum[:, :], csum[:, :], 1e-20, None, ALU.add))
            steps(dve.reciprocal(crec[:, :], csum[:, :]))
            dve.tensor_tensor(ck[:, :, :], ckr[:, :, :].rearrange("p k t -> p t k"), bc(crec[:, :], [P, NT, TOPK]), ALU.mult)
            dve.wait_ge(pos_done, 1)
            steps(dve.tensor_copy(cnt[:, :, :], pC[:, 1, 256:512].rearrange("p (t e) -> p e t", e=NE)))
            steps(dve.tensor_tensor_scan(flat(incl[:, :, :]), flat(d0[:, :, :]), flat(cnt[:, :, :]), 0.0, ALU.mult, ALU.add))
            steps(dve.tensor_tensor(excl[:, :, :], incl[:, :, :], cnt[:, :, :], ALU.subtract))
            steps(dve.tensor_tensor(nt8[:, :, :], bc(incl[:, :, NT - 1], [P, NE, 8]), iota256[:, :].unsqueeze(1).to_broadcast([P, NE, 8]), ALU.is_gt))
            steps(dve.tensor_reduce(nte[:, :], nt8[:, :, :], AX.X, ALU.add))
            steps(dve.tensor_tensor_scan(tinc[:, :], ton[:, :], nte[:, :], 0.0, ALU.mult, ALU.add))
            steps(dve.tensor_tensor(texc[:, :], tinc[:, :], nte[:, :], ALU.subtract))
            steps(dve.tensor_scalar(rowb[:, :], texc[:, :], float(MT), float(SHARED_ROWS), ALU.mult, ALU.add))
            steps(dve.tensor_tensor(excl[:, :, :], excl[:, :, :], bc(rowb[:, :], [P, NE, NT]), ALU.add))
            steps(dve.tensor_tensor(full[:, :, :], pC[:, 1, 0:256].rearrange("p (t e) -> p t e", e=NE), excl[:, :, :].rearrange("p e t -> p t e"), ALU.add))
            for k in range(TOPK):
                steps(dve.tensor_tensor(pr[:, :, :], oh[:, k], full[:, :, :], ALU.mult))
                steps(dve.tensor_reduce(slf[:, k], pr[:, :, :], AX.X, ALU.add))
            dve.tensor_copy(slot[:, :, :], slf[:, :, :].rearrange("p k t -> p t k")).then_inc(slots_ready, 1)
            steps(dve.tensor_scalar(texc[:, :], texc[:, :], float(SHARED_T), None, ALU.add))
            steps(dve.tensor_tensor(ecmp[:, :, :], bc(iotan[:, :], [1, ETILES + 1, NE]),
                                    texc[0:1, :].unsqueeze(1).to_broadcast([1, ETILES + 1, NE]), ALU.is_ge))
            steps(dve.tensor_reduce(ecf[:, :], ecmp[:, :, :], AX.X, ALU.add))
            dve.tensor_copy(etab[:, :], ecf[:, :])
            stage_end(dve, 2)
            if stop <= 2:
                return

            def x_split(i, k):
                u, q = 4 * i + k, k % 2
                dve.wait_ge(x_hi_e, done(u))
                dve.tensor_tensor(flat(x_lo[:, q]), pA[:, q], flat(x_hi[:, q]).bitcast(F32), ALU.subtract).then_inc(x_lo_e, 1)

            def gate(i, k):
                u, q = 4 * i + k, k % 2
                dve.wait_ge(sg_e, done(u))
                dve.wait_ge(hT_e, done(u - 2))
                dve.tensor_tensor(hh[:, q], sg[:, q], pB[:, q, FI:2 * FI], ALU.mult).then_inc(hh_e, 1)

            def h_split(i, k):
                u, q = 4 * i + k, k % 2
                dve.wait_ge(h_hi_e, done(u))
                dve.tensor_tensor(flat(h_lo[:, q]), pC[0:FH, q, 0:2 * P], flat(h_hi[:, q]).bitcast(F32), ALU.subtract).then_inc(h_lo_e, 1)

            x_split(0, 0)
            x_split(0, 1)
            gate(0, 0)
            for i, k, looped in expert_steps(dve):
                h_split(i, k - 1)
                if looped or 4 * i + k + 1 < HALVES:
                    x_split(i, k + 1)
                gate(i, k)
            h_split(0, HALVES - 1)
            stage_end(dve, 3)

            for t in range(NT):
                dve.wait_ge(gs_loaded[t % 2], 16 * (t // 2 + 1))
                dve.wait_ge(g_loaded[t % 2], 16 * TOPK * (t // 2 + 1))
                steps(dve.tensor_tensor(X[:, t, :], X[:, t, :], G[:, t % 2, TOPK, :], ALU.add))
                for k in range(TOPK):
                    ins = dve.scalar_tensor_tensor(out=X[:, t, :], in0=G[:, t % 2, k, :], scalar=ck[:, t, k:k + 1], in1=X[:, t, :],
                                                   op0=ALU.mult, op1=ALU.add)
                    if k < TOPK - 1:
                        steps(ins)
                ins.then_inc(g_used, 1)
                dve.wait_ge(g_used, t + 1)
            for t in range(NT):
                ins = stats_of(t)
            ins.then_inc(mv_ready, 1)
            dve.wait_ge(mv_ready, B + 2)
            dve.wait_ge(rstd_ready, B + 2)
            with dve.Fori(0, B) as b:
                dve.wait_ge(q_hi_x, done(b - 1))
                for i in range(CPB):
                    t = CPB * b + i
                    ins = dve.tensor_scalar(qf[:, i, :], X[:, bass.ds(t, 1), :].rearrange("p o f -> p (o f)"),
                                            mv[:, bass.ds(t, 1), 0], rstd[:, bass.ds(t, 1)], ALU.subtract, ALU.mult)
                ins.then_inc(qf_ready, 1)
                dve.wait_ge(q_hi_x, done(b))
                dve.tensor_tensor(q_lo[:, :, :], qf[:, :, :], q_hi[:, :, :].bitcast(F32), ALU.subtract).then_inc(q_lo_x, 1)
                for n in range(KC):
                    dve.wait_ge(s_hi_x, KC * b + n + 1)
                    dve.tensor_tensor(s_lo[:, n], sf[:, n], s_hi[:, n].bitcast(F32), ALU.subtract).then_inc(s_lo_x, 1)
                for i in range(CPB):
                    dve.wait_ge(o_done, done(CPB * b + i))
                    Xt = X[:, bass.ds(CPB * b + i, 1), :].rearrange("p o f -> p (o f)")
                    dve.tensor_tensor(Xt, Xt, pB[:, i % 2], ALU.add).then_inc(o_added, 1)
            stage_end(dve, 4)
            if stop <= 4:
                return

            for t in range(NT):
                ins = stats_of(t)
            ins.then_inc(mv_ready, 1)
            dve.wait_ge(mv_ready, B + 3)
            dve.wait_ge(rstd_ready, B + 3)
            for t in range(NT):
                if t >= 2:
                    dve.wait_ge(fT_done, t - 1)
                normed(xn4[:, t % 2], t).then_inc(xn4_ready, 1)
                if t >= 1:
                    f_split(t - 1)
            f_split(NT - 1)

            def gate_f(i, k):
                for j in range(HCB):
                    w = HCB * (8 * i + k) + j
                    dve.wait_ge(fsg_ready, done(w))
                    dve.wait_ge(fh_lo_ready, done(w - 2))
                    dve.tensor_tensor(fh[:, j], fsg[:, j], pB[:, j], ALU.mult).then_inc(fh_ready, 1)

            def add_f(i, k):
                v = 8 * i + k
                for tt in range(CPB):
                    t = CPB * (k % 4) + tt
                    dve.wait_ge(fdn, done(4 * v + tt, 20))
                    dve.tensor_tensor(X[:, t, :], X[:, t, :], (pC, pD)[tt // 2][:, tt % 2], ALU.add).then_inc(fadd, 1)

            gate_f(0, 0)
            for i, k, looped in ffn_steps(dve):
                gate_f(i, k)
                add_f(i, k - 1)
            add_f(0, UNITS - 1)

        @block.tensor
        def _(pe):
            for s in (qk_done, inter_done, intra_done, st_done, hT_e, o_done, fgu):
                pe.sem_inc(s, 2)
            for s in (xT_e, gu_e, dn_e):
                pe.sem_inc(s, 3)
            pe.sem_inc(fdn, 20)

            def product3(out_, pairs):
                n = len(pairs)
                for c, ((ah, al), (bh, bl)) in enumerate(pairs):
                    pe.matmul(out_, ah, bh, start=c == 0, stop=False)
                    pe.matmul(out_, ah, bl, start=False, stop=False)
                    ins = pe.matmul(out_, al, bh, start=False, stop=c == n - 1)
                return ins

            pe.wait_ge(consts_ready, 1)
            for b in range(B):
                pe.wait_ge(qn_ready, b + 1)
                for k in range(KC):
                    if b >= 1:
                        pe.wait_ge(xT_kept, KC * (b - 1) + k + 1)
                    for i in range(CPB):
                        ins = pe.transpose((pA, pB)[k // 2][:, k % 2, i * P:(i + 1) * P], qn[:, b % 2, i, k * P:(k + 1) * P], ident[:, :])
                    ins.then_inc(xT_done, 1)
                pe.wait_ge(wg_ready, 1)
                if b >= 2:
                    pe.wait_ge(gates_kept, b - 1)
                pe.wait_ge(ctxT_loaded[b % 2], 16 * (b // 2 + 1))
                for k in range(KC):
                    pe.matmul(pC[0:64, b % 2], wg[:, KC + k, :], ctxTb[:, b % 2, k], start=k == 0, stop=False)
                for k in range(KC):
                    pe.wait_ge(xT_kept, KC * b + k + 1)
                    ins = pe.matmul(pC[0:64, b % 2], wg[:, k, :], qT[:, k, b * S:(b + 1) * S], start=False, stop=k == KC - 1)
                ins.then_inc(gates_done, 1)
            pe.wait_ge(exps_ready, 1)
            for q, src in enumerate((WQ, WK, NR, Aq)):
                for c in range(CPB):
                    ins = pe.transpose((pA, pB)[q // 2][:, q % 2, c * P:(c + 1) * P], src[:, c * P:(c + 1) * P], ident[:, :])
                ins.then_inc(tok_done, 1)
            pe.wait_ge(dg_ready, 1)
            pe.matmul(pC[:, 0], onesf[:, 0:P], flat(DG[:, :, :]), start=True, stop=True).then_inc(tok_done, 1)
            stage_end(pe, 0)

            with pe.Fori(0, B) as b:
                for c in range(CPB):
                    p, t, ic = c % 2, CPB * b + c, 3 * b + c - 1
                    pe.wait_ge(tile_loaded[p], 48 * (2 * b + c // 2 + 1))
                    pe.wait_ge(qe_ready, done(t))
                    for j in range(NG):
                        pe.wait_ge(C_ready, done(NG * t + j - 2))
                        pe.matmul(pA[:, j % 2], kT[:, p, j], flat(qe[:, p, j]), start=True, stop=True).then_inc(qk_done, 1)
                    pe.wait_ge(h1_read, done(t - 1))
                    if c > 0:
                        pe.wait_ge(qs_ready, done(ic))
                        pe.wait_ge(St_ready, done(3 * b + c - 1))
                        for j in range(NG):
                            w = HPG * V1
                            ins = pe.matmul(pC[:, j // 2, j % 2 * w:(j % 2 + 1) * w], qs[:, p, j],
                                            flat(St[:, HPG * j:HPG * (j + 1), :]), start=True, stop=True)
                        ins.then_inc(inter_done, 1)
                    pe.wait_ge(v1_ready, done(t))
                    if c < CPB - 1:
                        pe.wait_ge(kw_ready, done(3 * b + c))
                        pe.wait_ge(stm_ready, done(3 * b + c - 1))
                        for j in range(NG):
                            w = HPG * V1
                            ins = pe.matmul(pD[:, j // 2, j % 2 * w:(j % 2 + 1) * w], flat(kw[:, p, HPG * j:HPG * (j + 1), :]),
                                            flat(v1[:, p, HPG * j:HPG * (j + 1), :]), start=True, stop=True)
                        ins.then_inc(st_done, 1)
                    for h in range(NH):
                        if h % HPG == 0:
                            pe.wait_ge(C_ready, done(NG * t + h // HPG))
                        ins = pe.matmul(pB[:, h // 8, h % 8 * V1:(h % 8 + 1) * V1], Cm[:, p, h, :], v1[:, p, h, :], start=True, stop=True)
                    ins.then_inc(intra_done, 1)
            stage_end(pe, 1)
            if stop <= 1:
                return

            def scores(t):
                pe.wait_ge(xT_kept, KC * B + t + 1)
                for k in range(KC):
                    ins = pe.matmul(pC[:, 0, t * NE:(t + 1) * NE], xT2[:, t % 2, k], rw[:, k, :], start=k == 0, stop=k == KC - 1)
                ins.then_inc(sc_done, 1)

            pe.wait_ge(rout_loaded, 32)
            for t in range(NT):
                pe.wait_ge(xn2_ready, t + 1)
                if t >= 2:
                    pe.wait_ge(xT_kept, KC * B + t - 1)
                for k in range(KC):
                    ins = pe.transpose(pA[:, t % 2, k * P:(k + 1) * P], xn2[:, t, k * P:(k + 1) * P], ident[:, :])
                ins.then_inc(xT_done, 1)
                if t >= 1:
                    scores(t - 1)
            scores(NT - 1)
            pe.wait_ge(sel_ready, 1)
            pe.wait_ge(consts_ready, 3)
            for t in range(NT):
                pe.matmul(pC[:, 1, t * NE:(t + 1) * NE], tri[:, :], selb[:, t, :], start=True, stop=True)
            pe.matmul(pC[:, 1, 256:512], onesb[:, :], flat(selb[:, :, :]), start=True, stop=True).then_inc(pos_done, 1)
            stage_end(pe, 2)
            if stop <= 2:
                return

            def x_turn(i, k):
                u, q, wp = 4 * i + k, k % 2, k // 2 % 2
                pe.wait_ge(xr_loaded[wp], 16 * (i + k // 4 + 1))
                pe.wait_ge(x_lo_e, done(u - 2))
                for c in range(KC):
                    ins = pe.transpose(pA[:, q, c * P:(c + 1) * P], xr[:, wp, q, c * P:(c + 1) * P], ident[:, :])
                ins.then_inc(xT_e, 1)

            def gate_up(i, k):
                u, q, wp, n = 4 * i + k, k % 2, k // 2 % 2, 2 * i + k // 2
                pe.wait_ge(x_lo_e, done(u))
                pe.wait_ge(gw_lo, done(n))
                pe.wait_ge(hh_e, done(u - 2))
                product3(pB[:, q, 0:2 * FI], [((x_hi[:, q, c], x_lo[:, q, c]), (gu_hi[:, wp, c], gu_lo[:, wp, c])) for c in range(KC)]).then_inc(gu_e, 1)

            def h_turn(i, k):
                u, q = 4 * i + k, k % 2
                pe.wait_ge(hh_e, done(u))
                pe.wait_ge(h_lo_e, done(u - 2))
                for c in range(2):
                    ins = pe.transpose(pC[0:FH, q, c * P:(c + 1) * P], hh[:, q, c * FH:(c + 1) * FH], ident[:, :])
                ins.then_inc(hT_e, 1)

            def down(i, k):
                u, q, wp, n = 4 * i + k, k % 2, k // 2 % 2, 2 * i + k // 2
                pe.wait_ge(h_lo_e, done(u))
                pe.wait_ge(dw_lo, done(n))
                pe.wait_ge(y_e, done(u - 2))
                product3(pD[:, q], [((h_hi[:, q, c], h_lo[:, q, c]), (dn_hi[:, wp, c], dn_lo[:, wp, c])) for c in range(2)]).then_inc(dn_e, 1)

            x_turn(0, 0)
            x_turn(0, 1)
            gate_up(0, 0)
            for i, k, looped in expert_steps(pe):
                h_turn(i, k - 1)
                if looped or 4 * i + k + 1 < HALVES:
                    x_turn(i, k + 1)
                gate_up(i, k)
                down(i, k - 1)
            h_turn(0, HALVES - 1)
            down(0, HALVES - 1)
            stage_end(pe, 3)

            with pe.Fori(0, B) as b:
                pe.wait_ge(ctx_lo, done(b))
                pe.wait_ge(q_lo_x, b + 1)
                for n in range(KC):
                    pe.wait_ge(s_sig, done(KC * b + n - 2))
                    cols = slice(n * P, (n + 1) * P)
                    product3(pA[:, n % 2], [((q_hi[:, i, cols], q_lo[:, i, cols]), (k_hi[:, i], k_lo[:, i])) for i in range(CPB)]).then_inc(s_done, 1)
                pe.wait_ge(s_lo_x, KC * (b + 1))
                for i in range(CPB):
                    pe.wait_ge(o_added, done(CPB * b + i - 2))
                    rows = slice(i * P, (i + 1) * P)
                    product3(pB[:, i % 2], [((v_hi[:, n, rows], v_lo[:, n, rows]), (s_hi[:, n], s_lo[:, n])) for n in range(KC)]).then_inc(o_done, 1)
            stage_end(pe, 4)
            if stop <= 4:
                return

            for t in range(NT):
                pe.wait_ge(xn4_ready, t + 1)
                if t >= 2:
                    pe.wait_ge(f_lo_ready, t - 1)
                for c in range(KC):
                    ins = pe.transpose(pA[:, t % 2, c * P:(c + 1) * P], xn4[:, t % 2, c * P:(c + 1) * P], ident[:, :])
                ins.then_inc(fT_done, 1)
            pe.wait_ge(f_lo_ready, NT)

            def gate_up_f(i, k):
                v, wp, tok = 8 * i + k, k // 4 % 2, slice(k % 4 * 512, (k % 4 + 1) * 512)
                pe.wait_ge(fw_lo, done(2 * i + k // 4))
                for j in range(HCB):
                    pe.wait_ge(fh_ready, done(HCB * v + j - 2))
                    for m, bank in ((0, pA[:, j]), (1, pB[:, j])):
                        def w(t_, c):
                            return t_[:, wp, m, c * BLK + j * P:c * BLK + (j + 1) * P]
                        ins = product3(bank, [((w(w_hi, c), w(w_lo, c)), (f_hi[:, c, tok], f_lo[:, c, tok])) for c in range(KC)])
                    ins.then_inc(fgu, 1)

            def down_f(i, k):
                v, q, wp = 8 * i + k, k % 2, k // 4 % 2
                pe.wait_ge(fh_lo_ready, done(HCB * v + HCB - 1))
                for tt in range(CPB):
                    pe.wait_ge(fadd, done(4 * v + tt - 4, 4))
                    cols = slice(tt * P, (tt + 1) * P)
                    product3((pC, pD)[tt // 2][:, tt % 2],
                             [((fh_hi[:, q, j, cols], fh_lo[:, q, j, cols]),
                               (w_hi[:, wp, 2, j * 512:(j + 1) * 512], w_lo[:, wp, 2, j * 512:(j + 1) * 512])) for j in range(HCB)]).then_inc(fdn, 1)

            gate_up_f(0, 0)
            for i, k, looped in ffn_steps(pe):
                gate_up_f(i, k)
                down_f(i, k - 1)
            down_f(0, UNITS - 1)


def kernel(**inputs):
    import numpy as np
    import concourse.bacc as bacc
    from concourse.bass_utils import run_bass_kernel_spmd

    arrays = layout(inputs)
    nc = bacc.Bacc("TRN2", target_bir_lowering=False, num_devices=1)
    args = [nc.dram_tensor(n, a.shape, mybir.dt.from_np(a.dtype), kind="ExternalInput").ap() for n, a in arrays.items()]
    out = nc.dram_tensor("out", (B, S, E), F32, kind="ExternalOutput").ap()
    build(nc, *args, out)
    return run_bass_kernel_spmd(nc, [arrays], core_ids=[0]).results[0]["out"]


def layout(inputs):
    import numpy as np

    g = {n: np.asarray(a) for n, a in inputs.items()}
    gate_up = np.concatenate([np.concatenate([g["L0_ffn_shared_gate_w"], g["L0_ffn_shared_up_w"]])[None], g["L0_ffn_gate_up_proj"]])
    down = np.concatenate([g["L0_ffn_shared_down_w"][None], g["L0_ffn_down_proj"]])
    a = {
        "x": g["x"], "ctx": g["ctx_2048"], "ctxT": g["ctx_2048"].transpose(0, 2, 1),
        "Wi": g["L0_xattn_Wi"], "bi": g["L0_xattn_bi"], "Wf": g["L0_xattn_Wf"], "bf": g["L0_xattn_bf"],
        "ln_scale": g["L0_xattn_ln_scale"],
        "router_wT": g["L0_ffn_router_w"].T, "e_bias": g["L0_ffn_e_bias"],
        "gate_upT": gate_up.transpose(0, 2, 1).reshape(NE + 1, KC, P, 2 * FI).transpose(0, 2, 1, 3),
        "downT": down.transpose(0, 2, 1).reshape(NE + 1, 2, FH, E).transpose(0, 2, 1, 3),
        "w_gateT": g["L1_ffn_w_gate"].reshape(NBLK, BLK, KC, P).transpose(0, 3, 2, 1).reshape(NBLK, P, KC * BLK),
        "w_upT": g["L1_ffn_w_up"].reshape(NBLK, BLK, KC, P).transpose(0, 3, 2, 1).reshape(NBLK, P, KC * BLK),
        "w_downT": g["L1_ffn_w_down"].T.reshape(NBLK, HCB, P, E).transpose(0, 2, 1, 3).reshape(NBLK, P, HCB * E),
    }
    return {n: np.ascontiguousarray(v) for n, v in a.items()}
```

```python
from contextlib import ExitStack, contextmanager
from itertools import chain

import concourse.bass as bass
from concourse import mybir

F32 = mybir.dt.float32
F32R = mybir.dt.float32r
BF16 = mybir.dt.bfloat16
I32 = mybir.dt.int32
U32 = mybir.dt.uint32
ALU = mybir.AluOpType
ACT = mybir.ActivationFunctionType
AX = mybir.AxisListType

P = 128
B, S, E = 4, 512, 512
NT = B * S // P
CPB = S // P
KC = E // P
NH, DH = 16, 32
HPG = P // DH
NG = NH // HPG
V1 = DH + 1
QSCALE = float(DH) ** -0.5
EPS_LN, EPS_H = 1e-5, 1e-6
NEG = -1e30

NE, TOPK, FI = 16, 4, 192
FH = FI // 2
MT = 256
SHARED_T = B * S // MT
ROUTED_T = (TOPK * B * S + NE * (MT - 1)) // MT
ETILES = SHARED_T + ROUTED_T
HALVES = 2 * ETILES
SHARED_ROWS = SHARED_T * MT
ROWS = ETILES * MT
ZROWS = (ROWS - SHARED_ROWS) // NT
ZP = ZROWS // 8
assert ZP * 8 * NT == ROWS - SHARED_ROWS and ZP <= P

HID = 2048
BLK = 256
NBLK = HID // BLK
HCB = BLK // P
XSCALE = float(S) ** -0.5

QK = 6
X_STEPS = 18
MLSTM_STEPS = 11


class Steps:

    def __init__(self, eng, sem):
        self.eng, self.sem, self.base, self.n = eng, sem, 0, 0

    def __call__(self, ins):
        ins.then_inc(self.sem, 1)
        self.n += 1
        self.eng.wait_ge(self.sem, self.base + self.n)

    def tell(self, ins):
        ins.then_inc(self.sem, 1)
        self.n += 1

    def before(self, k):
        self.eng.wait_ge(self.sem, self.base + self.n - k)

    @contextmanager
    def loop(self, trips, per):
        start = self.base + self.n
        with self.eng.Fori(0, trips) as i:
            self.base, self.n = start + i * per, 0
            yield i
            assert self.n == per, (self.n, per)
        self.base, self.n = start + trips * per, 0


def done(n, credit=2):
    return n + 1 + credit


class Arena:

    def __init__(self, nc, at):
        self.nc, self.at = nc, at

    def __call__(self, name, shape, dt=F32):
        size = {BF16: 2}.get(dt, 4)
        for n in shape[1:]:
            size *= n
        t = self.nc.alloc_sbuf_tensor_at(name, shape, dt, offset=self.at)
        self.at += (size + 31) // 32 * 32
        assert self.at <= self.nc.sbuf_usable_end, (name, self.at)
        return t


def build(nc, x, ctx, ctxT, Wi, bi, Wf, bf, ln_scale, router_wT, e_bias, gate_upT, downT,
          w_gateT, w_upT, w_downT, out, stop=99):
    with ExitStack() as stack:
        def sem(name):
            return stack.enter_context(nc.semaphore(name))

        base = (nc.sbuf_base + 63) // 64 * 64
        keep = Arena(nc, base)
        X = keep("X", [P, NT, E])
        ident = keep("ident", [P, P])
        stats = keep("stats", [P, NT, 6])
        mv = keep("mv", [P, NT, 2])
        std = keep("std", [P, NT])
        rstd = keep("rstd", [P, NT])
        statsx = keep("statsx", [P, CPB, 6])
        mvx = keep("mvx", [P, CPB, 2])
        stdx = keep("stdx", [P, CPB])
        rstdx = keep("rstdx", [P, CPB])
        eps = keep("eps", [P, 2])
        slot = keep("slot", [P, NT, TOPK], U32)
        ck = keep("ck", [P, NT, TOPK])
        etab = keep("etab", [1, ETILES + 1], I32)

        pA, pB, pC, pD = [stack.enter_context(nc.psum_tensor(f"p{n}", [P, 2, 512], F32)) for n in "ABCD"]

        M_dram = nc.dram_tensor("M_dram", (P, S), F32, kind="Internal").ap()
        Xs = nc.dram_tensor("Xs", (ROWS, E), F32, kind="Internal").ap()
        Ys = nc.dram_tensor("Ys", (ROWS, E), F32, kind="Internal").ap()

        a1 = Arena(nc, keep.at)
        qT = a1("qT", [P, NT, KC, P])
        tk = a1("tk", [P, 4, CPB, P])
        decB = a1("decB", [P, CPB, P])
        lnb = a1("lnb", [P, E])
        bms = a1("bms", [P, HPG])
        bmask = a1("bmask", [P, HPG])
        mask264 = a1("mask264", [P, 2 * HPG, V1])
        zero = a1("zero", [P, E])
        wg = a1("wg", [P, 3 * KC, 64])
        gb = a1("gb", [64, 1])
        a1a = Arena(nc, a1.at)
        ctxTb = a1a("ctxTb", [P, 2, KC, S])
        qn = a1a("qn", [P, 2, CPB, E])
        IG = a1a("IG", [P, S])
        FG = a1a("FG", [P, S])
        t1 = a1a("t1", [P, S])
        t2 = a1a("t2", [P, S])
        onesf = a1a("onesf", [P, S])
        Fc = a1a("Fc", [P, S])
        Aq = a1a("Aq", [P, S])
        Mq = a1a("Mq", [P, S])
        WQ = a1a("WQ", [P, S])
        WK = a1a("WK", [P, S])
        NR = a1a("NR", [P, S])
        mprev = a1a("mprev", [P, CPB])
        mneg = a1a("mneg", [P, CPB])
        dec = a1a("dec", [P, CPB])
        DG = a1a("DG", [P, CPB, P])
        a1b = Arena(nc, a1.at)
        kT = a1b("kT", [P, 2, KC, P])
        Mb = a1b("Mb", [P, 2, NH, P])
        cx = a1b("cx", [P, 2, E])
        v1 = a1b("v1", [P, 2, NH, V1])
        kw = a1b("kw", [P, 2, NH, DH])
        qs = a1b("qs", [P, 2, KC, P])
        qe = a1b("qe", [P, 2, NG, HPG, P])
        Dm = a1b("Dm", [P, 2, NH, P])
        Cm = a1b("Cm", [P, 2, NH, P])
        St = a1b("St", [P, NH, V1])
        stm = a1b("stm", [P, NH, V1])
        h1 = a1b("h1", [P, NH, V1])
        sq = a1b("sq", [P, NH, DH])
        hsum = a1b("hsum", [P, NH])
        den = a1b("den", [P, NT, NH])
        vsum = a1b("vsum", [P, NT, NH])
        rec = a1b("rec", [P, NT, NH])
        gain = a1b("gain", [P, NT, NH])

        a2 = Arena(nc, keep.at)
        xn2 = a2("xn2", [P, NT, E])
        xT2 = a2("xT2", [P, 2, KC, P])
        rw = a2("rw", [P, KC, NE])
        eb = a2("eb", [P, NE])
        sc = a2("sc", [P, NT, NE])
        sw = a2("sw", [P, NT, NE])
        eq = a2("eq", [P, NT, NE])
        oh = a2("oh", [P, TOPK, NT, NE])
        pr = a2("pr", [P, NT, NE])
        mx = a2("mx", [P, NT])
        ix = a2("ix", [P, NT])
        csum = a2("csum", [P, NT])
        crec = a2("crec", [P, NT])
        slf = a2("slf", [P, TOPK, NT])
        ckr = a2("ckr", [P, TOPK, NT])
        selb = a2("selb", [P, NT, NE], BF16)
        tri = a2("tri", [P, P], BF16)
        onesb = a2("onesb", [P, P], BF16)
        iotam = a2("iotam", [P, NE])
        iota256 = a2("iota256", [P, 8])
        iotan = a2("iotan", [1, ETILES + 1])
        cnt = a2("cnt", [P, NE, NT])
        d0 = a2("d0", [P, NE, NT])
        incl = a2("incl", [P, NE, NT])
        excl = a2("excl", [P, NE, NT])
        nt8 = a2("nt8", [P, NE, 8])
        nte = a2("nte", [P, NE])
        ton = a2("ton", [P, NE])
        tinc = a2("tinc", [P, NE])
        texc = a2("texc", [P, NE])
        rowb = a2("rowb", [P, NE])
        full = a2("full", [P, NT, NE])
        ecmp = a2("ecmp", [1, ETILES + 1, NE])
        ecf = a2("ecf", [1, ETILES + 1])

        a3 = Arena(nc, a2.at)
        gu_raw = a3("gu_raw", [P, 2, KC, 2 * FI])
        dn_raw = a3("dn_raw", [FH, 2, 2, E])
        gu_hi = a3("gu_hi", [P, 2, KC, 2 * FI], F32R)
        gu_lo = a3("gu_lo", [P, 2, KC, 2 * FI], F32R)
        dn_hi = a3("dn_hi", [FH, 2, 2, E], F32R)
        dn_lo = a3("dn_lo", [FH, 2, 2, E], F32R)
        xr = a3("xr", [P, 2, 2, E])
        x_hi = a3("x_hi", [P, 2, KC, P], F32R)
        x_lo = a3("x_lo", [P, 2, KC, P], F32R)
        sg = a3("sg", [P, 2, FI])
        hh = a3("hh", [P, 2, FI])
        h_hi = a3("h_hi", [FH, 2, 2, P], F32R)
        h_lo = a3("h_lo", [FH, 2, 2, P], F32R)
        yo = a3("yo", [P, 2, E])

        a4 = Arena(nc, keep.at)
        G = a4("G", [P, CPB, TOPK + 1, E])
        cr = a4("cr", [P, 2, CPB, E])
        k_hi = a4("k_hi", [P, CPB, E], F32R)
        k_lo = a4("k_lo", [P, CPB, E], F32R)
        v_hi = a4("v_hi", [P, KC, S], F32R)
        v_lo = a4("v_lo", [P, KC, S], F32R)
        qf = a4("qf", [P, CPB, E])
        q_hi = a4("q_hi", [P, CPB, E], F32R)
        q_lo = a4("q_lo", [P, CPB, E], F32R)
        sf = a4("sf", [P, KC, E])
        s_hi = a4("s_hi", [P, KC, E], F32R)
        s_lo = a4("s_lo", [P, KC, E], F32R)

        a5 = Arena(nc, keep.at)
        w_raw, w_hi, w_lo = [], [], []
        for p in range(2):
            w_raw.append(a5(f"w_raw{p}", [P, 3, KC * BLK]))
            w_hi.append(a5(f"w_hi{p}", [P, 3, KC * BLK], F32R))
            w_lo.append(a5(f"w_lo{p}", [P, 3, KC * BLK], F32R))
            assert p or a5.at <= keep.at + CPB * (TOPK + 1) * E * 4
        f_hi = a5("f_hi", [P, KC, NT * P], F32R)
        f_lo = a5("f_lo", [P, KC, NT * P], F32R)
        xn4 = a5("xn4", [P, CPB, E])
        fsg = a5("fsg", [P, 2, 512])
        fh = a5("fh", [P, 2, 512])
        fh_hi = a5("fh_hi", [P, 2, HCB, 512], F32R)
        fh_lo = a5("fh_lo", [P, 2, HCB, 512], F32R)

        sp_note, pool_note, act_note, dve_note = sem("sp_note"), sem("pool_note"), sem("act_note"), sem("dve_note")
        dve_step, act_step, pool_step = sem("dve_step"), sem("act_step"), sem("pool_step")
        stage_done = [sem(f"stage_done{k}") for k in range(6)]
        x_loaded = [sem(f"x_loaded{b}") for b in range(B)]
        ctxT_loaded = [sem(f"ctxT_loaded{b}") for b in range(2)]
        small_loaded, consts_ready = sem("small_loaded"), sem("consts_ready")
        wg_zeroed, wg_ready = sem("wg_zeroed"), sem("wg_ready")
        mv_ready, std_ready, qn_ready = sem("mv_ready"), sem("std_ready"), sem("qn_ready")
        xT_done, xT_kept = sem("xT_done"), sem("xT_kept")
        gates_done, gates_kept = sem("gates_done"), sem("gates_kept")
        lsig_ready, aM_ready, exps_ready, dg_ready = sem("lsig_ready"), sem("aM_ready"), sem("exps_ready"), sem("dg_ready")
        tok_done, M_stored, zero_filled = sem("tok_done"), sem("M_stored"), sem("zero_filled")
        tile_loaded = [sem(f"tile_loaded{p}") for p in range(2)]
        qk_done, inter_done, intra_done, st_done = sem("qk_done"), sem("inter_done"), sem("intra_done"), sem("st_done")
        arg_ready, C_ready, h1_read, stm_ready = sem("arg_ready"), sem("C_ready"), sem("h1_read"), sem("stm_ready")
        hc_ready, sq_used, var_ready = sem("hc_ready"), sem("sq_used"), sem("var_ready")
        qs_ready, v1_ready, D_ready, sq_ready, hl_ready, std_h_ready = [sem(n) for n in ("qs_ready", "v1_ready", "D_ready", "sq_ready", "hl_ready", "std_h_ready")]
        qe_ready, kw_ready, arg_masked, St_ready, St_decayed = [sem(n) for n in ("qe_ready", "kw_ready", "arg_masked", "St_ready", "St_decayed")]
        xn2_ready, rout_loaded = sem("xn2_ready"), sem("rout_loaded")
        sc_done, sc_ready, sel_ready, pos_done = sem("sc_done"), sem("sc_ready"), sem("sel_ready"), sem("pos_done")
        slots_ready, xs_written, etab_ready, shared_stored = [sem(n) for n in ("slots_ready", "xs_written", "etab_ready", "shared_stored")]
        ew_loaded = [sem(f"ew_loaded{p}") for p in range(2)]
        xr_loaded = [sem(f"xr_loaded{p}") for p in range(2)]
        gw_hi, gw_lo, dw_hi, dw_lo = sem("gw_hi"), sem("gw_lo"), sem("dw_hi"), sem("dw_lo")
        xT_e, x_hi_e, x_lo_e = sem("xT_e"), sem("x_hi_e"), sem("x_lo_e")
        gu_e, sg_e, hh_e = sem("gu_e"), sem("sg_e"), sem("hh_e")
        hT_e, h_hi_e, h_lo_e, dn_e, y_e = sem("hT_e"), sem("h_hi_e"), sem("h_lo_e"), sem("dn_e"), sem("y_e")
        ys_written = [sem(f"ys_written{q}") for q in range(2)]
        g_loaded = [sem(f"g_loaded{i}") for i in range(CPB)]
        gs_loaded = [sem(f"gs_loaded{i}") for i in range(CPB)]
        g_used, k_loaded, v_loaded = sem("g_used"), sem("k_loaded"), sem("v_loaded")
        k_hi_x, k_lo_x, v_hi_x, v_lo_x = [sem(n) for n in ("k_hi_x", "k_lo_x", "v_hi_x", "v_lo_x")]
        mvx_ready, stdx_ready, qf_ready, q_hi_x, q_lo_x = [sem(n) for n in ("mvx_ready", "stdx_ready", "qf_ready", "q_hi_x", "q_lo_x")]
        s_done, s_sig, s_hi_x, s_lo_x, o_done, o_added = [sem(n) for n in ("s_done", "s_sig", "s_hi_x", "s_lo_x", "o_done", "o_added")]
        xn4_ready, fT_done, f_hi_ready, f_lo_ready = [sem(n) for n in ("xn4_ready", "fT_done", "f_hi_ready", "f_lo_ready")]
        fw_loaded = [sem(f"fw_loaded{p}") for p in range(2)]
        fw_hi, fw_lo = sem("fw_hi"), sem("fw_lo")
        fgu, fsg_ready, fh_ready, fh_hi_ready, fh_lo_ready, fdn, fadd, next_stats = [
            sem(n) for n in ("fgu", "fsg_ready", "fh_ready", "fh_hi_ready", "fh_lo_ready", "fdn", "fadd", "next_stats")]
        out_written = sem("out_written")
        mixed = sem("mixed")

        ENGINES = 5

        def stage_end(eng, k):
            eng.drain().then_inc(stage_done[k], 1)
            eng.wait_ge(stage_done[k], ENGINES)

        def bc(ap, shape):
            while len(ap.shape) < len(shape):
                ap = ap.unsqueeze(len(ap.shape))
            return ap.to_broadcast(shape)

        def flat(ap):
            return ap.rearrange("p a b -> p (a b)")

        def heads(ap):
            return ap.rearrange("p (h d) -> p h d", h=NH)

        def heads_of(t):
            return qT[:, bass.ds(t, 1)].rearrange("p o k n -> p (o k n)").rearrange("p (h d) -> p h d", h=NH)

        def mlstm_tiles(loop):
            with loop(B - 1) as i:
                for k in range(1, CPB + 1):
                    yield i, k, True
            for k in range(1, CPB):
                yield B - 1, k, False

        def where(i, k):
            return CPB * i + k, i + k // CPB, k % CPB, k % 2, 48 * (2 * i + k // 2 + 1)

        E_LOOPS = (HALVES - 2) // 4 - 1

        S_LOOPS = 2 * SHARED_T // 4 - 1
        KEPT = 2 * S_LOOPS - 1

        def shared_steps(eng):
            with eng.Fori(0, S_LOOPS) as i:
                for k in range(1, 5):
                    yield i, k, True

        def routed_steps(eng):
            with eng.Fori(S_LOOPS, E_LOOPS) as i:
                for k in range(1, 5):
                    yield i, k, True
            for k in range(1, HALVES - 4 * E_LOOPS):
                yield E_LOOPS, k, False

        def both_steps(eng):
            yield from shared_steps(eng)
            yield from routed_steps(eng)

        def weights_loaded(i, m):
            skipped = 0 if isinstance(i, int) and 2 * i + m < 2 else S_LOOPS - m % 2
            return 32 * (i + m // 2 + 1 - skipped)

        def batch_steps(loop):
            with loop(B - 1) as b:
                yield b, True
            yield B - 1, False

        UNITS = NBLK * B
        F_LOOPS = (UNITS - B) // 8

        def ffn_first():
            for k in range(1, B):
                yield 0, k, True

        def ffn_steps(eng):
            with eng.Fori(0, F_LOOPS) as i:
                for k in range(B, B + 8):
                    yield i, k, True
            for k in range(B, UNITS - 8 * F_LOOPS):
                yield F_LOOPS, k, False

        def tbank(i):
            return (pC, pD)[i // 2][:, i % 2]

        block = stack.enter_context(nc.Block())

        @block.sync
        def _(sp):
            def store_X():
                for b in range(B):
                    sp.dma_start(out[b].rearrange("(i p) f -> p i f", p=P), X[:, CPB * b:CPB * (b + 1), :]).then_inc(out_written, 16)
                sp.wait_ge(out_written, 16 * B)

            for q in range(2):
                sp.sem_inc(ys_written[q], 16)
            for b in range(B):
                sp.dma_start(X[:, CPB * b:CPB * (b + 1), :],
                             x[b].rearrange("(i p) f -> p i f", p=P)).then_inc(x_loaded[b], 16)
                if b == 0:
                    sp.wait_ge(wg_zeroed, 1)
                    with nc.allow_non_contiguous_dma(reason="one value per partition"):
                        sp.dma_start(wg[:, :, 0:NH], Wi.rearrange("(c p) h -> p c h", p=P)).then_inc(small_loaded, 16)
                        sp.dma_start(wg[:, :, 32:32 + NH], Wf.rearrange("(c p) h -> p c h", p=P)).then_inc(small_loaded, 16)
                        sp.dma_start(gb[0:NH, :], bi.rearrange("(h o) -> h o", o=1)).then_inc(small_loaded, 16)
                        sp.dma_start(gb[32:32 + NH, :], bf.rearrange("(h o) -> h o", o=1)).then_inc(small_loaded, 16)
                    sp.dma_start(lnb[:, :], ln_scale.rearrange("(o f) -> o f", o=1).to_broadcast([P, E])).then_inc(small_loaded, 16)
                if b >= 2:
                    sp.wait_ge(gates_done, b - 1)
                sp.dma_start(ctxTb[:, b % 2], ctxT[b].rearrange("(k p) s -> p k s", p=P)).then_inc(ctxT_loaded[b % 2], 16)
            sp.wait_ge(aM_ready, 1)
            sp.dma_start(M_dram, Mq[:, :]).then_inc(M_stored, 16)
            sp.wait_ge(M_stored, 16)
            stage_end(sp, 0)

            with sp.Fori(0, B) as b:
                for c in range(CPB):
                    p, t = c % 2, CPB * b + c
                    zrow = sp.snap(t * ZROWS + SHARED_ROWS)
                    sp.wait_ge(qk_done, done(NG * (t - 2) + 3, QK))
                    sp.dma_start(kT[:, p], ctxT[bass.ds(b, 1), :, c * P:(c + 1) * P].rearrange("o (k p) s -> p (o k) s", p=P)).then_inc(tile_loaded[p], 16)
                    sp.dma_start(cx[:, p], ctx[bass.ds(b, 1), c * P:(c + 1) * P, :].rearrange("o p f -> p (o f)")).then_inc(tile_loaded[p], 16)
                    sp.dma_start(Mb[:, p], M_dram[bass.ds(b * 32, NH), c * P:(c + 1) * P].unsqueeze(0).to_broadcast([P, NH, P])).then_inc(tile_loaded[p], 16)
                    sp.dma_start(Xs[bass.ds(zrow, ZROWS), :].rearrange("(r p) f -> p r f", p=ZP),
                                 zero[0:ZP, :].unsqueeze(1).to_broadcast([ZP, 8, E])).then_inc(zero_filled, 16)
            sp.wait_ge(zero_filled, 16 * NT)
            stage_end(sp, 1)
            if stop <= 1:
                store_X()
                return

            sp.dma_start(rw[:, :, :], router_wT.rearrange("(k p) e -> p k e", p=P)).then_inc(rout_loaded, 16)
            sp.dma_start(eb[:, :], e_bias.rearrange("(o f) -> o f", o=1).to_broadcast([P, NE])).then_inc(rout_loaded, 16)

            def load_rows(i, m):
                p, n = m % 2, 2 * i + m
                if not isinstance(i, int):
                    n = sp.snap(n)
                row, turned = n * MT, done(2 * n - 3, 3)
                sp.wait_ge(xT_e, turned)
                sp.sem_inc(sp_note, 1)
                sp.dma_start(xr[:, p], Xs[bass.ds(row, MT), :].rearrange("(q p) f -> p q f", p=P)).then_inc(xr_loaded[p], 16)

            def load_weights(i, m, e=None):
                p, n = m % 2, 2 * i + m
                if not isinstance(i, int):
                    n = sp.snap(n)
                for s in (gw_hi, gw_lo, dw_hi, dw_lo):
                    sp.wait_ge(s, done(n - 2))
                sp.sem_inc(sp_note, 1)
                if e is None:
                    e = sp.value_load(etab[0:1, bass.ds(n, 1)], min_val=0, max_val=NE)
                sp.dma_start(gu_raw[:, p], gate_upT[bass.ds(e, 1)].rearrange("o p k f -> p (o k) f")).then_inc(ew_loaded[p], 16)
                sp.dma_start(dn_raw[:, p], downT[bass.ds(e, 1)].rearrange("o p j f -> p (o j) f")).then_inc(ew_loaded[p], 16)

            def store_half(i, k):
                u, q = 4 * i + k, k % 2
                sp.wait_ge(y_e, done(u))
                sp.dma_start(Ys[bass.ds(u * P, P), :], yo[:, q]).then_inc(ys_written[q], 16)

            load_weights(0, 0, e=0)
            load_weights(0, 1, e=0)
            sp.wait_ge(xn2_ready, NT)
            sp.dma_start(Xs[0:SHARED_ROWS, :].rearrange("(t p) f -> p t f", p=P), xn2[:, :, :]).then_inc(shared_stored, 16)
            sp.wait_ge(shared_stored, 16)
            for m in range(3):
                load_rows(0, m)
            load_weights(S_LOOPS, 1, e=0)
            with sp.Fori(0, S_LOOPS - 1) as i:
                for k in range(1, 5):
                    if k % 2 == 0:
                        load_rows(i, k // 2 + 2)
                    store_half(i, k - 1)
            for k in range(1, 5):
                if k == 2:
                    load_rows(S_LOOPS - 1, 3)
                if k == 4:
                    sp.wait_ge(etab_ready, 1)
                    load_weights(S_LOOPS - 1, 4)
                    sp.wait_ge(xs_written, 16 * NT * TOPK)
                    load_rows(S_LOOPS - 1, 4)
                store_half(S_LOOPS - 1, k - 1)
            for i, k, looped in routed_steps(sp):
                if k % 2 == 0 and (looped or 2 * i + k // 2 + 2 < ETILES):
                    load_rows(i, k // 2 + 2)
                    load_weights(i, k // 2 + 2)
                store_half(i, k - 1)
            store_half(0, HALVES - 1)
            for q in range(2):
                sp.wait_ge(ys_written[q], 16 * (ETILES + 1))
            stage_end(sp, 3)

            def load_k(b):
                sp.dma_start(cr[:, 0], ctx[bass.ds(b, 1)].rearrange("o (i p) f -> p (o i) f", p=P)).then_inc(k_loaded, 16)

            def load_v(b):
                sp.dma_start(cr[:, 1], ctxT[bass.ds(b, 1)].rearrange("o (k p) s -> p (o k) s", p=P)).then_inc(v_loaded, 16)

            def load_shared(b, i):
                sp.dma_start(G[:, i, TOPK, :], Ys[bass.ds((CPB * b + i) * P, P), :]).then_inc(gs_loaded[i], 16)

            for i in range(CPB):
                load_shared(0, i)
            load_k(0)
            load_v(0)
            with sp.Fori(0, B - 1) as b:
                sp.wait_ge(k_lo_x, b + 1)
                load_k(b + 1)
                for i in range(CPB):
                    sp.wait_ge(g_used, CPB * b + i + 1)
                    load_shared(b + 1, i)
                sp.wait_ge(v_lo_x, b + 1)
                load_v(b + 1)

            def load_block(i, p):
                blk = 2 * i + p
                sp.wait_ge(fw_hi, done(blk - 2))
                sp.wait_ge(fw_lo, done(blk - 2))
                for m, w in enumerate((w_gateT, w_upT, w_downT)):
                    sp.dma_start(w_raw[p][:, m], w[bass.ds(blk, 1)].rearrange("o p f -> p (o f)")).then_inc(fw_loaded[p], 16)

            sp.wait_ge(g_used, NT)
            load_block(0, 0)
            stage_end(sp, 4)
            if stop <= 4:
                store_X()
                return

            load_block(0, 1)
            with sp.Fori(1, NBLK // 2) as i:
                for p in range(2):
                    load_block(i, p)
            for g in range(B):
                sp.wait_ge(fadd, done(4 * (UNITS - B + g) + 3, 4))
                sp.dma_start(out[g].rearrange("(i p) f -> p i f", p=P), X[:, CPB * g:CPB * (g + 1), :]).then_inc(out_written, 16)
            sp.wait_ge(out_written, 16 * B)

        @block.gpsimd
        def _(pool):
            for s in (hl_ready, kw_ready, arg_masked, St_ready, gw_lo, dw_lo, fw_lo, fh_lo_ready):
                pool.sem_inc(s, 2)
            steps = Steps(pool, pool_step)
            steps(pool.memset(wg[:, :, :], 0.0))
            pool.sem_inc(wg_zeroed, 1)
            pool.memset(eps[:, 0:1], EPS_LN)
            pool.memset(eps[:, 1:2], EPS_H)
            pool.memset(onesf[:, :], 1.0)
            pool.memset(zero[:, :], 0.0)
            pool.memset(IG[:, :], 0.0)
            pool.memset(FG[:, :], 0.0)
            pool.memset(bms[:, :], QSCALE)
            pool.memset(bmask[:, :], 1.0)
            steps(pool.memset(ident[:, :], 0.0))
            steps(pool.affine_select(out=ident[:, :], in_=ident[:, :], compare_op=ALU.not_equal, fill=1.0,
                                     base=0, pattern=[[-1, P]], channel_multiplier=1))
            for m in (bms, bmask):
                steps(pool.affine_select(out=m[:, :], in_=m[:, :], compare_op=ALU.is_ge, fill=0.0,
                                         base=0, pattern=[[-DH, HPG]], channel_multiplier=1))
                steps(pool.affine_select(out=m[:, :], in_=m[:, :], compare_op=ALU.is_ge, fill=0.0,
                                         base=DH - 1, pattern=[[DH, HPG]], channel_multiplier=-1))
            for j in range(2):
                steps(pool.tensor_copy(mask264[:, HPG * j:HPG * (j + 1), :], bc(bmask[:, :], [P, HPG, V1])))
            pool.sem_inc(consts_ready, 1)
            stage_end(pool, 0)

            steps(pool.memset(v1[:, :, :, :], 1.0))
            pool.sem_inc(consts_ready, 1)
            masked = pool.to_reg(NEG)

            def weighted_k(i, k):
                t, b, c, p, loads = where(i, k)
                if c < CPB - 1:
                    pool.wait_ge(tile_loaded[p], loads)
                    pool.wait_ge(qk_done, done(NG * (t - 2) + 3, QK))
                    pool.tensor_tensor(kw[:, p], heads(cx[:, p]), bc(tk[:, 1, c, bass.ds(b * 32, NH)], [P, NH, DH]),
                                       ALU.mult).then_inc(kw_ready, 1)

            def mask(i, k):
                t, b, c, p, loads = where(i, k)
                pool.wait_ge(arg_ready, done(t))
                pool.sem_inc(pool_note, 1)
                pool.affine_select(out=Dm[:, p], in_=Dm[:, p], compare_op=ALU.is_ge, fill=masked,
                                   base=0, pattern=[[0, NH], [1, P]], channel_multiplier=-1).then_inc(arg_masked, 1)

            def state(i, k):
                t, b, c, p, loads = where(i, k)
                if c < CPB - 1:
                    pool.wait_ge(inter_done, done(3 * b + c - 1))
                    if c > 0:
                        pool.tensor_tensor(St[:, :, :], St[:, :, :], bc(decB[:, c, bass.ds(b * 32, NH)], [P, NH, V1]),
                                           ALU.mult).then_inc(St_decayed, 1)
                        pool.wait_ge(St_decayed, 3 * b + c + 1)
                    pool.wait_ge(stm_ready, done(3 * b + c))
                    if c == 0:
                        pool.sem_inc(St_decayed, 1)
                        pool.tensor_copy(St[:, :, :], stm[:, :, :]).then_inc(St_ready, 1)
                    else:
                        pool.tensor_tensor(St[:, :, :], St[:, :, :], stm[:, :, :], ALU.add).then_inc(St_ready, 1)

            def scaled(i, k):
                t = CPB * i + k
                pool.wait_ge(sq_ready, done(t))
                pool.sem_inc(pool_note, 1)
                hc = heads_of(t)
                pool.tensor_tensor(hc, hc, heads(lnb[:, :]), ALU.mult).then_inc(hl_ready, 1)

            weighted_k(0, 0)
            mask(0, 0)
            weighted_k(0, 1)
            mask(0, 1)
            state(0, 0)
            for i, k, looped in mlstm_tiles(lambda n: pool.Fori(0, n)):
                more = looped or CPB * i + k + 1 < NT
                if more:
                    weighted_k(i, k + 1)
                    mask(i, k + 1)
                scaled(i, k - 1)
                state(i, k)
            scaled(0, NT - 1)
            stage_end(pool, 1)
            if stop <= 1:
                return

            pool.memset(onesb[:, :], 1.0)
            pool.memset(tri[:, :], 1.0)
            pool.memset(d0[:, :, :], 1.0)
            pool.memset(ton[:, :], 1.0)
            pool.iota(iota256[:, :], [[MT, 8]], base=0, channel_multiplier=0, allow_small_or_imprecise_dtypes=True)
            pool.iota(iotan[:, :], [[1, ETILES + 1]], base=0, channel_multiplier=0, allow_small_or_imprecise_dtypes=True)
            steps(pool.iota(iotam[:, :], [[1, NE]], base=-99, channel_multiplier=0, allow_small_or_imprecise_dtypes=True))
            pool.affine_select(out=tri[:, :], in_=tri[:, :], compare_op=ALU.is_gt, fill=0.0,
                               base=0, pattern=[[1, P]], channel_multiplier=-1)
            steps(pool.affine_select(out=d0[:, :, :], in_=d0[:, :, :], compare_op=ALU.is_gt, fill=0.0,
                                     base=0, pattern=[[0, NE], [1, NT]], channel_multiplier=0))
            pool.sem_inc(consts_ready, 1)
            def gu_split(i, m):
                p, n = m % 2, 2 * i + m
                pool.wait_ge(gw_hi, done(n))
                pool.tensor_tensor(gu_lo[:, p], gu_raw[:, p], gu_hi[:, p].bitcast(F32), ALU.subtract).then_inc(gw_lo, 1)

            def dn_split(i, m):
                p, n = m % 2, 2 * i + m
                pool.wait_ge(dw_hi, done(n))
                pool.tensor_tensor(dn_lo[:, p], dn_raw[:, p], dn_hi[:, p].bitcast(F32), ALU.subtract).then_inc(dw_lo, 1)

            for m in range(2):
                gu_split(0, m)
                dn_split(0, m)
            for s in (gw_lo, dw_lo):
                pool.wait_ge(s, done(1))
                pool.sem_inc(s, KEPT)
            pool.wait_ge(slots_ready, 1)
            for t in range(NT):
                for k in range(TOPK):
                    pool.indirect_dma_start(out=Xs, out_offset=bass.IndirectOffsetOnAxis(ap=slot[:, t, k:k + 1], axis=0),
                                            in_=xn2[:, t, :], in_offset=None).then_inc(xs_written, 16)
            gu_split(S_LOOPS, 1)
            for i, k, looped in routed_steps(pool):
                if k % 2 == 1 and (looped or 2 * i + (k + 1) // 2 < ETILES):
                    dn_split(i, (k + 1) // 2)
                if k % 2 == 0 and (looped or 2 * i + (k + 2) // 2 < ETILES):
                    gu_split(i, (k + 2) // 2)
            stage_end(pool, 3)

            def gather(b, tiles):
                for i in tiles:
                    t = CPB * b + i
                    if b >= 1:
                        pool.wait_ge(g_used, t - CPB + 1)
                    for k in range(TOPK):
                        pool.indirect_dma_start(out=G[:, i, k, :], out_offset=None, in_=Ys,
                                                in_offset=bass.IndirectOffsetOnAxis(ap=slot[:, t, k:k + 1], axis=0)).then_inc(g_loaded[i], 16)

            gather(0, range(CPB))
            for b in range(B):
                pool.wait_ge(k_hi_x, b + 1)
                pool.tensor_tensor(k_lo[:, :, :], cr[:, 0], k_hi[:, :, :].bitcast(F32), ALU.subtract).then_inc(k_lo_x, 1)
                if b + 1 < B:
                    gather(b + 1, range(0, 2))
                pool.wait_ge(v_hi_x, b + 1)
                pool.tensor_tensor(v_lo[:, :, :], cr[:, 1], v_hi[:, :, :].bitcast(F32), ALU.subtract).then_inc(v_lo_x, 1)
                if b + 1 < B:
                    gather(b + 1, range(2, CPB))
            def w_split(i, m):
                p, blk = m % 2, 2 * i + m
                pool.wait_ge(fw_hi, done(blk))
                pool.tensor_tensor(w_lo[p][:, :, :], w_raw[p][:, :, :], w_hi[p][:, :, :].bitcast(F32), ALU.subtract).then_inc(fw_lo, 1)

            w_split(0, 0)
            stage_end(pool, 4)
            if stop <= 4:
                return

            def h_split(i, k):
                for j in range(HCB):
                    pool.wait_ge(fh_hi_ready, done(HCB * (8 * i + k) + j))
                    pool.tensor_tensor(fh_lo[:, k % 2, j], fh[:, j], fh_hi[:, k % 2, j].bitcast(F32), ALU.subtract).then_inc(fh_lo_ready, 1)

            h_split(0, 0)
            for i, k, looped in chain(ffn_first(), ffn_steps(pool)):
                h_split(i, k)
                if k % 4 == 2 and (looped or 2 * i + (k + 2) // 4 < NBLK):
                    w_split(i, (k + 2) // 4)

        @block.scalar
        def _(act):
            for s in (qe_ready, qs_ready, v1_ready, D_ready, sq_ready, gw_hi, dw_hi, x_hi_e, sg_e, h_hi_e, y_e,
                      s_sig, fw_hi, fsg_ready, fh_hi_ready):
                act.sem_inc(s, 2)
            steps = Steps(act, act_step)

            def std_of(tiles):
                return act.activation(std[:, tiles], mv[:, tiles, 1], ACT.Sqrt, bias=eps[:, 0:1])

            act.wait_ge(consts_ready, 1)
            for b in range(B):
                act.wait_ge(mv_ready, b + 1)
                std_of(slice(CPB * b, CPB * (b + 1))).then_inc(std_ready, 1)
                for k in range(KC):
                    act.wait_ge(xT_done, KC * b + k + 1)
                    act.activation(qT[:, CPB * b:CPB * (b + 1), k], (pA, pB)[k // 2][:, k % 2].rearrange("p (i n) -> p i n", n=P), ACT.Copy).then_inc(xT_kept, 1)
            act.wait_ge(gates_kept, B)
            steps(act.activation(t1[:, :], FG[:, :], ACT.Abs))
            steps(act.activation(t2[:, :], t1[:, :], ACT.Exp, scale=-1.0))
            act.activation(t1[:, :], t2[:, :], ACT.Ln, bias=1.0).then_inc(lsig_ready, 1)
            act.wait_ge(aM_ready, 2)
            for c in range(CPB):
                cs = slice(c * P, (c + 1) * P)
                act.activation(WQ[:, cs], Mq[:, cs], ACT.Exp, bias=mprev[:, c:c + 1], scale=-1.0)
                act.activation(WK[:, cs], Aq[:, cs], ACT.Exp, bias=mneg[:, c:c + 1])
                act.activation(dec[:, c:c + 1], mprev[:, c:c + 1], ACT.Exp, bias=mneg[:, c:c + 1])
            act.activation(NR[:, :], t2[:, :], ACT.Exp, scale=-1.0).then_inc(exps_ready, 1)
            for q in range(4):
                act.wait_ge(tok_done, q + 1)
                act.activation(flat(tk[:, q]), (pA, pB)[q // 2][:, q % 2], ACT.Copy)
            act.wait_ge(tok_done, 5)
            act.activation(flat(decB[:, :, :]), pC[:, 0], ACT.Copy)
            stage_end(act, 0)

            act.wait_ge(consts_ready, 2)

            def prepare(i, k):
                t, b, c, p, loads = where(i, k)
                act.wait_ge(qk_done, done(NG * (t - 2) + 3, QK))
                qt = qT[:, bass.ds(t, 1)].rearrange("p o k n -> p (o k) n")
                for h in range(HPG):
                    ins = act.activation(qe[:, p, :, h, :], qt, ACT.Copy, scale=bms[:, h:h + 1])
                ins.then_inc(qe_ready, 1)
                if c > 0:
                    act.activation(qs[:, p], qt, ACT.Copy, scale=QSCALE).then_inc(qs_ready, 1)
                act.wait_ge(tile_loaded[p], loads)
                act.wait_ge(intra_done, done(t - 2))
                act.activation(v1[:, p, :, 0:DH], heads(cx[:, p]), ACT.Copy).then_inc(v1_ready, 1)
                act.wait_ge(arg_masked, done(t))
                act.activation(Dm[:, p], Dm[:, p], ACT.Exp).then_inc(D_ready, 1)

            def squares(i, k):
                t = CPB * i + k
                act.wait_ge(hc_ready, done(t))
                act.wait_ge(sq_used, done(t - 1))
                act.sem_inc(act_note, 1)
                act.activation(sq[:, :, :], heads_of(t), ACT.Square).then_inc(sq_ready, 1)

            prepare(0, 0)
            prepare(0, 1)
            for i, k, looped in mlstm_tiles(lambda n: act.Fori(0, n)):
                if looped or CPB * i + k + 1 < NT:
                    prepare(i, k + 1)
                squares(i, k - 1)
            squares(0, NT - 1)
            act.wait_ge(var_ready, 1)
            act.activation(flat(gain[:, :, :]), flat(vsum[:, :, :]), ACT.Sqrt).then_inc(std_h_ready, 1)
            stage_end(act, 1)
            if stop <= 1:
                return

            act.wait_ge(mv_ready, B + 1)
            std_of(slice(0, NT)).then_inc(std_ready, 1)
            for t in range(NT):
                act.wait_ge(xT_done, KC * B + t + 1)
                if t >= 2:
                    act.wait_ge(sc_done, t - 1)
                act.activation(flat(xT2[:, t % 2]), pA[:, t % 2], ACT.Copy).then_inc(xT_kept, 1)

            def gu_split(i, m):
                p, n = m % 2, 2 * i + m
                act.wait_ge(ew_loaded[p], weights_loaded(i, m))
                act.wait_ge(gu_e, done(2 * n - 3, 3))
                act.activation(gu_hi[:, p], gu_raw[:, p], ACT.Copy).then_inc(gw_hi, 1)

            def dn_split(i, m):
                p, n = m % 2, 2 * i + m
                act.wait_ge(ew_loaded[p], weights_loaded(i, m))
                act.wait_ge(dn_e, done(2 * n - 3, 3))
                act.activation(dn_hi[:, p], dn_raw[:, p], ACT.Copy).then_inc(dw_hi, 1)

            def x_split(i, k):
                u, q = 4 * i + k, k % 2
                act.wait_ge(xT_e, done(u, 3))
                act.wait_ge(gu_e, done(u - 2, 3))
                act.activation(flat(x_hi[:, q]), pA[:, q], ACT.Copy).then_inc(x_hi_e, 1)

            def silu(i, k):
                u, q = 4 * i + k, k % 2
                act.wait_ge(gu_e, done(u, 3))
                act.wait_ge(hh_e, done(u - 2))
                act.activation(sg[:, q], pB[:, q, 0:FI], ACT.Silu).then_inc(sg_e, 1)

            def h_split(i, k):
                u, q = 4 * i + k, k % 2
                act.wait_ge(hT_e, done(u))
                act.wait_ge(dn_e, done(u - 2, 3))
                act.activation(flat(h_hi[:, q]), pC[0:FH, q, 0:2 * P], ACT.Copy).then_inc(h_hi_e, 1)

            def y_keep(i, k):
                u, q = 4 * i + k, k % 2
                act.wait_ge(dn_e, done(u, 3))
                act.wait_ge(ys_written[q], 16 * (2 * i + k // 2 + 1))
                act.activation(yo[:, q], pD[:, q], ACT.Copy).then_inc(y_e, 1)

            def step(i, k, looped):
                h_split(i, k - 1)
                if looped or 4 * i + k + 1 < HALVES:
                    x_split(i, k + 1)

            def step_end(i, k):
                silu(i, k)
                y_keep(i, k - 1)

            for m in range(2):
                gu_split(0, m)
                dn_split(0, m)
            for s in (gw_hi, dw_hi):
                act.wait_ge(s, done(1))
                act.sem_inc(s, KEPT)
            act.wait_ge(sc_done, NT)
            act.activation(flat(sc[:, :, :]), pC[:, 0, 0:NT * NE], ACT.Sigmoid).then_inc(sc_ready, 1)
            x_split(0, 0)
            x_split(0, 1)
            silu(0, 0)
            for i, k, looped in shared_steps(act):
                step(i, k, looped)
                step_end(i, k)
            gu_split(S_LOOPS, 1)
            for i, k, looped in routed_steps(act):
                step(i, k, looped)
                if k % 2 == 1 and (looped or 2 * i + (k + 1) // 2 < ETILES):
                    dn_split(i, (k + 1) // 2)
                if k % 2 == 0 and (looped or 2 * i + (k + 2) // 2 < ETILES):
                    gu_split(i, (k + 2) // 2)
                step_end(i, k)
            h_split(0, HALVES - 1)
            y_keep(0, HALVES - 1)
            stage_end(act, 3)

            def k_split(b):
                act.wait_ge(k_loaded, 16 * (b + 1))
                act.activation(k_hi[:, :, :], cr[:, 0], ACT.Copy).then_inc(k_hi_x, 1)

            def v_split(b):
                act.wait_ge(v_loaded, 16 * (b + 1))
                act.activation(v_hi[:, :, :], cr[:, 1], ACT.Copy).then_inc(v_hi_x, 1)

            def q_split(b):
                act.wait_ge(mvx_ready, b + 1)
                act.activation(stdx[:, :], mvx[:, :, 1], ACT.Sqrt, bias=eps[:, 0:1]).then_inc(stdx_ready, 1)
                act.wait_ge(qf_ready, b + 1)
                act.activation(q_hi[:, :, :], qf[:, :, :], ACT.Copy).then_inc(q_hi_x, 1)

            k_split(0)
            v_split(0)
            q_split(0)
            for b, more in batch_steps(lambda n: act.Fori(0, n)):
                for n in range(KC):
                    act.wait_ge(s_done, KC * b + n + 1)
                    act.activation(sf[:, n], pA[:, n % 2], ACT.Sigmoid, scale=XSCALE).then_inc(s_sig, 1)
                    act.wait_ge(s_sig, done(KC * b + n))
                    act.activation(s_hi[:, n], sf[:, n], ACT.Copy).then_inc(s_hi_x, 1)
                if more:
                    k_split(b + 1)
                    q_split(b + 1)
                    act.wait_ge(o_done, done(KC * b + KC - 1))
                    v_split(b + 1)
            def w_split(i, m):
                p, blk = m % 2, 2 * i + m
                act.wait_ge(fw_loaded[p], 48 * (i + m // 2 + 1))
                act.wait_ge(fdn, done(4 * (4 * blk - 5) + 3, 20))
                act.activation(w_hi[p][:, :, :], w_raw[p][:, :, :], ACT.Copy).then_inc(fw_hi, 1)

            w_split(0, 0)
            stage_end(act, 4)
            if stop <= 4:
                return

            act.wait_ge(mv_ready, B + 2)
            std_of(slice(0, NT)).then_inc(std_ready, 1)
            def f_split(g):
                for i in range(CPB):
                    t = CPB * g + i
                    act.wait_ge(fT_done, t + 1)
                    act.activation(f_hi[:, :, t * P:(t + 1) * P], tbank(i).rearrange("p (k n) -> p k n", k=KC), ACT.Copy).then_inc(f_hi_ready, 1)

            def gated(i, k):
                v = 8 * i + k
                for j in range(HCB):
                    act.wait_ge(fgu, done(HCB * v + j))
                    act.wait_ge(fh_ready, done(HCB * v + j - 2))
                    act.activation(fsg[:, j], pA[:, j], ACT.Silu).then_inc(fsg_ready, 1)
                for j in range(HCB):
                    act.wait_ge(fh_ready, done(HCB * v + j))
                    act.wait_ge(fdn, done(4 * (v - 2) + 3, 20))
                    act.activation(fh_hi[:, k % 2, j], fh[:, j], ACT.Copy).then_inc(fh_hi_ready, 1)

            f_split(0)
            f_split(1)
            gated(0, 0)
            for i, k, looped in ffn_first():
                if k + 1 < B:
                    f_split(k + 1)
                gated(i, k)
                if k == 2:
                    w_split(0, 1)
            for i, k, looped in ffn_steps(act):
                gated(i, k)
                if k % 4 == 2 and (looped or 2 * i + (k + 2) // 4 < NBLK):
                    w_split(i, (k + 2) // 4)

        @block.vector
        def _(dve):
            for s in (arg_ready, C_ready, h1_read, stm_ready, hc_ready, sq_used, x_lo_e, hh_e, h_lo_e, o_added, fh_ready):
                dve.sem_inc(s, 2)
            dve.sem_inc(fadd, 4)
            steps = Steps(dve, dve_step)

            def gates_keep(b):
                dve.wait_ge(gates_done, b + 1)
                dve.tensor_scalar(IG[32 * b:32 * b + NH, :], pC[0:NH, b % 2], gb[0:NH, 0:1], None, ALU.add)
                dve.tensor_scalar(FG[32 * b:32 * b + NH, :], pC[32:32 + NH, b % 2], gb[32:32 + NH, 0:1], None, ALU.add).then_inc(gates_kept, 1)

            def f_split(g):
                for i in range(CPB):
                    t = CPB * g + i
                    dve.wait_ge(f_hi_ready, t + 1)
                    ts = slice(t * P, (t + 1) * P)
                    dve.tensor_tensor(f_lo[:, :, ts], tbank(i).rearrange("p (k n) -> p k n", k=KC), f_hi[:, :, ts].bitcast(F32),
                                      ALU.subtract).then_inc(f_lo_ready, 1)

            def stats_of(t):
                steps(dve.bn_stats(stats[:, t, :], X[:, t, :]))
                return dve.bn_aggr(mv[:, t, :], stats[:, t, :])

            def normed(dst, t):
                return dve.tensor_scalar(dst, X[:, t, :], mv[:, t, 0:1], rstd[:, t:t + 1], ALU.subtract, ALU.mult)

            dve.wait_ge(small_loaded, 80)
            dve.tensor_tensor(wg[:, KC:2 * KC, :], wg[:, KC:2 * KC, :], wg[:, 2 * KC:, :], ALU.add).then_inc(wg_ready, 1)
            for b in range(B):
                dve.wait_ge(x_loaded[b], 16)
                for i in range(CPB):
                    ins = stats_of(CPB * b + i)
                ins.then_inc(mv_ready, 1)
                dve.wait_ge(mv_ready, b + 1)
                dve.wait_ge(std_ready, b + 1)
                steps(dve.reciprocal(rstd[:, CPB * b:CPB * (b + 1)], std[:, CPB * b:CPB * (b + 1)]))
                if b >= 2:
                    dve.wait_ge(xT_done, KC * (b - 1))
                for i in range(CPB):
                    ins = normed(qn[:, b % 2, i, :], CPB * b + i)
                ins.then_inc(qn_ready, 1)
                if b >= 1:
                    gates_keep(b - 1)
            gates_keep(B - 1)
            dve.wait_ge(gates_kept, B)
            dve.wait_ge(lsig_ready, 1)
            steps(dve.scalar_tensor_tensor(out=t2[:, :], in0=FG[:, :], scalar=0.0, in1=t1[:, :], op0=ALU.min, op1=ALU.subtract))
            steps(dve.tensor_tensor_scan(Fc[:, :], onesf[:, :], t2[:, :], 0.0, ALU.mult, ALU.add))
            steps(dve.tensor_tensor(Aq[:, :], IG[:, :], Fc[:, :], ALU.subtract))
            dve.tensor_tensor_scan(Mq[:, :], onesf[:, :], Aq[:, :], -3e38, ALU.mult, ALU.max).then_inc(aM_ready, 1)
            dve.wait_ge(aM_ready, 1)
            dve.tensor_tensor(t2[:, :], Fc[:, :], Mq[:, :], ALU.add)
            dve.tensor_copy(mprev[:, 0:1], Mq[:, 0:1])
            dve.tensor_copy(mprev[:, 1:CPB], Mq[:, P - 1:S - P:P])
            dve.tensor_scalar(mneg[:, :], Mq[:, P - 1:S:P], -1.0, None, ALU.mult).then_inc(aM_ready, 1)
            dve.wait_ge(exps_ready, 1)
            for c in range(CPB):
                ins = dve.tensor_scalar(DG[:, c, :], ident[:, :], dec[:, c:c + 1], None, ALU.mult)
            ins.then_inc(dg_ready, 1)
            stage_end(dve, 0)

            dve.wait_ge(small_loaded, 80)

            def exponents(i, k):
                t, b, c, p, loads = where(i, k)
                dve.wait_ge(tile_loaded[p], loads)
                dve.tensor_tensor(Dm[:, p], bc(tk[:, 3, c, bass.ds(b * 32, NH)], [P, NH, P]), Mb[:, p], ALU.subtract).then_inc(arg_ready, 1)

            def weights(i, k, groups):
                t, b, c, p, loads = where(i, k)
                dve.wait_ge(D_ready, done(t))
                dve.wait_ge(intra_done, done(t - 2))
                for j in groups:
                    dve.wait_ge(qk_done, done(NG * t + j, QK))
                    dve.tensor_tensor(Cm[:, p, HPG * j:HPG * (j + 1), :], Dm[:, p, HPG * j:HPG * (j + 1), :],
                                      pA[:, j % 2].rearrange("p (i s) -> p i s", i=HPG), ALU.mult).then_inc(C_ready, 1)

            def state_part(i, k):
                t, b, c, p, loads = where(i, k)
                if c < CPB - 1:
                    dve.wait_ge(st_done, done(3 * b + c))
                    dve.wait_ge(St_ready, done(3 * b + c - 1))
                    dve.tensor_tensor(stm[:, :, :].rearrange("p (j h) e -> p j (h e)", j=2), pD[:, :, 0:8 * V1],
                                      mask264[:, :, :].rearrange("p h e -> p (h e)").unsqueeze(1).to_broadcast([P, 2, 8 * V1]),
                                      ALU.mult).then_inc(stm_ready, 1)

            OUT = pB[:, :, 0:8 * V1].rearrange("p j (h e) -> p j h e", e=V1)
            INT = pC[:, :, 0:8 * V1].rearrange("p j (h e) -> p j h e", e=V1)
            H1 = h1[:, :, :].rearrange("p (j h) e -> p j h e", j=2)

            def gather_heads(i, k):
                t, b, c, p, loads = where(i, k)
                cols = bass.ds(b * 32, NH)
                dve.wait_ge(intra_done, done(t))
                if c == 0:
                    dve.tensor_copy(H1, OUT).then_inc(h1_read, 1)
                else:
                    dve.wait_ge(inter_done, done(3 * b + c - 1))
                    wq = tk[:, 0, c, cols].rearrange("p (j h) -> p j h", j=2).unsqueeze(3).to_broadcast([P, 2, 8, V1])
                    steps(dve.tensor_tensor(H1, INT, wq, ALU.mult))
                    dve.tensor_tensor(H1, H1, OUT, ALU.add).then_inc(h1_read, 1)

            def center(i, k):
                t, b, c, p, loads = where(i, k)
                dve.wait_ge(h1_read, done(t))
                steps(dve.tensor_reduce(hsum[:, :], h1[:, :, 0:DH], AX.X, ALU.add))
                dve.scalar_tensor_tensor(out=heads_of(t), in0=bc(hsum[:, :], [P, NH, DH]), scalar=-1.0 / DH, in1=h1[:, :, 0:DH],
                                         op0=ALU.mult, op1=ALU.add).then_inc(hc_ready, 1)
                steps(dve.tensor_copy(den[:, bass.ds(t, 1), :].rearrange("p o h -> p (o h)"), h1[:, :, DH]))

            def variance(i, k):
                t = CPB * i + k
                dve.wait_ge(sq_ready, done(t))
                dve.tensor_reduce(vsum[:, bass.ds(t, 1), :].rearrange("p o h -> p (o h)"), sq[:, :, :], AX.X, ALU.add).then_inc(sq_used, 1)

            exponents(0, 0)
            exponents(0, 1)
            weights(0, 0, range(NG))
            state_part(0, 0)
            for i, k, looped in mlstm_tiles(lambda n: steps.loop(n, MLSTM_STEPS)):
                gather_heads(i, k - 1)
                weights(i, k, range(0, 2))
                if looped or CPB * i + k + 1 < NT:
                    exponents(i, k + 1)
                weights(i, k, range(2, NG))
                center(i, k - 1)
                state_part(i, k)
                variance(i, k - 1)
            gather_heads(0, NT - 1)
            center(0, NT - 1)
            variance(0, NT - 1)
            dve.wait_ge(sq_used, done(NT - 1))
            dn, rc, vs, gn = flat(den[:, :, :]), flat(rec[:, :, :]), flat(vsum[:, :, :]), flat(gain[:, :, :])
            steps(dve.scalar_tensor_tensor(out=dn, in0=dn, scalar=-1.0, in1=dn, op0=ALU.mult, op1=ALU.max))
            nrm = tk[:, 2].rearrange("p c (b h) -> p b c h", b=B)[:, :, :, 0:NH]
            den4 = den[:, :, :].rearrange("p (b c) h -> p b c h", b=B)
            steps(dve.tensor_tensor(den4, den4, nrm, ALU.max))
            steps(dve.tensor_scalar(dn, dn, EPS_H, None, ALU.add))
            steps(dve.reciprocal(rc, dn))
            steps(dve.tensor_tensor(dn, rc, rc, ALU.mult))
            steps(dve.scalar_tensor_tensor(out=vs, in0=vs, scalar=1.0 / DH, in1=dn, op0=ALU.mult, op1=ALU.mult))
            dve.tensor_scalar(vs, vs, EPS_H, None, ALU.add).then_inc(var_ready, 1)
            dve.wait_ge(std_h_ready, 1)
            steps(dve.reciprocal(vs, gn))
            steps(dve.tensor_tensor(gn, rc, vs, ALU.mult))
            dve.wait_ge(hl_ready, done(NT - 1))
            for t in range(NT):
                hy = flat(qT[:, t]).rearrange("p (h d) -> p h d", h=NH)
                steps(dve.tensor_tensor(hy, hy, bc(gain[:, t, :], [P, NH, DH]), ALU.mult))
                dve.tensor_tensor(X[:, t, :], X[:, t, :], flat(qT[:, t]), ALU.add).then_inc(mixed, 1)
            dve.wait_ge(mixed, NT)
            stage_end(dve, 1)
            if stop <= 1:
                return

            for t in range(NT):
                ins = stats_of(t)
            ins.then_inc(mv_ready, 1)
            dve.wait_ge(mv_ready, B + 1)
            dve.wait_ge(std_ready, B + 1)
            steps(dve.reciprocal(rstd[:, :], std[:, :]))
            for t in range(NT):
                normed(xn2[:, t, :], t).then_inc(xn2_ready, 1)
            dve.wait_ge(rout_loaded, 32)
            dve.wait_ge(consts_ready, 3)
            dve.wait_ge(sc_ready, 1)
            steps(dve.tensor_tensor(sw[:, :, :], sc[:, :, :], eb[:, :].unsqueeze(1).to_broadcast([P, NT, NE]), ALU.add))
            iot = iotam[:, :].unsqueeze(1).to_broadcast([P, NT, NE])
            for k in range(TOPK):
                steps(dve.tensor_reduce(mx[:, :], sw[:, :, :], AX.X, ALU.max))
                steps(dve.tensor_tensor(eq[:, :, :], sw[:, :, :], bc(mx[:, :], [P, NT, NE]), ALU.is_equal))
                steps(dve.tensor_tensor(eq[:, :, :], eq[:, :, :], iot, ALU.mult))
                steps(dve.tensor_reduce(ix[:, :], eq[:, :, :], AX.X, ALU.min))
                steps(dve.tensor_tensor(oh[:, k], iot, bc(ix[:, :], [P, NT, NE]), ALU.is_equal))
                steps(dve.scalar_tensor_tensor(out=flat(sw[:, :, :]), in0=flat(oh[:, k]), scalar=NEG, in1=flat(sw[:, :, :]),
                                               op0=ALU.mult, op1=ALU.add))
                steps(dve.tensor_tensor(pr[:, :, :], oh[:, k], sc[:, :, :], ALU.mult))
                steps(dve.tensor_reduce(ckr[:, k], pr[:, :, :], AX.X, ALU.add))
            steps(dve.tensor_tensor(pr[:, :, :], oh[:, 0], oh[:, 1], ALU.add))
            steps(dve.tensor_tensor(eq[:, :, :], oh[:, 2], oh[:, 3], ALU.add))
            dve.tensor_tensor(selb[:, :, :], pr[:, :, :], eq[:, :, :], ALU.add).then_inc(sel_ready, 1)
            steps(dve.tensor_reduce(csum[:, :], ckr[:, :, :].rearrange("p k t -> p t k"), AX.X, ALU.add))
            steps(dve.tensor_scalar(csum[:, :], csum[:, :], 1e-20, None, ALU.add))
            steps(dve.reciprocal(crec[:, :], csum[:, :]))
            dve.tensor_tensor(ck[:, :, :], ckr[:, :, :].rearrange("p k t -> p t k"), bc(crec[:, :], [P, NT, TOPK]), ALU.mult)
            dve.wait_ge(pos_done, 1)
            steps(dve.tensor_copy(cnt[:, :, :], pC[:, 1, 256:512].rearrange("p (t e) -> p e t", e=NE)))
            steps(dve.tensor_tensor_scan(flat(incl[:, :, :]), flat(d0[:, :, :]), flat(cnt[:, :, :]), 0.0, ALU.mult, ALU.add))
            steps(dve.tensor_tensor(excl[:, :, :], incl[:, :, :], cnt[:, :, :], ALU.subtract))
            steps(dve.tensor_tensor(nt8[:, :, :], bc(incl[:, :, NT - 1], [P, NE, 8]), iota256[:, :].unsqueeze(1).to_broadcast([P, NE, 8]), ALU.is_gt))
            steps(dve.tensor_reduce(nte[:, :], nt8[:, :, :], AX.X, ALU.add))
            steps(dve.tensor_tensor_scan(tinc[:, :], ton[:, :], nte[:, :], 0.0, ALU.mult, ALU.add))
            steps(dve.tensor_tensor(texc[:, :], tinc[:, :], nte[:, :], ALU.subtract))
            steps(dve.tensor_scalar(rowb[:, :], texc[:, :], float(MT), float(SHARED_ROWS), ALU.mult, ALU.add))
            steps(dve.tensor_tensor(excl[:, :, :], excl[:, :, :], bc(rowb[:, :], [P, NE, NT]), ALU.add))
            steps(dve.tensor_tensor(full[:, :, :], pC[:, 1, 0:256].rearrange("p (t e) -> p t e", e=NE), excl[:, :, :].rearrange("p e t -> p t e"), ALU.add))
            for k in range(TOPK):
                steps(dve.tensor_tensor(pr[:, :, :], oh[:, k], full[:, :, :], ALU.mult))
                steps(dve.tensor_reduce(slf[:, k], pr[:, :, :], AX.X, ALU.add))
            dve.tensor_copy(slot[:, :, :], slf[:, :, :].rearrange("p k t -> p t k")).then_inc(slots_ready, 1)
            steps(dve.tensor_scalar(texc[:, :], texc[:, :], float(SHARED_T), None, ALU.add))
            steps(dve.tensor_tensor(ecmp[:, :, :], bc(iotan[:, :], [1, ETILES + 1, NE]),
                                    texc[0:1, :].unsqueeze(1).to_broadcast([1, ETILES + 1, NE]), ALU.is_ge))
            steps(dve.tensor_reduce(ecf[:, :], ecmp[:, :, :], AX.X, ALU.add))
            dve.tensor_copy(etab[:, :], ecf[:, :]).then_inc(etab_ready, 1)

            def x_split(i, k):
                u, q = 4 * i + k, k % 2
                dve.wait_ge(x_hi_e, done(u))
                dve.tensor_tensor(flat(x_lo[:, q]), pA[:, q], flat(x_hi[:, q]).bitcast(F32), ALU.subtract).then_inc(x_lo_e, 1)

            def gate(i, k):
                u, q = 4 * i + k, k % 2
                dve.wait_ge(sg_e, done(u))
                dve.wait_ge(hT_e, done(u - 2))
                dve.tensor_tensor(hh[:, q], sg[:, q], pB[:, q, FI:2 * FI], ALU.mult).then_inc(hh_e, 1)

            def h_split(i, k):
                u, q = 4 * i + k, k % 2
                dve.wait_ge(h_hi_e, done(u))
                dve.tensor_tensor(flat(h_lo[:, q]), pC[0:FH, q, 0:2 * P], flat(h_hi[:, q]).bitcast(F32), ALU.subtract).then_inc(h_lo_e, 1)

            x_split(0, 0)
            x_split(0, 1)
            gate(0, 0)
            for i, k, looped in both_steps(dve):
                h_split(i, k - 1)
                if looped or 4 * i + k + 1 < HALVES:
                    x_split(i, k + 1)
                gate(i, k)
            h_split(0, HALVES - 1)
            stage_end(dve, 3)

            def token_rows(t):
                return X[:, bass.ds(t, 1), :].rearrange("p o f -> p (o f)")

            def combine(b, tiles):
                for i in tiles:
                    t = CPB * b + i
                    dve.wait_ge(gs_loaded[i], 16 * (b + 1))
                    dve.wait_ge(g_loaded[i], 16 * TOPK * (b + 1))
                    steps.tell(dve.tensor_tensor(token_rows(t), token_rows(t), G[:, i, TOPK, :], ALU.add))
                for k in range(TOPK):
                    for i in tiles:
                        t = CPB * b + i
                        steps.before(len(tiles) - 1 if k < TOPK - 1 else len(tiles) - 1 - tiles.index(i))
                        ins = dve.scalar_tensor_tensor(out=token_rows(t), in0=G[:, i, k, :], scalar=ck[:, bass.ds(t, 1), k],
                                                       in1=token_rows(t), op0=ALU.mult, op1=ALU.add)
                        if k < TOPK - 1:
                            steps.tell(ins)
                        else:
                            ins.then_inc(g_used, 1)
            def measure(b):
                dve.wait_ge(g_used, CPB * (b + 1))
                dve.sem_inc(dve_note, 1)
                for i in range(CPB):
                    ins = dve.bn_stats(statsx[:, i, :], token_rows(CPB * b + i))
                steps(ins)
                dve.sem_inc(dve_note, 1)
                for i in range(CPB):
                    ins = dve.bn_aggr(mvx[:, i, :], statsx[:, i, :])
                ins.then_inc(mvx_ready, 1)

            def norm(b):
                dve.wait_ge(mvx_ready, b + 1)
                dve.wait_ge(stdx_ready, b + 1)
                steps(dve.reciprocal(rstdx[:, :], stdx[:, :]))
                for i in range(CPB):
                    ins = dve.tensor_scalar(qf[:, i, :], token_rows(CPB * b + i), mvx[:, i, 0:1], rstdx[:, i:i + 1], ALU.subtract, ALU.mult)
                ins.then_inc(qf_ready, 1)

            def q_split(b):
                dve.wait_ge(q_hi_x, b + 1)
                dve.tensor_tensor(q_lo[:, :, :], qf[:, :, :], q_hi[:, :, :].bitcast(F32), ALU.subtract).then_inc(q_lo_x, 1)

            def add_x(b, tiles):
                for i in tiles:
                    dve.wait_ge(o_done, done(CPB * b + i))
                    dve.tensor_tensor(token_rows(CPB * b + i), token_rows(CPB * b + i), pB[:, i % 2], ALU.add).then_inc(o_added, 1)

            def stats_next(b, tiles):
                dve.wait_ge(o_added, done(CPB * b + tiles[-1]))
                dve.sem_inc(dve_note, 1)
                for i in tiles:
                    dve.bn_stats(stats[:, bass.ds(CPB * b + i, 1), :].rearrange("p o f -> p (o f)"), token_rows(CPB * b + i)).then_inc(next_stats, 1)

            combine(0, range(0, 2))
            combine(0, range(2, CPB))
            measure(0)
            norm(0)
            q_split(0)
            for b, more in batch_steps(lambda n: steps.loop(n, X_STEPS)):
                for n in range(KC):
                    if more and n in (0, 2):
                        combine(b + 1, range(n, n + 2) if n == 0 else range(2, 3))
                    dve.wait_ge(s_hi_x, KC * b + n + 1)
                    dve.tensor_tensor(s_lo[:, n], sf[:, n], s_hi[:, n].bitcast(F32), ALU.subtract).then_inc(s_lo_x, 1)
                if more:
                    combine(b + 1, range(3, CPB))
                    measure(b + 1)
                add_x(b, range(0, 2))
                if more:
                    norm(b + 1)
                add_x(b, range(2, 3))
                stats_next(b, range(0, 3))
                add_x(b, range(3, CPB))
                if more:
                    q_split(b + 1)
                stats_next(b, range(3, CPB))
            dve.wait_ge(next_stats, NT)
            for t in range(NT):
                ins = dve.bn_aggr(mv[:, t, :], stats[:, t, :])
            ins.then_inc(mv_ready, 1)
            stage_end(dve, 4)
            if stop <= 4:
                return

            dve.wait_ge(mv_ready, B + 2)
            dve.wait_ge(std_ready, B + 2)
            steps(dve.reciprocal(rstd[:, :], std[:, :]))

            def prepare_f(g):
                if g >= 1:
                    dve.wait_ge(fT_done, CPB * g)
                for i in range(CPB):
                    normed(xn4[:, i], CPB * g + i).then_inc(xn4_ready, 1)
                f_split(g)

            def gate_f(i, k):
                for j in range(HCB):
                    w = HCB * (8 * i + k) + j
                    dve.wait_ge(fsg_ready, done(w))
                    dve.wait_ge(fh_lo_ready, done(w - 2))
                    dve.tensor_tensor(fh[:, j], fsg[:, j], pB[:, j], ALU.mult).then_inc(fh_ready, 1)

            def add_f(i, k):
                v = 8 * i + k
                for tt in range(CPB):
                    t = CPB * (k % 4) + tt
                    dve.wait_ge(fdn, done(4 * v + tt, 20))
                    dve.tensor_tensor(X[:, t, :], X[:, t, :], (pC, pD)[tt // 2][:, tt % 2], ALU.add).then_inc(fadd, 1)

            prepare_f(0)
            prepare_f(1)
            gate_f(0, 0)
            for i, k, looped in ffn_first():
                if k + 1 < B:
                    prepare_f(k + 1)
                gate_f(i, k)
                add_f(i, k - 1)
            for i, k, looped in ffn_steps(dve):
                gate_f(i, k)
                add_f(i, k - 1)
            add_f(0, UNITS - 1)

        @block.tensor
        def _(pe):
            pe.sem_inc(qk_done, QK)
            for s in (inter_done, intra_done, st_done, hT_e, o_done, fgu):
                pe.sem_inc(s, 2)
            for s in (xT_e, gu_e, dn_e):
                pe.sem_inc(s, 3)
            pe.sem_inc(fdn, 20)

            def product3(out_, pairs):
                n = len(pairs)
                for c, ((ah, al), (bh, bl)) in enumerate(pairs):
                    pe.matmul(out_, ah, bh, start=c == 0, stop=False)
                    pe.matmul(out_, ah, bl, start=False, stop=False)
                    ins = pe.matmul(out_, al, bh, start=False, stop=c == n - 1)
                return ins

            pe.wait_ge(consts_ready, 1)
            for b in range(B):
                pe.wait_ge(qn_ready, b + 1)
                for k in range(KC):
                    if b >= 1:
                        pe.wait_ge(xT_kept, KC * (b - 1) + k + 1)
                    for i in range(CPB):
                        ins = pe.transpose((pA, pB)[k // 2][:, k % 2, i * P:(i + 1) * P], qn[:, b % 2, i, k * P:(k + 1) * P], ident[:, :])
                    ins.then_inc(xT_done, 1)
                pe.wait_ge(wg_ready, 1)
                if b >= 2:
                    pe.wait_ge(gates_kept, b - 1)
                pe.wait_ge(ctxT_loaded[b % 2], 16 * (b // 2 + 1))
                for k in range(KC):
                    pe.matmul(pC[0:64, b % 2], wg[:, KC + k, :], ctxTb[:, b % 2, k], start=k == 0, stop=False)
                for k in range(KC):
                    pe.wait_ge(xT_kept, KC * b + k + 1)
                    ins = pe.matmul(pC[0:64, b % 2], wg[:, k, :], qT[:, CPB * b:CPB * (b + 1), k], start=False, stop=k == KC - 1)
                ins.then_inc(gates_done, 1)
            pe.wait_ge(exps_ready, 1)
            for q, src in enumerate((WQ, WK, NR, Aq)):
                for c in range(CPB):
                    ins = pe.transpose((pA, pB)[q // 2][:, q % 2, c * P:(c + 1) * P], src[:, c * P:(c + 1) * P], ident[:, :])
                ins.then_inc(tok_done, 1)
            pe.wait_ge(dg_ready, 1)
            pe.matmul(pC[:, 0], onesf[:, 0:P], flat(DG[:, :, :]), start=True, stop=True).then_inc(tok_done, 1)
            stage_end(pe, 0)

            def products(i, k):
                t, b, c, p, loads = where(i, k)
                pe.wait_ge(tile_loaded[p], loads)
                pe.wait_ge(qe_ready, done(t))
                for j in range(NG):
                    pe.wait_ge(C_ready, done(NG * t + j - 2))
                    pe.matmul(pA[:, j % 2], kT[:, p, j], flat(qe[:, p, j]), start=True, stop=True).then_inc(qk_done, 1)
                    if j == 1:
                        state_products(i, k)
                for h in range(NH):
                    if h % HPG == 0:
                        pe.wait_ge(C_ready, done(NG * t + h // HPG))
                    ins = pe.matmul(pB[:, h // 8, h % 8 * V1:(h % 8 + 1) * V1], Cm[:, p, h, :], v1[:, p, h, :], start=True, stop=True)
                ins.then_inc(intra_done, 1)

            def state_products(i, k):
                t, b, c, p, loads = where(i, k)
                pe.wait_ge(h1_read, done(t - 1))
                w = HPG * V1
                if c > 0:
                    pe.wait_ge(qs_ready, done(3 * b + c - 1))
                    pe.wait_ge(St_ready, done(3 * b + c - 1))
                    for j in range(NG):
                        ins = pe.matmul(pC[:, j // 2, j % 2 * w:(j % 2 + 1) * w], qs[:, p, j],
                                        flat(St[:, HPG * j:HPG * (j + 1), :]), start=True, stop=True)
                    ins.then_inc(inter_done, 1)
                pe.wait_ge(v1_ready, done(t))
                if c < CPB - 1:
                    pe.wait_ge(kw_ready, done(3 * b + c))
                    pe.wait_ge(stm_ready, done(3 * b + c - 1))
                    for j in range(NG):
                        ins = pe.matmul(pD[:, j // 2, j % 2 * w:(j % 2 + 1) * w], flat(kw[:, p, HPG * j:HPG * (j + 1), :]),
                                        flat(v1[:, p, HPG * j:HPG * (j + 1), :]), start=True, stop=True)
                    ins.then_inc(st_done, 1)

            products(0, 0)
            for i, k, looped in mlstm_tiles(lambda n: pe.Fori(0, n)):
                products(i, k)
            stage_end(pe, 1)
            if stop <= 1:
                return

            def scores(t):
                pe.wait_ge(xT_kept, KC * B + t + 1)
                for k in range(KC):
                    ins = pe.matmul(pC[:, 0, t * NE:(t + 1) * NE], xT2[:, t % 2, k], rw[:, k, :], start=k == 0, stop=k == KC - 1)
                ins.then_inc(sc_done, 1)

            pe.wait_ge(rout_loaded, 32)
            for t in range(NT):
                pe.wait_ge(xn2_ready, t + 1)
                if t >= 2:
                    pe.wait_ge(xT_kept, KC * B + t - 1)
                for k in range(KC):
                    ins = pe.transpose(pA[:, t % 2, k * P:(k + 1) * P], xn2[:, t, k * P:(k + 1) * P], ident[:, :])
                ins.then_inc(xT_done, 1)
                if t >= 1:
                    scores(t - 1)
            scores(NT - 1)
            pe.wait_ge(sel_ready, 1)
            pe.wait_ge(consts_ready, 3)
            for t in range(NT):
                pe.matmul(pC[:, 1, t * NE:(t + 1) * NE], tri[:, :], selb[:, t, :], start=True, stop=True)
            pe.matmul(pC[:, 1, 256:512], onesb[:, :], flat(selb[:, :, :]), start=True, stop=True).then_inc(pos_done, 1)

            def x_turn(i, k):
                u, q, wp = 4 * i + k, k % 2, k // 2 % 2
                pe.wait_ge(xr_loaded[wp], 16 * (i + k // 4 + 1))
                pe.wait_ge(x_lo_e, done(u - 2))
                for c in range(KC):
                    ins = pe.transpose(pA[:, q, c * P:(c + 1) * P], xr[:, wp, q, c * P:(c + 1) * P], ident[:, :])
                ins.then_inc(xT_e, 1)

            def gate_up(i, k):
                u, q, wp, n = 4 * i + k, k % 2, k // 2 % 2, 2 * i + k // 2
                pe.wait_ge(x_lo_e, done(u))
                pe.wait_ge(gw_lo, done(n))
                pe.wait_ge(hh_e, done(u - 2))
                product3(pB[:, q, 0:2 * FI], [((x_hi[:, q, c], x_lo[:, q, c]), (gu_hi[:, wp, c], gu_lo[:, wp, c])) for c in range(KC)]).then_inc(gu_e, 1)

            def h_turn(i, k):
                u, q = 4 * i + k, k % 2
                pe.wait_ge(hh_e, done(u))
                pe.wait_ge(h_lo_e, done(u - 2))
                for c in range(2):
                    ins = pe.transpose(pC[0:FH, q, c * P:(c + 1) * P], hh[:, q, c * FH:(c + 1) * FH], ident[:, :])
                ins.then_inc(hT_e, 1)

            def down(i, k):
                u, q, wp, n = 4 * i + k, k % 2, k // 2 % 2, 2 * i + k // 2
                pe.wait_ge(h_lo_e, done(u))
                pe.wait_ge(dw_lo, done(n))
                pe.wait_ge(y_e, done(u - 2))
                product3(pD[:, q], [((h_hi[:, q, c], h_lo[:, q, c]), (dn_hi[:, wp, c], dn_lo[:, wp, c])) for c in range(2)]).then_inc(dn_e, 1)

            x_turn(0, 0)
            x_turn(0, 1)
            gate_up(0, 0)
            for i, k, looped in both_steps(pe):
                h_turn(i, k - 1)
                if looped or 4 * i + k + 1 < HALVES:
                    x_turn(i, k + 1)
                gate_up(i, k)
                down(i, k - 1)
            h_turn(0, HALVES - 1)
            down(0, HALVES - 1)
            stage_end(pe, 3)

            with pe.Fori(0, B) as b:
                pe.wait_ge(k_lo_x, b + 1)
                pe.wait_ge(q_lo_x, b + 1)
                for n in range(KC):
                    pe.wait_ge(s_sig, done(KC * b + n - 2))
                    cols = slice(n * P, (n + 1) * P)
                    product3(pA[:, n % 2], [((q_hi[:, i, cols], q_lo[:, i, cols]), (k_hi[:, i], k_lo[:, i])) for i in range(CPB)]).then_inc(s_done, 1)
                pe.wait_ge(v_lo_x, b + 1)
                pe.wait_ge(s_lo_x, KC * (b + 1))
                for i in range(CPB):
                    pe.wait_ge(o_added, done(CPB * b + i - 2))
                    rows = slice(i * P, (i + 1) * P)
                    product3(pB[:, i % 2], [((v_hi[:, n, rows], v_lo[:, n, rows]), (s_hi[:, n], s_lo[:, n])) for n in range(KC)]).then_inc(o_done, 1)
            stage_end(pe, 4)
            if stop <= 4:
                return

            def f_turn(g):
                for i in range(CPB):
                    t = CPB * g + i
                    pe.wait_ge(xn4_ready, t + 1)
                    if g == 1:
                        pe.wait_ge(f_lo_ready, t - CPB + 1)
                    if g >= 3:
                        pe.wait_ge(fadd, done(4 * (g - 3) + i, 4))
                    for c in range(KC):
                        ins = pe.transpose(tbank(i)[:, c * P:(c + 1) * P], xn4[:, i, c * P:(c + 1) * P], ident[:, :])
                    ins.then_inc(fT_done, 1)

            def gate_up_f(i, k):
                v, wp, tok = 8 * i + k, k // 4 % 2, slice(k % 4 * 512, (k % 4 + 1) * 512)
                pe.wait_ge(fw_lo, done(2 * i + k // 4))
                for j in range(HCB):
                    pe.wait_ge(fh_ready, done(HCB * v + j - 2))
                    for m, bank in ((0, pA[:, j]), (1, pB[:, j])):
                        def w(t_, c):
                            return t_[wp][:, m, c * BLK + j * P:c * BLK + (j + 1) * P]
                        ins = product3(bank, [((w(w_hi, c), w(w_lo, c)), (f_hi[:, c, tok], f_lo[:, c, tok])) for c in range(KC)])
                    ins.then_inc(fgu, 1)

            def down_f(i, k):
                v, q, wp = 8 * i + k, k % 2, k // 4 % 2
                pe.wait_ge(fh_lo_ready, done(HCB * v + HCB - 1))
                for tt in range(CPB):
                    pe.wait_ge(fadd, done(4 * v + tt - 4, 4))
                    cols = slice(tt * P, (tt + 1) * P)
                    product3((pC, pD)[tt // 2][:, tt % 2],
                             [((fh_hi[:, q, j, cols], fh_lo[:, q, j, cols]),
                               (w_hi[wp][:, 2, j * 512:(j + 1) * 512], w_lo[wp][:, 2, j * 512:(j + 1) * 512])) for j in range(HCB)]).then_inc(fdn, 1)

            f_turn(0)
            f_turn(1)
            pe.wait_ge(f_lo_ready, CPB)
            gate_up_f(0, 0)
            for i, k, looped in ffn_first():
                if k + 1 < B:
                    if k == 1:
                        pe.wait_ge(f_lo_ready, 2 * CPB)
                    f_turn(k + 1)
                else:
                    pe.wait_ge(f_lo_ready, CPB * B)
                gate_up_f(i, k)
                if k + 1 < B:
                    pe.wait_ge(f_lo_ready, CPB * (k + 2))
                down_f(i, k - 1)
            for i, k, looped in ffn_steps(pe):
                gate_up_f(i, k)
                down_f(i, k - 1)
            down_f(0, UNITS - 1)


def kernel(**inputs):
    import numpy as np
    import concourse.bacc as bacc
    from concourse.bass_utils import run_bass_kernel_spmd

    arrays = layout(inputs)
    nc = bacc.Bacc("TRN2", target_bir_lowering=False, num_devices=1)
    args = [nc.dram_tensor(n, a.shape, mybir.dt.from_np(a.dtype), kind="ExternalInput").ap() for n, a in arrays.items()]
    out = nc.dram_tensor("out", (B, S, E), F32, kind="ExternalOutput").ap()
    build(nc, *args, out)
    return run_bass_kernel_spmd(nc, [arrays], core_ids=[0]).results[0]["out"]


def layout(inputs):
    import numpy as np

    g = {n: np.asarray(a) for n, a in inputs.items()}
    gate_up = np.concatenate([np.concatenate([g["L0_ffn_shared_gate_w"], g["L0_ffn_shared_up_w"]])[None], g["L0_ffn_gate_up_proj"]])
    down = np.concatenate([g["L0_ffn_shared_down_w"][None], g["L0_ffn_down_proj"]])
    a = {
        "x": g["x"], "ctx": g["ctx_2048"], "ctxT": g["ctx_2048"].transpose(0, 2, 1),
        "Wi": g["L0_xattn_Wi"], "bi": g["L0_xattn_bi"], "Wf": g["L0_xattn_Wf"], "bf": g["L0_xattn_bf"],
        "ln_scale": g["L0_xattn_ln_scale"],
        "router_wT": g["L0_ffn_router_w"].T, "e_bias": g["L0_ffn_e_bias"],
        "gate_upT": gate_up.transpose(0, 2, 1).reshape(NE + 1, KC, P, 2 * FI).transpose(0, 2, 1, 3),
        "downT": down.transpose(0, 2, 1).reshape(NE + 1, 2, FH, E).transpose(0, 2, 1, 3),
        "w_gateT": g["L1_ffn_w_gate"].reshape(NBLK, BLK, KC, P).transpose(0, 3, 2, 1).reshape(NBLK, P, KC * BLK),
        "w_upT": g["L1_ffn_w_up"].reshape(NBLK, BLK, KC, P).transpose(0, 3, 2, 1).reshape(NBLK, P, KC * BLK),
        "w_downT": g["L1_ffn_w_down"].T.reshape(NBLK, HCB, P, E).transpose(0, 2, 1, 3).reshape(NBLK, P, HCB * E),
    }
    return {n: np.ascontiguousarray(v) for n, v in a.items()}
```

```python
from contextlib import ExitStack, contextmanager
from itertools import chain

import concourse.bass as bass
from concourse import mybir

F32 = mybir.dt.float32
F32R = mybir.dt.float32r
BF16 = mybir.dt.bfloat16
I32 = mybir.dt.int32
U32 = mybir.dt.uint32
ALU = mybir.AluOpType
ACT = mybir.ActivationFunctionType
AX = mybir.AxisListType

P = 128
B, S, E = 4, 512, 512
NT = B * S // P
CPB = S // P
KC = E // P
NH, DH = 16, 32
HPG = P // DH
NG = NH // HPG
V1 = DH + 1
QSCALE = float(DH) ** -0.5
EPS_LN, EPS_H = 1e-5, 1e-6
NEG = -1e30
VH = 13

NE, TOPK, FI = 16, 4, 192
FH = FI // 2
MT = 256
SHARED_T = B * S // MT
ROUTED_T = (TOPK * B * S + NE * (MT - 1)) // MT
ETILES = SHARED_T + ROUTED_T
HALVES = 2 * ETILES
SHARED_ROWS = SHARED_T * MT
ROWS = ROUTED_T * MT
ZROWS = ROWS // NT
ZP = ZROWS // 8
assert ZP * 8 * NT == ROWS and ZP <= P

HID = 2048
BLK = 256
NBLK = HID // BLK
HCB = BLK // P
XSCALE = float(S) ** -0.5

QK = 6
X_STEPS = 13
MLSTM_STEPS = 11


class Steps:

    def __init__(self, eng, sem):
        self.eng, self.sem, self.base, self.n = eng, sem, 0, 0

    def __call__(self, ins):
        ins.then_inc(self.sem, 1)
        self.n += 1
        self.eng.wait_ge(self.sem, self.base + self.n)

    def tell(self, ins):
        ins.then_inc(self.sem, 1)
        self.n += 1

    def before(self, k):
        self.eng.wait_ge(self.sem, self.base + self.n - k)

    @contextmanager
    def loop(self, trips, per):
        start = self.base + self.n
        with self.eng.Fori(0, trips) as i:
            self.base, self.n = start + i * per, 0
            yield i
            assert self.n == per, (self.n, per)
        self.base, self.n = start + trips * per, 0


def done(n, credit=2):
    return n + 1 + credit


class Arena:

    def __init__(self, nc, at):
        self.nc, self.at = nc, at

    def __call__(self, name, shape, dt=F32):
        size = {BF16: 2}.get(dt, 4)
        for n in shape[1:]:
            size *= n
        t = self.nc.alloc_sbuf_tensor_at(name, shape, dt, offset=self.at)
        self.at += (size + 31) // 32 * 32
        assert self.at <= self.nc.sbuf_usable_end, (name, self.at)
        return t


def build(nc, x, ctx, ctxT, Wi, bi, Wf, bf, ln_scale, router_wT, e_bias, gate_upT, downT,
          w_gateT, w_upT, w_downT, out):
    with ExitStack() as stack:
        def sem(name):
            return stack.enter_context(nc.semaphore(name))

        base = (nc.sbuf_base + 63) // 64 * 64
        keep = Arena(nc, base)
        X = keep("X", [P, NT, E])
        ident = keep("ident", [P, P])
        stats = keep("stats", [P, NT, 6])
        mv = keep("mv", [P, NT, 2])
        std = keep("std", [P, NT])
        rstd = keep("rstd", [P, NT])
        gain = keep("gain", [P, NT, NH])
        zero = keep("zero", [P, E])
        statsx = keep("statsx", [P, CPB, 6])
        mvx = keep("mvx", [P, CPB, 2])
        stdx = keep("stdx", [P, CPB])
        rstdx = keep("rstdx", [P, CPB])
        eps = keep("eps", [P, 2])
        slot = keep("slot", [P, NT, TOPK], U32)
        ck = keep("ck", [P, NT, TOPK])
        etab = keep("etab", [1, ETILES + 1], I32)

        pA, pB, pC, pD = [stack.enter_context(nc.psum_tensor(f"p{n}", [P, 2, 512], F32)) for n in "ABCD"]

        M_dram = nc.dram_tensor("M_dram", (P, S), F32, kind="Internal").ap()
        Xt = nc.dram_tensor("Xt", (SHARED_ROWS, E), F32, kind="Internal").ap()
        Xs = nc.dram_tensor("Xs", (ROWS, E), F32, kind="Internal").ap()
        Ys = nc.dram_tensor("Ys", (ROWS, E), F32, kind="Internal").ap()

        a1 = Arena(nc, keep.at)
        qT = a1("qT", [P, NT, KC, P])
        tk = a1("tk", [P, 4, CPB, P])
        decB = a1("decB", [P, CPB, P])
        lnb = a1("lnb", [P, E])
        bms = a1("bms", [P, HPG])
        bmask = a1("bmask", [P, HPG])
        mask264 = a1("mask264", [P, 2 * HPG, V1])
        wg = a1("wg", [P, 3 * KC, 64])
        gb = a1("gb", [64, 1])
        a1a = Arena(nc, a1.at)
        ctxTb = a1a("ctxTb", [P, 2, KC, S])
        qn = a1a("qn", [P, 2, CPB, E])
        IG = a1a("IG", [P, S])
        FG = a1a("FG", [P, S])
        t1 = a1a("t1", [P, S])
        t2 = a1a("t2", [P, S])
        onesf = a1a("onesf", [P, S])
        Fc = a1a("Fc", [P, S])
        Aq = a1a("Aq", [P, S])
        Mq = a1a("Mq", [P, S])
        WQ = a1a("WQ", [P, S])
        WK = a1a("WK", [P, S])
        NR = a1a("NR", [P, S])
        mprev = a1a("mprev", [P, CPB])
        mneg = a1a("mneg", [P, CPB])
        dec = a1a("dec", [P, CPB])
        DG = a1a("DG", [P, CPB, P])
        a1b = Arena(nc, a1.at)
        kT = a1b("kT", [P, 2, KC, P])
        Mb = a1b("Mb", [P, 2, NH, P])
        cx = a1b("cx", [P, 2, E])
        v1 = a1b("v1", [P, 2, NH, V1])
        kw = a1b("kw", [P, 2, NH, DH])
        qs = a1b("qs", [P, 2, KC, P])
        qe = a1b("qe", [P, 2, NG, HPG, P])
        Dm = a1b("Dm", [P, 2, NH, P])
        Cm = a1b("Cm", [P, 2, NH, P])
        St = a1b("St", [P, NH, V1])
        stm = a1b("stm", [P, NH, V1])
        h1 = a1b("h1", [P, NH, V1])
        sq = a1b("sq", [P, NH, DH])
        hsum = a1b("hsum", [P, NH])
        den = a1b("den", [P, NT, NH])
        vsum = a1b("vsum", [P, NT, NH])
        rec = a1b("rec", [P, NT, NH])

        a2 = Arena(nc, keep.at)
        xn2 = a2("xn2", [P, NT, E])
        xT2 = a2("xT2", [P, 2, KC, P])
        rw = a2("rw", [P, KC, NE])
        eb = a2("eb", [P, NE])
        sc = a2("sc", [P, NT, NE])
        sw = a2("sw", [P, NT, NE])
        eq = a2("eq", [P, NT, NE])
        oh = a2("oh", [P, TOPK, NT, NE])
        pr = a2("pr", [P, NT, NE])
        pr4 = a2("pr4", [P, TOPK, NT, NE])
        mx = a2("mx", [P, NT])
        ix = a2("ix", [P, NT])
        csum = a2("csum", [P, NT])
        crec = a2("crec", [P, NT])
        slf = a2("slf", [P, TOPK, NT])
        ckr = a2("ckr", [P, TOPK, NT])
        selb = a2("selb", [P, NT, NE], BF16)
        tri = a2("tri", [P, P], BF16)
        onesb = a2("onesb", [P, P], BF16)
        iotam = a2("iotam", [P, NE])
        iota256 = a2("iota256", [P, 8])
        iotan = a2("iotan", [1, ETILES + 1])
        cnt = a2("cnt", [P, NE, NT])
        d0 = a2("d0", [P, NE, NT])
        incl = a2("incl", [P, NE, NT])
        excl = a2("excl", [P, NE, NT])
        nt8 = a2("nt8", [P, NE, 8])
        nte = a2("nte", [P, NE])
        ton = a2("ton", [P, NE])
        tinc = a2("tinc", [P, NE])
        texc = a2("texc", [P, NE])
        rowb = a2("rowb", [P, NE])
        full = a2("full", [P, NT, NE])
        ecmp = a2("ecmp", [1, ETILES + 1, NE])
        ecf = a2("ecf", [1, ETILES + 1])

        a3 = Arena(nc, a2.at)
        gu_raw = a3("gu_raw", [P, 2, KC, 2 * FI])
        dn_raw = a3("dn_raw", [FH, 2, 2, E])
        gu_hi = a3("gu_hi", [P, 2, KC, 2 * FI], F32R)
        gu_lo = a3("gu_lo", [P, 2, KC, 2 * FI], F32R)
        dn_hi = a3("dn_hi", [FH, 2, 2, E], F32R)
        dn_lo = a3("dn_lo", [FH, 2, 2, E], F32R)
        xr = a3("xr", [P, 2, 2, E])
        x_hi = a3("x_hi", [P, 2, KC, P], F32R)
        x_lo = a3("x_lo", [P, 2, KC, P], F32R)
        sg = a3("sg", [P, 2, FI])
        hh = a3("hh", [P, 2, FI])
        h_hi = a3("h_hi", [FH, 2, 2, P], F32R)
        h_lo = a3("h_lo", [FH, 2, 2, P], F32R)
        yo = a3("yo", [P, 2, E])

        a4 = Arena(nc, keep.at)
        G = a4("G", [P, CPB, TOPK, E])
        qf = a4("qf", [P, CPB, E])
        cr = Arena(nc, a3.at)("cr", [P, 2, CPB, E])
        k_hi = a4("k_hi", [P, CPB, E], F32R)
        k_lo = a4("k_lo", [P, CPB, E], F32R)
        v_hi = a4("v_hi", [P, KC, S], F32R)
        v_lo = a4("v_lo", [P, KC, S], F32R)
        q_hi = a4("q_hi", [P, CPB, E], F32R)
        q_lo = a4("q_lo", [P, CPB, E], F32R)
        sf = a4("sf", [P, KC, E])
        s_hi = a4("s_hi", [P, KC, E], F32R)
        s_lo = a4("s_lo", [P, KC, E], F32R)

        a5 = Arena(nc, keep.at)
        w_raw, w_hi, w_lo = [], [], []
        for p in range(2):
            w_raw.append(a5(f"w_raw{p}", [P, 3, KC * BLK]))
            w_hi.append(a5(f"w_hi{p}", [P, 3, KC * BLK], F32R))
            w_lo.append(a5(f"w_lo{p}", [P, 3, KC * BLK], F32R))
            assert p or a5.at <= keep.at + 4 * (CPB * TOPK * E + CPB * E)
        f_hi = a5("f_hi", [P, KC, NT * P], F32R)
        f_lo = a5("f_lo", [P, KC, NT * P], F32R)
        xn4 = a5("xn4", [P, CPB, E])
        fsg = a5("fsg", [P, 2, 512])
        fh = a5("fh", [P, 2, 512])
        fh_hi = a5("fh_hi", [P, 2, HCB, 512], F32R)
        fh_lo = a5("fh_lo", [P, 2, HCB, 512], F32R)

        sp_note, pool_note, act_note, dve_note = sem("sp_note"), sem("pool_note"), sem("act_note"), sem("dve_note")
        dve_step, act_step, pool_step = sem("dve_step"), sem("act_step"), sem("pool_step")
        stage_done = [sem(f"stage_done{k}") for k in range(6)]
        x_loaded = [sem(f"x_loaded{b}") for b in range(B)]
        ctxT_loaded = [sem(f"ctxT_loaded{b}") for b in range(2)]
        small_loaded, consts_ready = sem("small_loaded"), sem("consts_ready")
        wg_zeroed, wg_ready = sem("wg_zeroed"), sem("wg_ready")
        mv_ready, std_ready, qn_ready = sem("mv_ready"), sem("std_ready"), sem("qn_ready")
        xT_done, xT_kept = sem("xT_done"), sem("xT_kept")
        gates_done, gates_kept = sem("gates_done"), sem("gates_kept")
        lsig_ready, aM_ready, exps_ready, dg_ready = sem("lsig_ready"), sem("aM_ready"), sem("exps_ready"), sem("dg_ready")
        tok_done, M_stored, zero_filled = sem("tok_done"), sem("M_stored"), sem("zero_filled")
        tile_loaded = [sem(f"tile_loaded{p}") for p in range(2)]
        qk_done, inter_done, intra_done, st_done = sem("qk_done"), sem("inter_done"), sem("intra_done"), sem("st_done")
        arg_made = sem("arg_made")
        arg_ready, C_ready, h1_read, stm_ready = sem("arg_ready"), sem("C_ready"), sem("h1_read"), sem("stm_ready")
        hc_ready, sq_used, var_ready = sem("hc_ready"), sem("sq_used"), sem("var_ready")
        qs_ready, v1_ready, D_ready, sq_ready, hl_ready, std_h_ready = [sem(n) for n in ("qs_ready", "v1_ready", "D_ready", "sq_ready", "hl_ready", "std_h_ready")]
        qe_ready, kw_ready, arg_masked, St_ready, St_decayed = [sem(n) for n in ("qe_ready", "kw_ready", "arg_masked", "St_ready", "St_decayed")]
        xn2_ready, rout_loaded = sem("xn2_ready"), sem("rout_loaded")
        sc_done, sc_ready, sel_ready, pos_done = sem("sc_done"), sem("sc_ready"), sem("sel_ready"), sem("pos_done")
        slots_ready, xs_written, etab_ready, shared_stored = [sem(n) for n in ("slots_ready", "xs_written", "etab_ready", "shared_stored")]
        ew_loaded = [sem(f"ew_loaded{p}") for p in range(2)]
        xr_loaded = [sem(f"xr_loaded{p}") for p in range(2)]
        gw_hi, gw_lo, dw_hi, dw_lo = sem("gw_hi"), sem("gw_lo"), sem("dw_hi"), sem("dw_lo")
        xT_e, x_hi_e, x_lo_e = sem("xT_e"), sem("x_hi_e"), sem("x_lo_e")
        gu_e, sg_e, hh_e = sem("gu_e"), sem("sg_e"), sem("hh_e")
        hT_e, h_hi_e, h_lo_e, dn_e, y_e, y_added = [sem(n) for n in ("hT_e", "h_hi_e", "h_lo_e", "dn_e", "y_e", "y_added")]
        ys_written = [sem(f"ys_written{q}") for q in range(2)]
        g_loaded = [sem(f"g_loaded{i}") for i in range(CPB)]
        g_used, k_loaded, v_loaded = sem("g_used"), sem("k_loaded"), sem("v_loaded")
        k_hi_x, k_lo_x, v_hi_x, v_lo_x = [sem(n) for n in ("k_hi_x", "k_lo_x", "v_hi_x", "v_lo_x")]
        statsx_ready, mvx_ready, stdx_ready, qf_ready, q_hi_x, q_lo_x = [sem(n) for n in ("statsx_ready", "mvx_ready", "stdx_ready", "qf_ready", "q_hi_x", "q_lo_x")]
        s_done, s_sig, s_hi_x, s_lo_x, o_done, o_added = [sem(n) for n in ("s_done", "s_sig", "s_hi_x", "s_lo_x", "o_done", "o_added")]
        xn4_ready, fT_done, f_hi_ready, f_lo_ready = [sem(n) for n in ("xn4_ready", "fT_done", "f_hi_ready", "f_lo_ready")]
        fw_loaded = [sem(f"fw_loaded{p}") for p in range(2)]
        fw_hi, fw_lo = sem("fw_hi"), sem("fw_lo")
        fgu, fsg_ready, fh_ready, fh_hi_ready, fh_lo_ready, fdn, fadd, next_stats = [
            sem(n) for n in ("fgu", "fsg_ready", "fh_ready", "fh_hi_ready", "fh_lo_ready", "fdn", "fadd", "next_stats")]
        out_written = sem("out_written")
        scaled_heads, mixed = sem("scaled_heads"), sem("mixed")

        ENGINES = 5

        def stage_end(eng, k):
            eng.drain().then_inc(stage_done[k], 1)
            eng.wait_ge(stage_done[k], ENGINES)

        def bc(ap, shape):
            while len(ap.shape) < len(shape):
                ap = ap.unsqueeze(len(ap.shape))
            return ap.to_broadcast(shape)

        def flat(ap):
            return ap.rearrange("p a b -> p (a b)")

        def heads(ap):
            return ap.rearrange("p (h d) -> p h d", h=NH)

        def heads_of(t):
            return qT[:, bass.ds(t, 1)].rearrange("p o k n -> p (o k n)").rearrange("p (h d) -> p h d", h=NH)

        def mlstm_tiles(loop):
            with loop(B - 1) as i:
                for k in range(1, CPB + 1):
                    yield i, k, True
            for k in range(1, CPB):
                yield B - 1, k, False

        def where(i, k):
            return CPB * i + k, i + k // CPB, k % CPB, k % 2, 48 * (2 * i + k // 2 + 1)

        E_LOOPS = (HALVES - 2) // 4 - 1

        S_LOOPS = 2 * SHARED_T // 4 - 1

        def shared_steps(eng):
            with eng.Fori(0, S_LOOPS) as i:
                for k in range(1, 5):
                    yield i, k, True

        def border_steps():
            for k in range(1, 5):
                yield S_LOOPS, k, True

        def routed_steps(eng):
            with eng.Fori(S_LOOPS + 1, E_LOOPS) as i:
                for k in range(1, 5):
                    yield i, k, True
            for k in range(1, HALVES - 4 * E_LOOPS):
                yield E_LOOPS, k, False

        def kept(i, m):
            return isinstance(i, int) and 2 * i + m < SHARED_T

        def weights_loaded(i, m):
            skipped = 0 if isinstance(i, int) and 2 * i + m < 2 else SHARED_T // 2 - 1
            return 32 * (i + m // 2 + 1 - skipped)

        def batch_steps(loop):
            with loop(B - 1) as b:
                yield b, True
            yield B - 1, False

        UNITS = NBLK * B
        F_LOOPS = (UNITS - B) // 8

        def ffn_first():
            for k in range(1, B):
                yield 0, k, True

        def ffn_steps(eng):
            with eng.Fori(0, F_LOOPS) as i:
                for k in range(B, B + 8):
                    yield i, k, True
            for k in range(B, UNITS - 8 * F_LOOPS):
                yield F_LOOPS, k, False

        def tbank(i):
            return (pC, pD)[i // 2][:, i % 2]

        block = stack.enter_context(nc.Block())

        @block.sync
        def _(sp):
            for q in range(2):
                sp.sem_inc(ys_written[q], 16)
            for b in range(B):
                sp.dma_start(X[:, CPB * b:CPB * (b + 1), :],
                             x[b].rearrange("(i p) f -> p i f", p=P)).then_inc(x_loaded[b], 16)
                if b == 0:
                    sp.wait_ge(wg_zeroed, 1)
                    with nc.allow_non_contiguous_dma(reason="one value per partition"):
                        sp.dma_start(wg[:, :, 0:NH], Wi.rearrange("(c p) h -> p c h", p=P)).then_inc(small_loaded, 16)
                        sp.dma_start(wg[:, :, 32:32 + NH], Wf.rearrange("(c p) h -> p c h", p=P)).then_inc(small_loaded, 16)
                        sp.dma_start(gb[0:NH, :], bi.rearrange("(h o) -> h o", o=1)).then_inc(small_loaded, 16)
                        sp.dma_start(gb[32:32 + NH, :], bf.rearrange("(h o) -> h o", o=1)).then_inc(small_loaded, 16)
                    sp.dma_start(lnb[:, :], ln_scale.rearrange("(o f) -> o f", o=1).to_broadcast([P, E])).then_inc(small_loaded, 16)
                if b >= 2:
                    sp.wait_ge(gates_done, b - 1)
                sp.dma_start(ctxTb[:, b % 2], ctxT[b].rearrange("(k p) s -> p k s", p=P)).then_inc(ctxT_loaded[b % 2], 16)
            def fill(t):
                sp.dma_start(Xs[bass.ds(t * ZROWS, ZROWS), :].rearrange("(r p) f -> p r f", p=ZP),
                             zero[0:ZP, :].unsqueeze(1).to_broadcast([ZP, 8, E])).then_inc(zero_filled, 16)

            sp.wait_ge(consts_ready, 1)
            for t in range(8, 12):
                fill(t)
            sp.wait_ge(aM_ready, 1)
            sp.dma_start(M_dram, Mq[:, :]).then_inc(M_stored, 16)
            sp.wait_ge(M_stored, 16)
            stage_end(sp, 0)

            with sp.Fori(0, B) as b:
                for c in range(CPB):
                    p, t = c % 2, CPB * b + c
                    sp.wait_ge(qk_done, done(NG * (t - 2) + 3, QK))
                    sp.dma_start(kT[:, p], ctxT[bass.ds(b, 1), :, c * P:(c + 1) * P].rearrange("o (k p) s -> p (o k) s", p=P)).then_inc(tile_loaded[p], 16)
                    sp.dma_start(cx[:, p], ctx[bass.ds(b, 1), c * P:(c + 1) * P, :].rearrange("o p f -> p (o f)")).then_inc(tile_loaded[p], 16)
                    sp.dma_start(Mb[:, p], M_dram[bass.ds(b * 32, NH), c * P:(c + 1) * P].unsqueeze(0).to_broadcast([P, NH, P])).then_inc(tile_loaded[p], 16)
                    if p == 1:
                        fill(sp.snap(2 * b + c // 2))
            stage_end(sp, 1)

            sp.dma_start(rw[:, :, :], router_wT.rearrange("(k p) e -> p k e", p=P)).then_inc(rout_loaded, 16)
            sp.dma_start(eb[:, :], e_bias.rearrange("(o f) -> o f", o=1).to_broadcast([P, NE])).then_inc(rout_loaded, 16)

            for t in range(12, NT):
                fill(t)

            def load_rows(i, m, shared=False):
                p, n = m % 2, 2 * i + m
                if not isinstance(i, int):
                    n = sp.snap(n)
                rows, row = (Xt, n * MT) if shared else (Xs, (n - SHARED_T) * MT)
                turned = done(2 * n - 3, 3)
                sp.wait_ge(xT_e, turned)
                sp.sem_inc(sp_note, 1)
                sp.dma_start(xr[:, p], rows[bass.ds(row, MT), :].rearrange("(q p) f -> p q f", p=P)).then_inc(xr_loaded[p], 16)

            def load_weights(i, m, e=None):
                p, n = m % 2, 2 * i + m
                if not isinstance(i, int):
                    n = sp.snap(n)
                for s in (gw_hi, gw_lo, dw_hi, dw_lo):
                    sp.wait_ge(s, done(n - 2))
                sp.sem_inc(sp_note, 1)
                if e is None:
                    e = sp.value_load(etab[0:1, bass.ds(n, 1)], min_val=0, max_val=NE)
                sp.dma_start(gu_raw[:, p], gate_upT[bass.ds(e, 1)].rearrange("o p k f -> p (o k) f")).then_inc(ew_loaded[p], 16)
                sp.dma_start(dn_raw[:, p], downT[bass.ds(e, 1)].rearrange("o p j f -> p (o j) f")).then_inc(ew_loaded[p], 16)

            def store_half(i, k):
                u, q = 4 * i + k, k % 2
                sp.wait_ge(y_e, done(u))
                sp.dma_start(Ys[bass.ds((u - 2 * SHARED_T) * P, P), :], yo[:, q]).then_inc(ys_written[q], 16)

            load_weights(0, 0, e=0)
            load_weights(0, 1, e=0)
            sp.wait_ge(xn2_ready, NT)
            sp.dma_start(Xt.rearrange("(t p) f -> p t f", p=P), xn2[:, :, :]).then_inc(shared_stored, 16)
            sp.wait_ge(shared_stored, 16)
            for m in range(3):
                load_rows(0, m, shared=True)
            with sp.Fori(0, S_LOOPS - 1) as i:
                for m in (3, 4):
                    load_rows(i, m, shared=True)
            load_rows(S_LOOPS - 1, 3, shared=True)
            sp.wait_ge(etab_ready, 1)
            load_weights(S_LOOPS - 1, 4)
            sp.wait_ge(xs_written, 16 * NT * TOPK)
            load_rows(S_LOOPS - 1, 4)
            for m in (3, 4):
                load_rows(S_LOOPS, m)
                load_weights(S_LOOPS, m)

            def load_k(b):
                sp.dma_start(cr[:, 0], ctx[bass.ds(b, 1)].rearrange("o (i p) f -> p (o i) f", p=P)).then_inc(k_loaded, 16)

            def load_v(b):
                sp.dma_start(cr[:, 1], ctxT[bass.ds(b, 1)].rearrange("o (k p) s -> p (o k) s", p=P)).then_inc(v_loaded, 16)

            for i, k, looped in routed_steps(sp):
                if not looped and k == 1:
                    load_k(0)
                    load_v(0)
                if k % 2 == 0 and (looped or 2 * i + k // 2 + 2 < ETILES):
                    load_rows(i, k // 2 + 2)
                    load_weights(i, k // 2 + 2)
                store_half(i, k - 1)
            store_half(0, HALVES - 1)
            for q in range(2):
                sp.wait_ge(ys_written[q], 16 * (ETILES - SHARED_T + 1))
            stage_end(sp, 3)

            with sp.Fori(0, B - 1) as b:
                sp.wait_ge(k_lo_x, b + 1)
                load_k(b + 1)
                sp.wait_ge(v_lo_x, b + 1)
                load_v(b + 1)

            def load_block(i, p):
                blk = 2 * i + p
                sp.wait_ge(fw_hi, done(blk - 2))
                sp.wait_ge(fw_lo, done(blk - 2))
                for m, w in enumerate((w_gateT, w_upT, w_downT)):
                    sp.dma_start(w_raw[p][:, m], w[bass.ds(blk, 1)].rearrange("o p f -> p (o f)")).then_inc(fw_loaded[p], 16)

            sp.wait_ge(g_used, NT)
            sp.wait_ge(q_lo_x, NT)
            load_block(0, 0)
            stage_end(sp, 4)

            load_block(0, 1)
            with sp.Fori(1, NBLK // 2) as i:
                for p in range(2):
                    load_block(i, p)
            for g in range(B):
                sp.wait_ge(fadd, done(4 * (UNITS - B + g) + 3, 4))
                sp.dma_start(out[g].rearrange("(i p) f -> p i f", p=P), X[:, CPB * g:CPB * (g + 1), :]).then_inc(out_written, 16)
            sp.wait_ge(out_written, 16 * B)

        @block.gpsimd
        def _(pool):
            for s in (hl_ready, kw_ready, arg_masked, St_ready, gw_lo, dw_lo, fw_lo, fh_lo_ready):
                pool.sem_inc(s, 2)
            steps = Steps(pool, pool_step)
            steps(pool.memset(wg[:, :, :], 0.0))
            pool.sem_inc(wg_zeroed, 1)
            pool.memset(eps[:, 0:1], EPS_LN)
            pool.memset(eps[:, 1:2], EPS_H)
            pool.memset(onesf[:, :], 1.0)
            pool.memset(zero[:, :], 0.0)
            pool.memset(IG[:, :], 0.0)
            pool.memset(FG[:, :], 0.0)
            pool.memset(bms[:, :], QSCALE)
            pool.memset(bmask[:, :], 1.0)
            steps(pool.memset(ident[:, :], 0.0))
            steps(pool.affine_select(out=ident[:, :], in_=ident[:, :], compare_op=ALU.not_equal, fill=1.0,
                                     base=0, pattern=[[-1, P]], channel_multiplier=1))
            for m in (bms, bmask):
                steps(pool.affine_select(out=m[:, :], in_=m[:, :], compare_op=ALU.is_ge, fill=0.0,
                                         base=0, pattern=[[-DH, HPG]], channel_multiplier=1))
                steps(pool.affine_select(out=m[:, :], in_=m[:, :], compare_op=ALU.is_ge, fill=0.0,
                                         base=DH - 1, pattern=[[DH, HPG]], channel_multiplier=-1))
            for j in range(2):
                steps(pool.tensor_copy(mask264[:, HPG * j:HPG * (j + 1), :], bc(bmask[:, :], [P, HPG, V1])))
            pool.sem_inc(consts_ready, 1)
            stage_end(pool, 0)

            steps(pool.memset(v1[:, :, :, :], 1.0))
            pool.sem_inc(consts_ready, 1)
            masked = pool.to_reg(NEG)

            def weighted_k(i, k):
                t, b, c, p, loads = where(i, k)
                if c < CPB - 1:
                    pool.wait_ge(tile_loaded[p], loads)
                    pool.wait_ge(qk_done, done(NG * (t - 2) + 3, QK))
                    pool.tensor_tensor(kw[:, p], heads(cx[:, p]), bc(tk[:, 1, c, bass.ds(b * 32, NH)], [P, NH, DH]),
                                       ALU.mult).then_inc(kw_ready, 1)

            def mask(i, k):
                t, b, c, p, loads = where(i, k)
                pool.wait_ge(tile_loaded[p], loads)
                if not isinstance(t, int) or t >= 2:
                    pool.wait_ge(C_ready, done(NG * (t - 2) + 3))
                pool.tensor_tensor(Dm[:, p, VH:], bc(tk[:, 3, c, bass.ds(b * 32 + VH, NH - VH)], [P, NH - VH, P]), Mb[:, p, VH:],
                                   ALU.subtract).then_inc(arg_made, 1)
                pool.wait_ge(arg_made, t + 1)
                pool.sem_inc(pool_note, 1)
                pool.wait_ge(arg_ready, done(t))
                pool.sem_inc(pool_note, 1)
                pool.affine_select(out=Dm[:, p], in_=Dm[:, p], compare_op=ALU.is_ge, fill=masked,
                                   base=0, pattern=[[0, NH], [1, P]], channel_multiplier=-1).then_inc(arg_masked, 1)

            def state(i, k):
                t, b, c, p, loads = where(i, k)
                if c < CPB - 1:
                    if c > 0:
                        pool.wait_ge(inter_done, done(3 * b + c - 1))
                        pool.tensor_tensor(St[:, :, :], St[:, :, :], bc(decB[:, c, bass.ds(b * 32, NH)], [P, NH, V1]),
                                           ALU.mult).then_inc(St_decayed, 1)
                        pool.wait_ge(St_decayed, 3 * b + c + 1)
                    pool.wait_ge(stm_ready, done(3 * b + c))
                    if c == 0:
                        pool.sem_inc(St_decayed, 1)
                        pool.sem_inc(St_ready, 1)
                    else:
                        pool.tensor_tensor(St[:, :, :], St[:, :, :], stm[:, :, :], ALU.add).then_inc(St_ready, 1)

            def scaled(i, k):
                t = CPB * i + k
                pool.wait_ge(sq_ready, done(t))
                pool.sem_inc(pool_note, 1)
                hc = heads_of(t)
                pool.tensor_tensor(hc, hc, heads(lnb[:, :]), ALU.mult).then_inc(hl_ready, 1)

            weighted_k(0, 0)
            mask(0, 0)
            weighted_k(0, 1)
            mask(0, 1)
            state(0, 0)
            for i, k, looped in mlstm_tiles(lambda n: pool.Fori(0, n)):
                more = looped or CPB * i + k + 1 < NT
                if more:
                    weighted_k(i, k + 1)
                    mask(i, k + 1)
                state(i, k)
                scaled(i, k - 1)
            scaled(0, NT - 1)
            stage_end(pool, 1)
            for g in range(1, B):
                gs = slice(CPB * g, CPB * (g + 1))
                pool.wait_ge(scaled_heads, g + 1)
                pool.wait_ge(mixed, g)
                pool.tensor_tensor(flat(X[:, gs, :]), flat(X[:, gs, :]), qT[:, gs].rearrange("p c k n -> p (c k n)"), ALU.add).then_inc(mixed, 1)

            pool.memset(onesb[:, :], 1.0)
            pool.memset(tri[:, :], 1.0)
            pool.memset(d0[:, :, :], 1.0)
            pool.memset(ton[:, :], 1.0)
            pool.iota(iota256[:, :], [[MT, 8]], base=0, channel_multiplier=0, allow_small_or_imprecise_dtypes=True)
            pool.iota(iotan[:, :], [[1, ETILES + 1]], base=0, channel_multiplier=0, allow_small_or_imprecise_dtypes=True)
            steps(pool.iota(iotam[:, :], [[1, NE]], base=-99, channel_multiplier=0, allow_small_or_imprecise_dtypes=True))
            pool.affine_select(out=tri[:, :], in_=tri[:, :], compare_op=ALU.is_gt, fill=0.0,
                               base=0, pattern=[[1, P]], channel_multiplier=-1)
            steps(pool.affine_select(out=d0[:, :, :], in_=d0[:, :, :], compare_op=ALU.is_gt, fill=0.0,
                                     base=0, pattern=[[0, NE], [1, NT]], channel_multiplier=0))
            pool.sem_inc(consts_ready, 1)
            def gu_split(i, m):
                p, n = m % 2, 2 * i + m
                pool.wait_ge(gw_hi, done(n))
                pool.tensor_tensor(gu_lo[:, p], gu_raw[:, p], gu_hi[:, p].bitcast(F32), ALU.subtract).then_inc(gw_lo, 1)

            def dn_split(i, m):
                p, n = m % 2, 2 * i + m
                pool.wait_ge(dw_hi, done(n))
                pool.tensor_tensor(dn_lo[:, p], dn_raw[:, p], dn_hi[:, p].bitcast(F32), ALU.subtract).then_inc(dw_lo, 1)

            for m in range(2):
                gu_split(0, m)
                dn_split(0, m)
            for s in (gw_lo, dw_lo):
                pool.wait_ge(s, done(1))
                pool.sem_inc(s, SHARED_T - 2)
            pool.wait_ge(zero_filled, 16 * NT)
            pool.wait_ge(slots_ready, 1)
            for t in range(NT):
                for k in range(TOPK):
                    pool.indirect_dma_start(out=Xs, out_offset=bass.IndirectOffsetOnAxis(ap=slot[:, t, k:k + 1], axis=0),
                                            in_=xn2[:, t, :], in_offset=None).then_inc(xs_written, 16)
            for i, k, looped in chain(border_steps(), routed_steps(pool)):
                if k % 2 == 1 and (looped or 2 * i + (k + 1) // 2 < ETILES) and not kept(i, (k + 1) // 2):
                    dn_split(i, (k + 1) // 2)
                if k % 2 == 0 and (looped or 2 * i + (k + 2) // 2 < ETILES):
                    gu_split(i, (k + 2) // 2)
            stage_end(pool, 3)

            def gather(b, tiles):
                for i in tiles:
                    t = CPB * b + i
                    if b >= 1:
                        pool.wait_ge(g_used, t - CPB + 1)
                    for k in range(TOPK):
                        pool.indirect_dma_start(out=G[:, i, k, :], out_offset=None, in_=Ys,
                                                in_offset=bass.IndirectOffsetOnAxis(ap=slot[:, t, k:k + 1], axis=0)).then_inc(g_loaded[i], 16)

            gather(0, range(CPB))
            gather(1, range(CPB))
            for b in range(1, B):
                pool.wait_ge(k_hi_x, b + 1)
                pool.tensor_tensor(k_lo[:, :, :], cr[:, 0], k_hi[:, :, :].bitcast(F32), ALU.subtract).then_inc(k_lo_x, 1)
                if b < B - 1:
                    gather(b + 1, range(CPB))
                pool.wait_ge(v_hi_x, b + 1)
                pool.tensor_tensor(v_lo[:, :, :], cr[:, 1], v_hi[:, :, :].bitcast(F32), ALU.subtract).then_inc(v_lo_x, 1)
            def w_split(i, m):
                p, blk = m % 2, 2 * i + m
                pool.wait_ge(fw_hi, done(blk))
                pool.tensor_tensor(w_lo[p][:, :, :], w_raw[p][:, :, :], w_hi[p][:, :, :].bitcast(F32), ALU.subtract).then_inc(fw_lo, 1)

            w_split(0, 0)
            stage_end(pool, 4)

            def h_split(i, k):
                for j in range(HCB):
                    pool.wait_ge(fh_hi_ready, done(HCB * (8 * i + k) + j))
                    pool.tensor_tensor(fh_lo[:, k % 2, j], fh[:, j], fh_hi[:, k % 2, j].bitcast(F32), ALU.subtract).then_inc(fh_lo_ready, 1)

            h_split(0, 0)
            for i, k, looped in chain(ffn_first(), ffn_steps(pool)):
                h_split(i, k)
                if k % 4 == 2 and (looped or 2 * i + (k + 2) // 4 < NBLK):
                    w_split(i, (k + 2) // 4)

        @block.scalar
        def _(act):
            act.sem_inc(y_e, 2 + 2 * SHARED_T)
            for s in (qe_ready, qs_ready, v1_ready, D_ready, sq_ready, gw_hi, dw_hi, x_hi_e, sg_e, h_hi_e,
                      s_sig, fw_hi, fsg_ready, fh_hi_ready):
                act.sem_inc(s, 2)
            steps = Steps(act, act_step)

            def std_of(tiles):
                return act.activation(std[:, tiles], mv[:, tiles, 1], ACT.Sqrt, bias=eps[:, 0:1])

            act.wait_ge(consts_ready, 1)
            for b in range(B):
                act.wait_ge(mv_ready, b + 1)
                std_of(slice(CPB * b, CPB * (b + 1))).then_inc(std_ready, 1)
                for k in range(KC):
                    act.wait_ge(xT_done, KC * b + k + 1)
                    act.activation(qT[:, CPB * b:CPB * (b + 1), k], (pA, pB)[k // 2][:, k % 2].rearrange("p (i n) -> p i n", n=P), ACT.Copy).then_inc(xT_kept, 1)
            act.activation(t2[:, 0:1], eps[:, 0:1], ACT.Exp)
            act.wait_ge(gates_kept, B)
            steps(act.activation(t1[:, :], FG[:, :], ACT.Abs))
            steps(act.activation(t2[:, :], t1[:, :], ACT.Exp, scale=-1.0))
            act.activation(t1[:, :], t2[:, :], ACT.Ln, bias=1.0).then_inc(lsig_ready, 1)
            act.wait_ge(aM_ready, 2)
            for c in range(CPB):
                cs = slice(c * P, (c + 1) * P)
                act.activation(WQ[:, cs], Mq[:, cs], ACT.Exp, bias=mprev[:, c:c + 1], scale=-1.0)
                act.activation(WK[:, cs], Aq[:, cs], ACT.Exp, bias=mneg[:, c:c + 1])
                act.activation(dec[:, c:c + 1], mprev[:, c:c + 1], ACT.Exp, bias=mneg[:, c:c + 1])
            act.activation(NR[:, :], t2[:, :], ACT.Exp, scale=-1.0).then_inc(exps_ready, 1)
            for q in range(4):
                act.wait_ge(tok_done, q + 1)
                act.activation(flat(tk[:, q]), (pA, pB)[q // 2][:, q % 2], ACT.Copy)
            act.wait_ge(tok_done, 5)
            act.activation(flat(decB[:, :, :]), pC[:, 0], ACT.Copy)
            stage_end(act, 0)

            act.wait_ge(consts_ready, 2)

            def spread_q(i, k):
                t, b, c, p, loads = where(i, k)
                act.wait_ge(qk_done, done(NG * (t - 2) + 3, QK))
                qt = qT[:, bass.ds(t, 1)].rearrange("p o k n -> p (o k) n")
                for h in range(HPG):
                    ins = act.activation(qe[:, p, :, h, :], qt, ACT.Copy, scale=bms[:, h:h + 1])
                ins.then_inc(qe_ready, 1)
                if c > 0:
                    act.activation(qs[:, p], qt, ACT.Copy, scale=QSCALE).then_inc(qs_ready, 1)

            def values(i, k):
                t, b, c, p, loads = where(i, k)
                act.wait_ge(tile_loaded[p], loads)
                act.wait_ge(intra_done, done(t - 2))
                act.activation(v1[:, p, :, 0:DH], heads(cx[:, p]), ACT.Copy).then_inc(v1_ready, 1)

            def decays(i, k):
                t, b, c, p, loads = where(i, k)
                act.wait_ge(arg_masked, done(t))
                act.activation(Dm[:, p], Dm[:, p], ACT.Exp).then_inc(D_ready, 1)

            def squares(i, k):
                t = CPB * i + k
                act.wait_ge(hc_ready, done(t))
                act.wait_ge(sq_used, done(t - 1))
                act.sem_inc(act_note, 1)
                act.activation(sq[:, :, :], heads_of(t), ACT.Square).then_inc(sq_ready, 1)

            for k in range(2):
                spread_q(0, k)
                values(0, k)
                decays(0, k)
            spread_q(0, 2)
            for i, k, looped in mlstm_tiles(lambda n: act.Fori(0, n)):
                if looped or CPB * i + k + 1 < NT:
                    values(i, k + 1)
                    decays(i, k + 1)
                squares(i, k - 1)
                if looped or CPB * i + k + 2 < NT:
                    spread_q(i, k + 2)
            squares(0, NT - 1)
            act.wait_ge(var_ready, 1)
            act.activation(flat(gain[:, :, :]), flat(vsum[:, :, :]), ACT.Sqrt).then_inc(std_h_ready, 1)
            stage_end(act, 1)

            for t in range(NT):
                if t % CPB == 0:
                    act.wait_ge(mv_ready, B + 1 + t // CPB)
                    std_of(slice(t, t + CPB)).then_inc(std_ready, 1)
                act.wait_ge(xT_done, KC * B + t + 1)
                if t >= 2:
                    act.wait_ge(sc_done, t - 1)
                act.activation(flat(xT2[:, t % 2]), pA[:, t % 2], ACT.Copy).then_inc(xT_kept, 1)

            def gu_split(i, m):
                p, n = m % 2, 2 * i + m
                act.wait_ge(ew_loaded[p], weights_loaded(i, m))
                act.wait_ge(gu_e, done(2 * n - 3, 3))
                act.activation(gu_hi[:, p], gu_raw[:, p], ACT.Copy).then_inc(gw_hi, 1)

            def dn_split(i, m):
                p, n = m % 2, 2 * i + m
                act.wait_ge(ew_loaded[p], weights_loaded(i, m))
                act.wait_ge(dn_e, done(2 * n - 3, 3))
                act.activation(dn_hi[:, p], dn_raw[:, p], ACT.Copy).then_inc(dw_hi, 1)

            def x_split(i, k):
                u, q = 4 * i + k, k % 2
                act.wait_ge(xT_e, done(u, 3))
                act.wait_ge(gu_e, done(u - 2, 3))
                act.activation(flat(x_hi[:, q]), pA[:, q], ACT.Copy).then_inc(x_hi_e, 1)

            def silu(i, k):
                u, q = 4 * i + k, k % 2
                act.wait_ge(gu_e, done(u, 3))
                act.wait_ge(hh_e, done(u - 2))
                act.activation(sg[:, q], pB[:, q, 0:FI], ACT.Silu).then_inc(sg_e, 1)

            def h_split(i, k):
                u, q = 4 * i + k, k % 2
                act.wait_ge(hT_e, done(u))
                act.wait_ge(dn_e, done(u - 2, 3))
                act.activation(flat(h_hi[:, q]), pC[0:FH, q, 0:2 * P], ACT.Copy).then_inc(h_hi_e, 1)

            def y_keep(i, k):
                u, q = 4 * i + k, k % 2
                act.wait_ge(dn_e, done(u, 3))
                act.wait_ge(ys_written[q], 16 * (2 * i + k // 2 + 1 - SHARED_T))
                act.activation(yo[:, q], pD[:, q], ACT.Copy).then_inc(y_e, 1)

            def step(i, k, looped, routed, stored):
                h_split(i, k - 1)
                if looped or 4 * i + k + 1 < HALVES:
                    x_split(i, k + 1)
                if routed and k % 2 == 1 and (looped or 2 * i + (k + 1) // 2 < ETILES) and not kept(i, (k + 1) // 2):
                    dn_split(i, (k + 1) // 2)
                if routed and k % 2 == 0 and (looped or 2 * i + (k + 2) // 2 < ETILES):
                    gu_split(i, (k + 2) // 2)
                silu(i, k)
                if stored:
                    y_keep(i, k - 1)

            act.wait_ge(sc_done, NT)
            act.activation(flat(sc[:, :, :]), pC[:, 0, 0:NT * NE], ACT.Sigmoid).then_inc(sc_ready, 1)
            for m in range(2):
                gu_split(0, m)
                dn_split(0, m)
            for s in (gw_hi, dw_hi):
                act.wait_ge(s, done(1))
                act.sem_inc(s, SHARED_T - 2)
            x_split(0, 0)
            x_split(0, 1)
            silu(0, 0)
            for i, k, looped in shared_steps(act):
                step(i, k, looped, routed=False, stored=False)
            for i, k, looped in border_steps():
                step(i, k, looped, routed=True, stored=False)
            for i, k, looped in routed_steps(act):
                step(i, k, looped, routed=True, stored=True)
            h_split(0, HALVES - 1)
            y_keep(0, HALVES - 1)
            stage_end(act, 3)

            def k_split(b):
                act.wait_ge(k_loaded, 16 * (b + 1))
                act.activation(k_hi[:, :, :], cr[:, 0], ACT.Copy).then_inc(k_hi_x, 1)

            def v_split(b):
                act.wait_ge(v_loaded, 16 * (b + 1))
                act.activation(v_hi[:, :, :], cr[:, 1], ACT.Copy).then_inc(v_hi_x, 1)

            def q_split(b):
                act.wait_ge(mvx_ready, b + 1)
                act.activation(stdx[:, :], mvx[:, :, 1], ACT.Sqrt, bias=eps[:, 0:1]).then_inc(stdx_ready, 1)
                for i in range(CPB):
                    act.wait_ge(qf_ready, CPB * b + i + 1)
                    act.activation(q_hi[:, i], qf[:, i, :], ACT.Copy).then_inc(q_hi_x, 1)

            k_split(0)
            v_split(0)
            q_split(0)
            for b, more in batch_steps(lambda n: act.Fori(0, n)):
                for n in range(KC):
                    act.wait_ge(s_done, KC * b + n + 1)
                    act.activation(sf[:, n], pA[:, n % 2], ACT.Sigmoid, scale=XSCALE).then_inc(s_sig, 1)
                    act.wait_ge(s_sig, done(KC * b + n))
                    act.activation(s_hi[:, n], sf[:, n], ACT.Copy).then_inc(s_hi_x, 1)
                if more:
                    k_split(b + 1)
                    q_split(b + 1)
                    act.wait_ge(o_done, done(KC * b + KC - 1))
                    v_split(b + 1)
            def w_split(i, m):
                p, blk = m % 2, 2 * i + m
                act.wait_ge(fw_loaded[p], 48 * (i + m // 2 + 1))
                act.wait_ge(fdn, done(4 * (4 * blk - 5) + 3, 20))
                act.activation(w_hi[p][:, :, :], w_raw[p][:, :, :], ACT.Copy).then_inc(fw_hi, 1)

            w_split(0, 0)
            stage_end(act, 4)

            act.wait_ge(mv_ready, 2 * B + 1)
            std_of(slice(0, NT)).then_inc(std_ready, 1)
            def f_split(g):
                for i in range(CPB):
                    t = CPB * g + i
                    act.wait_ge(fT_done, t + 1)
                    act.activation(f_hi[:, :, t * P:(t + 1) * P], tbank(i).rearrange("p (k n) -> p k n", k=KC), ACT.Copy).then_inc(f_hi_ready, 1)

            def gated(i, k):
                v = 8 * i + k
                for j in range(HCB):
                    act.wait_ge(fgu, done(HCB * v + j))
                    act.wait_ge(fh_ready, done(HCB * v + j - 2))
                    act.activation(fsg[:, j], pA[:, j], ACT.Silu).then_inc(fsg_ready, 1)
                for j in range(HCB):
                    act.wait_ge(fh_ready, done(HCB * v + j))
                    act.wait_ge(fdn, done(4 * (v - 2) + 3, 20))
                    act.activation(fh_hi[:, k % 2, j], fh[:, j], ACT.Copy).then_inc(fh_hi_ready, 1)

            f_split(0)
            f_split(1)
            gated(0, 0)
            for i, k, looped in ffn_first():
                if k + 1 < B:
                    f_split(k + 1)
                gated(i, k)
                if k == 2:
                    w_split(0, 1)
            for i, k, looped in ffn_steps(act):
                gated(i, k)
                if k % 4 == 2 and (looped or 2 * i + (k + 2) // 4 < NBLK):
                    w_split(i, (k + 2) // 4)

        @block.vector
        def _(dve):
            for s in (arg_ready, C_ready, h1_read, stm_ready, hc_ready, sq_used, y_added, x_lo_e, hh_e, h_lo_e, o_added, fh_ready):
                dve.sem_inc(s, 2)
            dve.sem_inc(fadd, 4)
            steps = Steps(dve, dve_step)

            def gates_keep(b):
                dve.wait_ge(gates_done, b + 1)
                dve.tensor_scalar(IG[32 * b:32 * b + NH, :], pC[0:NH, b % 2], gb[0:NH, 0:1], None, ALU.add)
                dve.tensor_scalar(FG[32 * b:32 * b + NH, :], pC[32:32 + NH, b % 2], gb[32:32 + NH, 0:1], None, ALU.add).then_inc(gates_kept, 1)

            def f_split(g):
                for i in range(CPB):
                    t = CPB * g + i
                    dve.wait_ge(f_hi_ready, t + 1)
                    ts = slice(t * P, (t + 1) * P)
                    dve.tensor_tensor(f_lo[:, :, ts], tbank(i).rearrange("p (k n) -> p k n", k=KC), f_hi[:, :, ts].bitcast(F32),
                                      ALU.subtract).then_inc(f_lo_ready, 1)

            def stats_of(t):
                steps(dve.bn_stats(stats[:, t, :], X[:, t, :]))
                return dve.bn_aggr(mv[:, t, :], stats[:, t, :])

            def normed(dst, t):
                return dve.tensor_scalar(dst, X[:, t, :], mv[:, t, 0:1], rstd[:, t:t + 1], ALU.subtract, ALU.mult)

            dve.wait_ge(small_loaded, 80)
            dve.tensor_tensor(wg[:, KC:2 * KC, :], wg[:, KC:2 * KC, :], wg[:, 2 * KC:, :], ALU.add).then_inc(wg_ready, 1)
            for b in range(B):
                dve.wait_ge(x_loaded[b], 16)
                for i in range(CPB):
                    ins = stats_of(CPB * b + i)
                ins.then_inc(mv_ready, 1)
                dve.wait_ge(mv_ready, b + 1)
                dve.wait_ge(std_ready, b + 1)
                steps(dve.reciprocal(rstd[:, CPB * b:CPB * (b + 1)], std[:, CPB * b:CPB * (b + 1)]))
                if b >= 2:
                    dve.wait_ge(xT_done, KC * (b - 1))
                for i in range(CPB):
                    ins = normed(qn[:, b % 2, i, :], CPB * b + i)
                ins.then_inc(qn_ready, 1)
                if b >= 1:
                    gates_keep(b - 1)
            gates_keep(B - 1)
            dve.wait_ge(gates_kept, B)
            dve.wait_ge(lsig_ready, 1)
            steps(dve.scalar_tensor_tensor(out=t2[:, :], in0=FG[:, :], scalar=0.0, in1=t1[:, :], op0=ALU.min, op1=ALU.subtract))
            steps(dve.tensor_tensor_scan(Fc[:, :], onesf[:, :], t2[:, :], 0.0, ALU.mult, ALU.add))
            steps(dve.tensor_tensor(Aq[:, :], IG[:, :], Fc[:, :], ALU.subtract))
            dve.tensor_tensor_scan(Mq[:, :], onesf[:, :], Aq[:, :], -3e38, ALU.mult, ALU.max).then_inc(aM_ready, 1)
            dve.wait_ge(aM_ready, 1)
            dve.tensor_tensor(t2[:, :], Fc[:, :], Mq[:, :], ALU.add)
            dve.tensor_copy(mprev[:, 0:1], Mq[:, 0:1])
            dve.tensor_copy(mprev[:, 1:CPB], Mq[:, P - 1:S - P:P])
            dve.tensor_scalar(mneg[:, :], Mq[:, P - 1:S:P], -1.0, None, ALU.mult).then_inc(aM_ready, 1)
            dve.wait_ge(exps_ready, 1)
            for c in range(CPB):
                ins = dve.tensor_scalar(DG[:, c, :], ident[:, :], dec[:, c:c + 1], None, ALU.mult)
            ins.then_inc(dg_ready, 1)
            stage_end(dve, 0)

            dve.wait_ge(small_loaded, 80)

            def exponents(i, k):
                t, b, c, p, loads = where(i, k)
                dve.wait_ge(tile_loaded[p], loads)
                dve.tensor_tensor(Dm[:, p, 0:VH], bc(tk[:, 3, c, bass.ds(b * 32, VH)], [P, VH, P]), Mb[:, p, 0:VH], ALU.subtract).then_inc(arg_ready, 1)

            def weights(i, k, groups):
                t, b, c, p, loads = where(i, k)
                dve.wait_ge(D_ready, done(t))
                dve.wait_ge(intra_done, done(t - 2))
                for j in groups:
                    dve.wait_ge(qk_done, done(NG * t + j, QK))
                    dve.tensor_tensor(Cm[:, p, HPG * j:HPG * (j + 1), :], Dm[:, p, HPG * j:HPG * (j + 1), :],
                                      pA[:, j % 2].rearrange("p (i s) -> p i s", i=HPG), ALU.mult).then_inc(C_ready, 1)

            def state_part(i, k):
                t, b, c, p, loads = where(i, k)
                if c < CPB - 1:
                    dve.wait_ge(st_done, done(3 * b + c))
                    dve.wait_ge(St_ready, done(3 * b + c - 1))
                    part = stm
                    if c == 0:
                        part = St
                        dve.wait_ge(inter_done, done(3 * b - 1))
                    dve.tensor_tensor(part[:, :, :].rearrange("p (j h) e -> p j (h e)", j=2), pD[:, :, 0:8 * V1],
                                      mask264[:, :, :].rearrange("p h e -> p (h e)").unsqueeze(1).to_broadcast([P, 2, 8 * V1]),
                                      ALU.mult).then_inc(stm_ready, 1)

            OUT = pB[:, :, 0:8 * V1].rearrange("p j (h e) -> p j h e", e=V1)
            INT = pC[:, :, 0:8 * V1].rearrange("p j (h e) -> p j h e", e=V1)
            H1 = h1[:, :, :].rearrange("p (j h) e -> p j h e", j=2)

            def gather_heads(i, k):
                t, b, c, p, loads = where(i, k)
                cols = bass.ds(b * 32, NH)
                dve.wait_ge(intra_done, done(t))
                if c == 0:
                    dve.tensor_copy(H1, OUT).then_inc(h1_read, 1)
                else:
                    dve.wait_ge(inter_done, done(3 * b + c - 1))
                    wq = tk[:, 0, c, cols].rearrange("p (j h) -> p j h", j=2).unsqueeze(3).to_broadcast([P, 2, 8, V1])
                    steps(dve.tensor_tensor(H1, INT, wq, ALU.mult))
                    dve.tensor_tensor(H1, H1, OUT, ALU.add).then_inc(h1_read, 1)

            def center(i, k):
                t, b, c, p, loads = where(i, k)
                dve.wait_ge(h1_read, done(t))
                steps(dve.tensor_reduce(hsum[:, :], h1[:, :, 0:DH], AX.X, ALU.add))
                dve.scalar_tensor_tensor(out=heads_of(t), in0=bc(hsum[:, :], [P, NH, DH]), scalar=-1.0 / DH, in1=h1[:, :, 0:DH],
                                         op0=ALU.mult, op1=ALU.add).then_inc(hc_ready, 1)
                steps(dve.tensor_copy(den[:, bass.ds(t, 1), :].rearrange("p o h -> p (o h)"), h1[:, :, DH]))

            def variance(i, k):
                t = CPB * i + k
                dve.wait_ge(sq_ready, done(t))
                dve.tensor_reduce(vsum[:, bass.ds(t, 1), :].rearrange("p o h -> p (o h)"), sq[:, :, :], AX.X, ALU.add).then_inc(sq_used, 1)

            exponents(0, 0)
            exponents(0, 1)
            weights(0, 0, range(NG))
            state_part(0, 0)
            for i, k, looped in mlstm_tiles(lambda n: steps.loop(n, MLSTM_STEPS)):
                gather_heads(i, k - 1)
                weights(i, k, range(0, 2))
                if looped or CPB * i + k + 1 < NT:
                    exponents(i, k + 1)
                weights(i, k, range(2, NG))
                center(i, k - 1)
                state_part(i, k)
                variance(i, k - 1)
            gather_heads(0, NT - 1)
            center(0, NT - 1)
            variance(0, NT - 1)
            dve.wait_ge(sq_used, done(NT - 1))
            dn, rc, vs, gn = flat(den[:, :, :]), flat(rec[:, :, :]), flat(vsum[:, :, :]), flat(gain[:, :, :])
            steps(dve.scalar_tensor_tensor(out=dn, in0=dn, scalar=-1.0, in1=dn, op0=ALU.mult, op1=ALU.max))
            nrm = tk[:, 2].rearrange("p c (b h) -> p b c h", b=B)[:, :, :, 0:NH]
            den4 = den[:, :, :].rearrange("p (b c) h -> p b c h", b=B)
            steps(dve.tensor_tensor(den4, den4, nrm, ALU.max))
            steps(dve.tensor_scalar(dn, dn, EPS_H, None, ALU.add))
            steps(dve.reciprocal(rc, dn))
            steps(dve.tensor_tensor(dn, rc, rc, ALU.mult))
            steps(dve.scalar_tensor_tensor(out=vs, in0=vs, scalar=1.0 / DH, in1=dn, op0=ALU.mult, op1=ALU.mult))
            dve.tensor_scalar(vs, vs, EPS_H, None, ALU.add).then_inc(var_ready, 1)
            dve.wait_ge(std_h_ready, 1)
            steps(dve.reciprocal(vs, gn))
            steps(dve.tensor_tensor(gn, rc, vs, ALU.mult))
            stage_end(dve, 1)

            def gained(g):
                gs = slice(CPB * g, CPB * (g + 1))
                hy = qT[:, gs].rearrange("p c k n -> p c (k n)").rearrange("p c (h d) -> p c h d", h=NH)
                dve.tensor_tensor(hy, hy, bc(gain[:, gs, :], [P, CPB, NH, DH]), ALU.mult).then_inc(scaled_heads, 1)

            def stats_r(g):
                dve.wait_ge(mixed, g + 1)
                for i in range(CPB):
                    ins = dve.bn_stats(stats[:, CPB * g + i, :], X[:, CPB * g + i, :])
                steps(ins)
                for i in range(CPB):
                    ins = dve.bn_aggr(mv[:, CPB * g + i, :], stats[:, CPB * g + i, :])
                ins.then_inc(mv_ready, 1)

            def norm_r(g):
                gs = slice(CPB * g, CPB * (g + 1))
                dve.wait_ge(mv_ready, B + 1 + g)
                dve.wait_ge(std_ready, B + 1 + g)
                steps(dve.reciprocal(rstd[:, gs], std[:, gs]))
                for t in range(CPB * g, CPB * (g + 1)):
                    normed(xn2[:, t, :], t).then_inc(xn2_ready, 1)

            gained(0)
            dve.wait_ge(scaled_heads, 1)
            dve.tensor_tensor(flat(X[:, 0:CPB, :]), flat(X[:, 0:CPB, :]), qT[:, 0:CPB].rearrange("p c k n -> p (c k n)"), ALU.add).then_inc(mixed, 1)
            stats_r(0)
            gained(1)
            gained(2)
            norm_r(0)
            gained(3)
            for g in range(1, B):
                stats_r(g)
                norm_r(g)
            dve.wait_ge(rout_loaded, 32)
            dve.wait_ge(consts_ready, 3)
            dve.wait_ge(sc_ready, 1)
            steps(dve.tensor_tensor(sw[:, :, :], sc[:, :, :], eb[:, :].unsqueeze(1).to_broadcast([P, NT, NE]), ALU.add))
            iot = iotam[:, :].unsqueeze(1).to_broadcast([P, NT, NE])
            for k in range(TOPK):
                steps(dve.tensor_reduce(mx[:, :], sw[:, :, :], AX.X, ALU.max))
                steps(dve.tensor_tensor(eq[:, :, :], sw[:, :, :], bc(mx[:, :], [P, NT, NE]), ALU.is_equal))
                steps(dve.tensor_tensor(eq[:, :, :], eq[:, :, :], iot, ALU.mult))
                steps(dve.tensor_reduce(ix[:, :], eq[:, :, :], AX.X, ALU.min))
                steps(dve.tensor_tensor(oh[:, k], iot, bc(ix[:, :], [P, NT, NE]), ALU.is_equal))
                steps(dve.scalar_tensor_tensor(out=flat(sw[:, :, :]), in0=flat(oh[:, k]), scalar=NEG, in1=flat(sw[:, :, :]),
                                               op0=ALU.mult, op1=ALU.add))
            steps(dve.tensor_tensor(pr[:, :, :], oh[:, 0], oh[:, 1], ALU.add))
            steps(dve.tensor_tensor(eq[:, :, :], oh[:, 2], oh[:, 3], ALU.add))
            dve.tensor_tensor(selb[:, :, :], pr[:, :, :], eq[:, :, :], ALU.add).then_inc(sel_ready, 1)
            steps(dve.tensor_tensor(pr4[:, :, :, :], oh[:, :, :, :], sc[:, :, :].unsqueeze(1).to_broadcast([P, TOPK, NT, NE]), ALU.mult))
            steps(dve.tensor_reduce(ckr[:, :, :], pr4[:, :, :, :], AX.X, ALU.add))
            steps(dve.tensor_reduce(csum[:, :], ckr[:, :, :].rearrange("p k t -> p t k"), AX.X, ALU.add))
            steps(dve.tensor_scalar(csum[:, :], csum[:, :], 1e-20, None, ALU.add))
            steps(dve.reciprocal(crec[:, :], csum[:, :]))
            dve.tensor_tensor(ck[:, :, :], ckr[:, :, :].rearrange("p k t -> p t k"), bc(crec[:, :], [P, NT, TOPK]), ALU.mult)
            dve.wait_ge(pos_done, 1)
            steps(dve.tensor_copy(cnt[:, :, :], pC[:, 1, 256:512].rearrange("p (t e) -> p e t", e=NE)))
            steps(dve.tensor_tensor_scan(flat(incl[:, :, :]), flat(d0[:, :, :]), flat(cnt[:, :, :]), 0.0, ALU.mult, ALU.add))
            steps(dve.tensor_tensor(excl[:, :, :], incl[:, :, :], cnt[:, :, :], ALU.subtract))
            steps(dve.tensor_tensor(nt8[:, :, :], bc(incl[:, :, NT - 1], [P, NE, 8]), iota256[:, :].unsqueeze(1).to_broadcast([P, NE, 8]), ALU.is_gt))
            steps(dve.tensor_reduce(nte[:, :], nt8[:, :, :], AX.X, ALU.add))
            steps(dve.tensor_tensor_scan(tinc[:, :], ton[:, :], nte[:, :], 0.0, ALU.mult, ALU.add))
            steps(dve.tensor_tensor(texc[:, :], tinc[:, :], nte[:, :], ALU.subtract))
            steps(dve.tensor_scalar(rowb[:, :], texc[:, :], float(MT), None, ALU.mult))
            steps(dve.tensor_tensor(excl[:, :, :], excl[:, :, :], bc(rowb[:, :], [P, NE, NT]), ALU.add))
            steps(dve.tensor_tensor(full[:, :, :], pC[:, 1, 0:256].rearrange("p (t e) -> p t e", e=NE), excl[:, :, :].rearrange("p e t -> p t e"), ALU.add))
            steps(dve.tensor_tensor(pr4[:, :, :, :], oh[:, :, :, :], full[:, :, :].unsqueeze(1).to_broadcast([P, TOPK, NT, NE]), ALU.mult))
            steps(dve.tensor_reduce(slf[:, :, :], pr4[:, :, :, :], AX.X, ALU.add))
            dve.tensor_copy(slot[:, :, :], slf[:, :, :].rearrange("p k t -> p t k")).then_inc(slots_ready, 1)
            steps(dve.tensor_scalar(texc[:, :], texc[:, :], float(SHARED_T), None, ALU.add))
            steps(dve.tensor_tensor(ecmp[:, :, :], bc(iotan[:, :], [1, ETILES + 1, NE]),
                                    texc[0:1, :].unsqueeze(1).to_broadcast([1, ETILES + 1, NE]), ALU.is_ge))
            steps(dve.tensor_reduce(ecf[:, :], ecmp[:, :, :], AX.X, ALU.add))
            dve.tensor_copy(etab[:, :], ecf[:, :]).then_inc(etab_ready, 1)

            def x_split(i, k):
                u, q = 4 * i + k, k % 2
                dve.wait_ge(x_hi_e, done(u))
                dve.tensor_tensor(flat(x_lo[:, q]), pA[:, q], flat(x_hi[:, q]).bitcast(F32), ALU.subtract).then_inc(x_lo_e, 1)

            def gate(i, k):
                u, q = 4 * i + k, k % 2
                dve.wait_ge(sg_e, done(u))
                dve.wait_ge(hT_e, done(u - 2))
                dve.tensor_tensor(hh[:, q], sg[:, q], pB[:, q, FI:2 * FI], ALU.mult).then_inc(hh_e, 1)

            def h_split(i, k):
                u, q = 4 * i + k, k % 2
                dve.wait_ge(h_hi_e, done(u))
                dve.tensor_tensor(flat(h_lo[:, q]), pC[0:FH, q, 0:2 * P], flat(h_hi[:, q]).bitcast(F32), ALU.subtract).then_inc(h_lo_e, 1)

            x_split(0, 0)
            x_split(0, 1)
            gate(0, 0)
            def add_shared(i, k):
                u, q = 4 * i + k, k % 2
                dve.wait_ge(dn_e, done(u, 3))
                Xu = X[:, bass.ds(u, 1), :].rearrange("p o f -> p (o f)")
                dve.tensor_tensor(Xu, Xu, pD[:, q], ALU.add).then_inc(y_added, 1)

            def step(i, k, looped):
                h_split(i, k - 1)
                if looped or 4 * i + k + 1 < HALVES:
                    x_split(i, k + 1)
                gate(i, k)

            for i, k, looped in chain(shared_steps(dve), border_steps()):
                step(i, k, looped)
                add_shared(i, k - 1)
            for i, k, looped in routed_steps(dve):
                step(i, k, looped)
            h_split(0, HALVES - 1)
            stage_end(dve, 3)

            def token_rows(t):
                return X[:, bass.ds(t, 1), :].rearrange("p o f -> p (o f)")

            def combine(b, tiles):
                for i in tiles:
                    dve.wait_ge(g_loaded[i], 16 * TOPK * (b + 1))
                for k in range(TOPK):
                    for i in tiles:
                        t = CPB * b + i
                        if k > 0:
                            steps.before(len(tiles) - 1 if k < TOPK - 1 else len(tiles) - 1 - tiles.index(i))
                        ins = dve.scalar_tensor_tensor(out=token_rows(t), in0=G[:, i, k, :], scalar=ck[:, bass.ds(t, 1), k],
                                                       in1=token_rows(t), op0=ALU.mult, op1=ALU.add)
                        if k < TOPK - 1:
                            steps.tell(ins)
                        else:
                            ins.then_inc(g_used, 1)
            def stats_x(b, tiles):
                dve.wait_ge(g_used, CPB * b + tiles[-1] + 1)
                dve.sem_inc(dve_note, 1)
                for i in tiles:
                    dve.bn_stats(statsx[:, i, :], token_rows(CPB * b + i)).then_inc(statsx_ready, 1)

            def measure(b):
                dve.wait_ge(statsx_ready, CPB * (b + 1))
                dve.sem_inc(dve_note, 1)
                for i in range(CPB):
                    ins = dve.bn_aggr(mvx[:, i, :], statsx[:, i, :])
                ins.then_inc(mvx_ready, 1)

            def norm(b):
                dve.wait_ge(mvx_ready, b + 1)
                dve.wait_ge(stdx_ready, b + 1)
                steps(dve.reciprocal(rstdx[:, :], stdx[:, :]))
                norm_tiles(b, range(0, 2))

            def norm_tiles(b, tiles):
                for i in tiles:
                    dve.tensor_scalar(qf[:, i, :], token_rows(CPB * b + i), mvx[:, i, 0:1], rstdx[:, i:i + 1],
                                      ALU.subtract, ALU.mult).then_inc(qf_ready, 1)

            def q_split(b, i):
                dve.wait_ge(q_hi_x, CPB * b + i + 1)
                dve.tensor_tensor(q_lo[:, i], qf[:, i, :], q_hi[:, i].bitcast(F32), ALU.subtract).then_inc(q_lo_x, 1)

            def q_rest(b):
                q_split(b, 0)
                norm_tiles(b, range(2, 3))
                q_split(b, 1)
                norm_tiles(b, range(3, 4))
                q_split(b, 2)
                q_split(b, 3)

            def add_x(b, tiles):
                for i in tiles:
                    dve.wait_ge(o_done, done(CPB * b + i))
                    dve.tensor_tensor(token_rows(CPB * b + i), token_rows(CPB * b + i), pB[:, i % 2], ALU.add).then_inc(o_added, 1)

            def stats_next(b, tiles):
                dve.wait_ge(o_added, done(CPB * b + tiles[-1]))
                dve.sem_inc(dve_note, 1)
                for i in tiles:
                    dve.bn_stats(stats[:, bass.ds(CPB * b + i, 1), :].rearrange("p o f -> p (o f)"), token_rows(CPB * b + i)).then_inc(next_stats, 1)

            dve.wait_ge(k_hi_x, 1)
            dve.tensor_tensor(k_lo[:, :, :], cr[:, 0], k_hi[:, :, :].bitcast(F32), ALU.subtract).then_inc(k_lo_x, 1)
            dve.wait_ge(v_hi_x, 1)
            dve.tensor_tensor(v_lo[:, :, :], cr[:, 1], v_hi[:, :, :].bitcast(F32), ALU.subtract).then_inc(v_lo_x, 1)
            for i in range(CPB):
                combine(0, range(i, i + 1))
                stats_x(0, range(i, i + 1))
            measure(0)
            norm(0)
            q_rest(0)
            for b, more in batch_steps(lambda n: steps.loop(n, X_STEPS)):
                for n in range(KC):
                    if more and n in (0, 2):
                        combine(b + 1, range(n, n + 2) if n == 0 else range(2, 3))
                    dve.wait_ge(s_hi_x, KC * b + n + 1)
                    dve.tensor_tensor(s_lo[:, n], sf[:, n], s_hi[:, n].bitcast(F32), ALU.subtract).then_inc(s_lo_x, 1)
                if more:
                    combine(b + 1, range(3, CPB))
                add_x(b, range(0, 2))
                if more:
                    stats_x(b + 1, range(CPB))
                    measure(b + 1)
                    norm(b + 1)
                add_x(b, range(2, 3))
                if more:
                    q_rest(b + 1)
                add_x(b, range(3, CPB))
                stats_next(b, range(CPB))
            dve.wait_ge(next_stats, NT)
            for t in range(NT):
                ins = dve.bn_aggr(mv[:, t, :], stats[:, t, :])
            ins.then_inc(mv_ready, 1)
            stage_end(dve, 4)

            dve.wait_ge(mv_ready, 2 * B + 1)
            dve.wait_ge(std_ready, 2 * B + 1)
            steps(dve.reciprocal(rstd[:, :], std[:, :]))

            def norm_f(g):
                if g >= 1:
                    dve.wait_ge(fT_done, CPB * g)
                for i in range(CPB):
                    normed(xn4[:, i], CPB * g + i).then_inc(xn4_ready, 1)

            def gate_f(i, k):
                for j in range(HCB):
                    w = HCB * (8 * i + k) + j
                    dve.wait_ge(fsg_ready, done(w))
                    dve.wait_ge(fh_lo_ready, done(w - 2))
                    dve.tensor_tensor(fh[:, j], fsg[:, j], pB[:, j], ALU.mult).then_inc(fh_ready, 1)

            def add_f(i, k):
                v = 8 * i + k
                for tt in range(CPB):
                    t = CPB * (k % 4) + tt
                    dve.wait_ge(fdn, done(4 * v + tt, 20))
                    dve.tensor_tensor(X[:, t, :], X[:, t, :], (pC, pD)[tt // 2][:, tt % 2], ALU.add).then_inc(fadd, 1)

            for g in range(2):
                norm_f(g)
                f_split(g)
            norm_f(2)
            gate_f(0, 0)
            for i, k, looped in ffn_first():
                if k + 1 < B:
                    f_split(k + 1)
                if k + 2 < B:
                    norm_f(k + 2)
                gate_f(i, k)
                add_f(i, k - 1)
            for i, k, looped in ffn_steps(dve):
                gate_f(i, k)
                add_f(i, k - 1)
            add_f(0, UNITS - 1)

        @block.tensor
        def _(pe):
            pe.sem_inc(qk_done, QK)
            for s in (inter_done, intra_done, st_done, hT_e, o_done, fgu):
                pe.sem_inc(s, 2)
            for s in (xT_e, gu_e, dn_e):
                pe.sem_inc(s, 3)
            pe.sem_inc(fdn, 20)

            def product3(out_, pairs, ready=()):
                n = len(pairs)
                for c, ((ah, al), (bh, bl)) in enumerate(pairs):
                    if ready:
                        pe.wait_ge(*ready[c])
                    pe.matmul(out_, ah, bh, start=c == 0, stop=False)
                    pe.matmul(out_, ah, bl, start=False, stop=False)
                    ins = pe.matmul(out_, al, bh, start=False, stop=c == n - 1)
                return ins

            pe.wait_ge(consts_ready, 1)
            for b in range(B):
                pe.wait_ge(wg_ready, 1)
                if b >= 2:
                    pe.wait_ge(gates_kept, b - 1)
                pe.wait_ge(ctxT_loaded[b % 2], 16 * (b // 2 + 1))
                for k in range(KC):
                    pe.matmul(pC[0:64, b % 2], wg[:, KC + k, :], ctxTb[:, b % 2, k], start=k == 0, stop=False)
                pe.wait_ge(qn_ready, b + 1)
                for k in range(KC):
                    if b >= 1:
                        pe.wait_ge(xT_kept, KC * (b - 1) + k + 1)
                    for i in range(CPB):
                        ins = pe.transpose((pA, pB)[k // 2][:, k % 2, i * P:(i + 1) * P], qn[:, b % 2, i, k * P:(k + 1) * P], ident[:, :])
                    ins.then_inc(xT_done, 1)
                for k in range(KC):
                    pe.wait_ge(xT_kept, KC * b + k + 1)
                    ins = pe.matmul(pC[0:64, b % 2], wg[:, k, :], qT[:, CPB * b:CPB * (b + 1), k], start=False, stop=k == KC - 1)
                ins.then_inc(gates_done, 1)
            pe.wait_ge(exps_ready, 1)
            for q, src in enumerate((WQ, WK, NR, Aq)):
                for c in range(CPB):
                    ins = pe.transpose((pA, pB)[q // 2][:, q % 2, c * P:(c + 1) * P], src[:, c * P:(c + 1) * P], ident[:, :])
                ins.then_inc(tok_done, 1)
            pe.wait_ge(dg_ready, 1)
            pe.matmul(pC[:, 0], onesf[:, 0:P], flat(DG[:, :, :]), start=True, stop=True).then_inc(tok_done, 1)
            stage_end(pe, 0)

            def products(i, k):
                t, b, c, p, loads = where(i, k)
                pe.wait_ge(tile_loaded[p], loads)
                pe.wait_ge(qe_ready, done(t))
                for j in range(NG):
                    pe.wait_ge(C_ready, done(NG * t + j - 2))
                    pe.matmul(pA[:, j % 2], kT[:, p, j], flat(qe[:, p, j]), start=True, stop=True).then_inc(qk_done, 1)
                    if j == 1:
                        state_products(i, k)
                for h in range(NH):
                    if h % HPG == 0:
                        pe.wait_ge(C_ready, done(NG * t + h // HPG))
                    ins = pe.matmul(pB[:, h // 8, h % 8 * V1:(h % 8 + 1) * V1], Cm[:, p, h, :], v1[:, p, h, :], start=True, stop=True)
                ins.then_inc(intra_done, 1)

            def state_products(i, k):
                t, b, c, p, loads = where(i, k)
                pe.wait_ge(h1_read, done(t - 1))
                w = HPG * V1
                if c > 0:
                    pe.wait_ge(qs_ready, done(3 * b + c - 1))
                    pe.wait_ge(St_ready, done(3 * b + c - 1))
                    for j in range(NG):
                        ins = pe.matmul(pC[:, j // 2, j % 2 * w:(j % 2 + 1) * w], qs[:, p, j],
                                        flat(St[:, HPG * j:HPG * (j + 1), :]), start=True, stop=True)
                    ins.then_inc(inter_done, 1)
                pe.wait_ge(v1_ready, done(t))
                if c < CPB - 1:
                    pe.wait_ge(kw_ready, done(3 * b + c))
                    pe.wait_ge(stm_ready, done(3 * b + c - 1))
                    for j in range(NG):
                        ins = pe.matmul(pD[:, j // 2, j % 2 * w:(j % 2 + 1) * w], flat(kw[:, p, HPG * j:HPG * (j + 1), :]),
                                        flat(v1[:, p, HPG * j:HPG * (j + 1), :]), start=True, stop=True)
                    ins.then_inc(st_done, 1)

            products(0, 0)
            for i, k, looped in mlstm_tiles(lambda n: pe.Fori(0, n)):
                products(i, k)
            stage_end(pe, 1)

            def scores(t):
                pe.wait_ge(xT_kept, KC * B + t + 1)
                for k in range(KC):
                    ins = pe.matmul(pC[:, 0, t * NE:(t + 1) * NE], xT2[:, t % 2, k], rw[:, k, :], start=k == 0, stop=k == KC - 1)
                ins.then_inc(sc_done, 1)

            pe.wait_ge(rout_loaded, 32)
            for t in range(NT):
                pe.wait_ge(xn2_ready, t + 1)
                if t >= 2:
                    pe.wait_ge(xT_kept, KC * B + t - 1)
                for k in range(KC):
                    ins = pe.transpose(pA[:, t % 2, k * P:(k + 1) * P], xn2[:, t, k * P:(k + 1) * P], ident[:, :])
                ins.then_inc(xT_done, 1)
                if t >= 1:
                    scores(t - 1)
            scores(NT - 1)
            pe.wait_ge(sel_ready, 1)
            pe.wait_ge(consts_ready, 3)
            for t in range(NT):
                pe.matmul(pC[:, 1, t * NE:(t + 1) * NE], tri[:, :], selb[:, t, :], start=True, stop=True)
            pe.matmul(pC[:, 1, 256:512], onesb[:, :], flat(selb[:, :, :]), start=True, stop=True).then_inc(pos_done, 1)

            def x_turn(i, k):
                u, q, wp = 4 * i + k, k % 2, k // 2 % 2
                pe.wait_ge(xr_loaded[wp], 16 * (i + k // 4 + 1))
                pe.wait_ge(x_lo_e, done(u - 2))
                for c in range(KC):
                    ins = pe.transpose(pA[:, q, c * P:(c + 1) * P], xr[:, wp, q, c * P:(c + 1) * P], ident[:, :])
                ins.then_inc(xT_e, 1)

            def gate_up(i, k):
                u, q, wp, n = 4 * i + k, k % 2, k // 2 % 2, 2 * i + k // 2
                pe.wait_ge(x_lo_e, done(u))
                pe.wait_ge(gw_lo, done(n))
                pe.wait_ge(hh_e, done(u - 2))
                product3(pB[:, q, 0:2 * FI], [((x_hi[:, q, c], x_lo[:, q, c]), (gu_hi[:, wp, c], gu_lo[:, wp, c])) for c in range(KC)]).then_inc(gu_e, 1)

            def h_turn(i, k):
                u, q = 4 * i + k, k % 2
                pe.wait_ge(hh_e, done(u))
                pe.wait_ge(h_lo_e, done(u - 2))
                for c in range(2):
                    ins = pe.transpose(pC[0:FH, q, c * P:(c + 1) * P], hh[:, q, c * FH:(c + 1) * FH], ident[:, :])
                ins.then_inc(hT_e, 1)

            def down(i, k, read_by):
                u, q, wp, n = 4 * i + k, k % 2, k // 2 % 2, 2 * i + k // 2
                pe.wait_ge(h_lo_e, done(u))
                pe.wait_ge(dw_lo, done(n))
                pe.wait_ge(read_by, done(u - 2))
                product3(pD[:, q], [((h_hi[:, q, c], h_lo[:, q, c]), (dn_hi[:, wp, c], dn_lo[:, wp, c])) for c in range(2)]).then_inc(dn_e, 1)

            x_turn(0, 0)
            x_turn(0, 1)
            gate_up(0, 0)
            def step(i, k, looped, read_by):
                first_routed = isinstance(i, int) and 4 * i + k + 1 == 2 * SHARED_T
                h_turn(i, k - 1)
                if not first_routed and (looped or 4 * i + k + 1 < HALVES):
                    x_turn(i, k + 1)
                gate_up(i, k)
                down(i, k - 1, read_by)
                if first_routed:
                    x_turn(i, k + 1)

            for i, k, looped in chain(shared_steps(pe), border_steps()):
                step(i, k, looped, y_added)
            pe.wait_ge(y_added, done(2 * SHARED_T - 1))
            for i, k, looped in routed_steps(pe):
                step(i, k, looped, y_e)
            h_turn(0, HALVES - 1)
            down(0, HALVES - 1, y_e)
            stage_end(pe, 3)

            with pe.Fori(0, B) as b:
                pe.wait_ge(k_lo_x, b + 1)
                for n in range(KC):
                    pe.wait_ge(s_sig, done(KC * b + n - 2))
                    cols = slice(n * P, (n + 1) * P)
                    product3(pA[:, n % 2], [((q_hi[:, i, cols], q_lo[:, i, cols]), (k_hi[:, i], k_lo[:, i])) for i in range(CPB)],
                             [(q_lo_x, CPB * b + i + 1) for i in range(CPB)] if n == 0 else ()).then_inc(s_done, 1)
                pe.wait_ge(v_lo_x, b + 1)
                for i in range(CPB):
                    pe.wait_ge(o_added, done(CPB * b + i - 2))
                    rows = slice(i * P, (i + 1) * P)
                    product3(pB[:, i % 2], [((v_hi[:, n, rows], v_lo[:, n, rows]), (s_hi[:, n], s_lo[:, n])) for n in range(KC)],
                             [(s_lo_x, KC * b + n + 1) for n in range(KC)] if i == 0 else ()).then_inc(o_done, 1)
            stage_end(pe, 4)

            def f_turn(g):
                for i in range(CPB):
                    t = CPB * g + i
                    pe.wait_ge(xn4_ready, t + 1)
                    if g == 1:
                        pe.wait_ge(f_lo_ready, t - CPB + 1)
                    if g >= 3:
                        pe.wait_ge(fadd, done(4 * (g - 3) + i, 4))
                    for c in range(KC):
                        ins = pe.transpose(tbank(i)[:, c * P:(c + 1) * P], xn4[:, i, c * P:(c + 1) * P], ident[:, :])
                    ins.then_inc(fT_done, 1)

            def gate_up_f(i, k):
                v, wp, tok = 8 * i + k, k // 4 % 2, slice(k % 4 * 512, (k % 4 + 1) * 512)
                pe.wait_ge(fw_lo, done(2 * i + k // 4))
                for j in range(HCB):
                    pe.wait_ge(fh_ready, done(HCB * v + j - 2))
                    for m, bank in ((0, pA[:, j]), (1, pB[:, j])):
                        def w(t_, c):
                            return t_[wp][:, m, c * BLK + j * P:c * BLK + (j + 1) * P]
                        ins = product3(bank, [((w(w_hi, c), w(w_lo, c)), (f_hi[:, c, tok], f_lo[:, c, tok])) for c in range(KC)])
                    ins.then_inc(fgu, 1)

            def down_f(i, k):
                v, q, wp = 8 * i + k, k % 2, k // 4 % 2
                pe.wait_ge(fh_lo_ready, done(HCB * v + HCB - 1))
                for tt in range(CPB):
                    pe.wait_ge(fadd, done(4 * v + tt - 4, 4))
                    cols = slice(tt * P, (tt + 1) * P)
                    product3((pC, pD)[tt // 2][:, tt % 2],
                             [((fh_hi[:, q, j, cols], fh_lo[:, q, j, cols]),
                               (w_hi[wp][:, 2, j * 512:(j + 1) * 512], w_lo[wp][:, 2, j * 512:(j + 1) * 512])) for j in range(HCB)]).then_inc(fdn, 1)

            f_turn(0)
            f_turn(1)
            pe.wait_ge(f_lo_ready, CPB)
            gate_up_f(0, 0)
            for i, k, looped in ffn_first():
                if k + 1 < B:
                    if k == 1:
                        pe.wait_ge(f_lo_ready, 2 * CPB)
                    f_turn(k + 1)
                else:
                    pe.wait_ge(f_lo_ready, CPB * B)
                gate_up_f(i, k)
                if k + 1 < B:
                    pe.wait_ge(f_lo_ready, CPB * (k + 2))
                down_f(i, k - 1)
            for i, k, looped in ffn_steps(pe):
                gate_up_f(i, k)
                down_f(i, k - 1)
            down_f(0, UNITS - 1)


def kernel(**inputs):
    import numpy as np
    import concourse.bacc as bacc
    from concourse.bass_utils import run_bass_kernel_spmd

    arrays = layout(inputs)
    nc = bacc.Bacc("TRN2", target_bir_lowering=False, num_devices=1)
    args = [nc.dram_tensor(n, a.shape, mybir.dt.from_np(a.dtype), kind="ExternalInput").ap() for n, a in arrays.items()]
    out = nc.dram_tensor("out", (B, S, E), F32, kind="ExternalOutput").ap()
    build(nc, *args, out)
    return run_bass_kernel_spmd(nc, [arrays], core_ids=[0]).results[0]["out"]


def layout(inputs):
    import numpy as np

    g = {n: np.asarray(a) for n, a in inputs.items()}
    gate_up = np.concatenate([np.concatenate([g["L0_ffn_shared_gate_w"], g["L0_ffn_shared_up_w"]])[None], g["L0_ffn_gate_up_proj"]])
    down = np.concatenate([g["L0_ffn_shared_down_w"][None], g["L0_ffn_down_proj"]])
    a = {
        "x": g["x"], "ctx": g["ctx_2048"], "ctxT": g["ctx_2048"].transpose(0, 2, 1),
        "Wi": g["L0_xattn_Wi"], "bi": g["L0_xattn_bi"], "Wf": g["L0_xattn_Wf"], "bf": g["L0_xattn_bf"],
        "ln_scale": g["L0_xattn_ln_scale"],
        "router_wT": g["L0_ffn_router_w"].T, "e_bias": g["L0_ffn_e_bias"],
        "gate_upT": gate_up.transpose(0, 2, 1).reshape(NE + 1, KC, P, 2 * FI).transpose(0, 2, 1, 3),
        "downT": down.transpose(0, 2, 1).reshape(NE + 1, 2, FH, E).transpose(0, 2, 1, 3),
        "w_gateT": g["L1_ffn_w_gate"].reshape(NBLK, BLK, KC, P).transpose(0, 3, 2, 1).reshape(NBLK, P, KC * BLK),
        "w_upT": g["L1_ffn_w_up"].reshape(NBLK, BLK, KC, P).transpose(0, 3, 2, 1).reshape(NBLK, P, KC * BLK),
        "w_downT": g["L1_ffn_w_down"].T.reshape(NBLK, HCB, P, E).transpose(0, 2, 1, 3).reshape(NBLK, P, HCB * E),
    }
    return {n: np.ascontiguousarray(v) for n, v in a.items()}
```
